# Optimizing a Trainium2 kernel written in Bass

```python
import numpy as np
import jax
import jax.numpy as jnp

def _softmax(x, axis=-1):
    return jax.nn.softmax(x, axis=axis)

def _gelu(x):
    return jax.nn.gelu(x, approximate=True)

def _silu(x):
    return jax.nn.silu(x)

def _sigmoid(x):
    return jax.nn.sigmoid(x)

def _layernorm(x, axis=-1, eps=1e-05):
    m = jnp.mean(x, axis=axis, keepdims=True)
    v = jnp.var(x, axis=axis, keepdims=True)
    return (x - m) / jnp.sqrt(v + eps)

def _scatter_add(tgt, idx, src, axis=0):
    return tgt.at[idx].add(src)

def _segment_sum(src, seg, n):
    return jax.ops.segment_sum(src, seg, n)
kernel_name = 'mk_gps_d1_gnn_r8_8505ab'

def setup_inputs(seed: int=0):
    np.random.seed(seed)
    _w = jnp.asarray

    def _rec_inputs():
        import jax
        import jax.numpy as jnp
        _gk = jax.random.key(seed)
        x = -0.0003929 + 0.9999 * jax.random.normal(jax.random.fold_in(_gk, 1), (6250, 256), jnp.float32)
        src = jax.random.randint(jax.random.fold_in(_gk, 2), (100000,), 0, 6250, jnp.int32)
        dst = jax.random.randint(jax.random.fold_in(_gk, 3), (100000,), 0, 6250, jnp.int32)
        _o = jnp.argsort(dst, stable=True)
        src = src[_o]
        dst = dst[_o]
        edge_weight = 0.00540447 + 1.00226 * jax.random.normal(jax.random.fold_in(_gk, 12), (100000,), jnp.float32)
        return (x, src, dst, edge_weight)
    x, src, dst, edge_weight = _rec_inputs()

    def _L0_gnn_setup():
        import jax, jax.numpy as jnp
        import numpy as np
        from itertools import combinations
        NDIM = 256
        BATCH = 8192

        def _build_mat(rots, idx_i, idx_j, ndim):

            def step(mat, t):
                i, j, theta = t
                c = jnp.cos(theta)
                s = jnp.sin(theta)
                ri = mat[i]
                rj = mat[j]
                mat = mat.at[i].set(c * ri - s * rj)
                mat = mat.at[j].set(s * ri + c * rj)
                return (mat, None)
            mat0 = jnp.eye(ndim, dtype=rots.dtype)
            mat, _ = jax.lax.scan(step, mat0, (idx_i, idx_j, rots))
            return mat.T
        key = jax.random.key(seed)
        k1, k2 = jax.random.split(key)
        pairs = np.array(list(combinations(range(NDIM), 2)), dtype=np.int32)
        return {'x': jax.random.normal(k1, (BATCH, NDIM), dtype=jnp.float32), 'rots': jax.random.normal(k2, (pairs.shape[0],), dtype=jnp.float32), 'idx_i': jnp.asarray(pairs[:, 0]), 'idx_j': jnp.asarray(pairs[:, 1])}
    _L0_gnn_all = _L0_gnn_setup()
    _L0_gnn_in = {k: v for k, v in _L0_gnn_all.items() if k in ()}
    del _L0_gnn_all

    def _L0_mix_setup():
        import jax, jax.numpy as jnp
        import numpy as np
        BN_EPS = 1e-05
        key = jax.random.key(seed)
        ks = jax.random.split(key, 4)
        B, N, D = (8, 1024, 256)
        outD = 256
        s = 1.0 / np.sqrt(D)
        return {'feature': jax.random.normal(ks[0], (B, N, D), dtype=jnp.float32), 'W_qk': jax.random.normal(ks[1], (2, D, D), dtype=jnp.float32) * s, 'b_qk': jnp.zeros((2, D), dtype=jnp.float32), 'W_v': jax.random.normal(ks[2], (D, outD), dtype=jnp.float32) * s, 'b_v': jnp.zeros((outD,), dtype=jnp.float32), 'gamma': jnp.ones((D,), dtype=jnp.float32), 'beta': jnp.zeros((D,), dtype=jnp.float32)}
    _L0_mix_all = _L0_mix_setup()
    _L0_mix_in = {k: v for k, v in _L0_mix_all.items() if k in ('W_qk', 'b_qk', 'W_v', 'b_v', 'gamma', 'beta')}
    del _L0_mix_all

    def _L0_ffn_setup():
        import jax, jax.numpy as jnp
        import numpy as np
        E = 8
        K = 2
        D = 256
        H = 512
        DOUT = 256
        EPS = 1e-05
        key = jax.random.key(seed)
        ks = jax.random.split(key, 9)
        s = 0.02
        return {'x': jax.random.normal(ks[0], (4, 1024, D), jnp.float32), 'gamma': 1.0 + 0.05 * jax.random.normal(ks[1], (D,), jnp.float32), 'beta': 0.05 * jax.random.normal(ks[2], (D,), jnp.float32), 'Wr': 0.01 * jax.random.normal(ks[3], (D, E), jnp.float32), 'br': jnp.zeros((E,), jnp.float32), 'W1': s * jax.random.normal(ks[4], (E, D, H), jnp.float32), 'b1': s * jax.random.normal(ks[5], (E, H), jnp.float32), 'W2': s * jax.random.normal(ks[6], (E, H, DOUT), jnp.float32), 'b2': s * jax.random.normal(ks[7], (E, DOUT), jnp.float32)}
    _L0_ffn_all = _L0_ffn_setup()
    _L0_ffn_in = {k: v for k, v in _L0_ffn_all.items() if k in ('gamma', 'beta', 'Wr', 'br', 'W1', 'b1', 'W2', 'b2')}
    del _L0_ffn_all
    return {'x': x, 'src': src, 'dst': dst, 'edge_weight': edge_weight, 'L0_mix_W_qk': _L0_mix_in['W_qk'], 'L0_mix_b_qk': _L0_mix_in['b_qk'], 'L0_mix_W_v': _L0_mix_in['W_v'], 'L0_mix_b_v': _L0_mix_in['b_v'], 'L0_mix_gamma': _L0_mix_in['gamma'], 'L0_mix_beta': _L0_mix_in['beta'], 'L0_ffn_gamma': _L0_ffn_in['gamma'], 'L0_ffn_beta': _L0_ffn_in['beta'], 'L0_ffn_Wr': _L0_ffn_in['Wr'], 'L0_ffn_br': _L0_ffn_in['br'], 'L0_ffn_W1': _L0_ffn_in['W1'], 'L0_ffn_b1': _L0_ffn_in['b1'], 'L0_ffn_W2': _L0_ffn_in['W2'], 'L0_ffn_b2': _L0_ffn_in['b2']}

def reference(x, src, dst, edge_weight, L0_mix_W_qk, L0_mix_b_qk, L0_mix_W_v, L0_mix_b_v, L0_mix_gamma, L0_mix_beta, L0_ffn_gamma, L0_ffn_beta, L0_ffn_Wr, L0_ffn_br, L0_ffn_W1, L0_ffn_b1, L0_ffn_W2, L0_ffn_b2):
    import jax
    import jax.numpy as jnp

    def _L0_gnn_ref(x, rots, idx_i, idx_j):
        import jax, jax.numpy as jnp
        import numpy as np
        from itertools import combinations
        NDIM = 256
        BATCH = 8192

        def _build_mat(rots, idx_i, idx_j, ndim):

            def step(mat, t):
                i, j, theta = t
                c = jnp.cos(theta)
                s = jnp.sin(theta)
                ri = mat[i]
                rj = mat[j]
                mat = mat.at[i].set(c * ri - s * rj)
                mat = mat.at[j].set(s * ri + c * rj)
                return (mat, None)
            mat0 = jnp.eye(ndim, dtype=rots.dtype)
            mat, _ = jax.lax.scan(step, mat0, (idx_i, idx_j, rots))
            return mat.T
        m = _build_mat(rots, idx_i, idx_j, x.shape[-1])
        return x @ m

    def _L0_mix_ref(feature, W_qk, b_qk, W_v, b_v, gamma, beta):
        import jax, jax.numpy as jnp
        import numpy as np
        BN_EPS = 1e-05
        QK = jnp.einsum('bnd,kde->bkne', feature, W_qk) + b_qk[None, :, None, :]
        value = jnp.einsum('bnd,de->bne', feature, W_v) + b_v
        query = QK[:, 0]
        key = QK[:, 1]
        sm = jax.nn.softmax(key, axis=1)
        lam = jnp.einsum('bnd,bne->bde', sm, value)
        mean = jnp.mean(lam, axis=(0, 2), keepdims=True)
        var = jnp.var(lam, axis=(0, 2), keepdims=True)
        bn = (lam - mean) * jax.lax.rsqrt(var + BN_EPS)
        bn = bn * gamma[None, :, None] + beta[None, :, None]
        return jnp.einsum('bnd,bde->bne', query, bn)

    def _L0_ffn_ref(x, gamma, beta, Wr, br, W1, b1, W2, b2):
        import jax, jax.numpy as jnp
        import numpy as np
        E = 8
        K = 2
        D = 256
        H = 512
        DOUT = 256
        EPS = 1e-05
        mu = jnp.mean(x, axis=-1, keepdims=True)
        var = jnp.mean(jnp.square(x - mu), axis=-1, keepdims=True)
        xn = (x - mu) * jax.lax.rsqrt(var + EPS) * gamma + beta
        logits = jnp.einsum('bsd,de->bse', xn, Wr) + br
        top_vals, top_idx = jax.lax.top_k(logits, K)
        w = jax.nn.softmax(top_vals, axis=-1)
        w_full = jnp.einsum('bsk,bske->bse', w, jax.nn.one_hot(top_idx, E, dtype=w.dtype))
        y = jnp.zeros(x.shape[:-1] + (DOUT,), x.dtype)
        for e in range(E):
            h = jax.nn.gelu(jnp.einsum('bsd,dh->bsh', xn, W1[e]) + b1[e], approximate=False)
            y_e = jnp.einsum('bsh,hd->bsd', h, W2[e]) + b2[e]
            y = y + y_e * w_full[..., e, None]
        return y
    xn = _layernorm(x, axis=-1)
    x = x + _L0_gnn_ref(xn, edge_weight, src, dst) + _L0_mix_ref(xn[None], L0_mix_W_qk, L0_mix_b_qk, L0_mix_W_v, L0_mix_b_v, L0_mix_gamma, L0_mix_beta)[0]
    x = x + _L0_ffn_ref(_layernorm(x, axis=-1)[None], L0_ffn_gamma, L0_ffn_beta, L0_ffn_Wr, L0_ffn_br, L0_ffn_W1, L0_ffn_b1, L0_ffn_W2, L0_ffn_b2)[0]
    return x

_drawn_inputs = setup_inputs


def setup_inputs(seed=0):
    import zlib

    import numpy as np

    out = dict(_drawn_inputs(seed))
    spreads = {'L0_mix_b_qk': (0.0, 0.1),
     'L0_mix_b_v': (0.0, 0.1),
     'L0_mix_gamma': (1.0, 0.2),
     'L0_mix_beta': (0.0, 0.277),
     'L0_ffn_br': (0.0, 0.8)}
    factors = {'edge_weight': 48.496,
     'L0_ffn_gamma': 8.0,
     'L0_ffn_beta': 8.0,
     'L0_ffn_Wr': 8.0,
     'L0_ffn_W1': 8.0,
     'L0_ffn_b1': 59.333,
     'L0_ffn_W2': 8.0,
     'L0_ffn_b2': 64.0}
    for name, (base, spread) in spreads.items():
        noise = np.random.default_rng([zlib.crc32(name.encode()), seed]).standard_normal(out[name].shape)
        drawn = base * np.exp(spread * noise) if base else spread * noise
        out[name] = jnp.asarray(drawn.astype(out[name].dtype))
    for name, factor in factors.items():
        out[name] = (out[name] * factor).astype(out[name].dtype)
    return out
```

```python
from contextlib import ExitStack

import concourse.bass as bass
from concourse import mybir

F32 = mybir.dt.float32
BF16 = mybir.dt.bfloat16
I32 = mybir.dt.int32
U32 = mybir.dt.uint32
ALU = mybir.AluOpType
ACT = mybir.ActivationFunctionType
AX_X = mybir.AxisListType.X

P = 128
PI = 3.141592653589793
MAGIC = 12582912.0
TURN_HI = 6.28125
TURN_MID = 0.0019350051879882812
TURN_LO = 2.0 * PI - TURN_HI - TURN_MID


def gnn_layer(nc, x, src, dst, edge_weight, W_qk, b_qk, W_v, b_v, bn_gamma, bn_beta,
              gamma, beta, Wr, br, W1, b1, W2, b2, out):
    N, D = x.shape
    NE = src.shape[0]
    NX, _, H = W1.shape
    KB = D // P
    NT = (N + P - 1) // P
    FULL = N // P
    TAIL = N - FULL * P
    EPS = 1e-5

    EP = 125
    EL = NE // EP
    BL = 200
    NB = NE // BL
    REC = 8
    CAP = P - 1
    G = 4
    NOROW = 512.0
    LEVELS = 7

    GRP = 4 * P
    STRIDE = N + P + 22
    MT = (2 * N + P - 1) // P + NX
    MT += MT % 2
    SPARE = MT - (2 * N) // P
    assert EP * EL == NE and EL % BL == 0 and TAIL and D == 2 * P and H % P == 0

    ctx = ExitStack()
    with ctx:
        def sb(name, shape, dt=F32):
            return ctx.enter_context(nc.sbuf_tensor(name, shape, dt))

        def sem(name):
            return ctx.enter_context(nc.semaphore(name))

        def dram(name, shape, dt=F32):
            return nc.dram_tensor(name, shape, dt).ap()

        incl_d = dram("incl_d", [NB, BL])
        incl_out = incl_d.rearrange("(p c) l -> p (c l)", p=EP)
        ends_d = dram("ends_d", [EP, NB // EP])
        rec_d = dram("rec_d", [NE, REC])
        send_d = dram("send_d", [(NX + 1) * STRIDE, D])
        back_d = dram("back_d", [MT * P, D])

        R1 = sb("R1", [P, NT * D])
        R2 = sb("R2", [P, KB * NT * P])
        R3 = sb("R3", [P, NX * (KB * H + (H // P) * D)])

        class Carve:
            def __init__(self, region):
                self.region, self.at = region, 0

            def __call__(self, *shape, dt=F32, parts=P):
                n = 1
                for s in shape:
                    n *= s
                words = n if dt in (F32, I32, U32) else (n + 1) // 2
                v = self.region[0:parts, self.at:self.at + words]
                self.at += words
                assert self.at <= self.region.shape[1]
                if dt != F32:
                    v = v.bitcast(dt)
                if len(shape) == 2:
                    v = v.rearrange("p (a b) -> p a b", a=shape[0])
                if len(shape) == 3:
                    v = v.rearrange("p (a b c) -> p a b c", a=shape[0], b=shape[1])
                return v

        x_all = R1[:, :].rearrange("p (t d) -> p t d", t=NT)
        x2_all = x_all
        xnT = R2[:, :].rearrange("p (k n) -> p k n", k=KB)

        prep = Carve(R3)
        i_f, j_f, g_i, g_j, cnt, incl, theta, turn = [prep(EL, parts=EP) for _ in range(8)]
        i_raw, j_raw = incl.bitcast(I32), cnt.bitcast(I32)
        rec = prep(EL, REC, parts=EP)
        ex = prep(KB, GRP)
        exT = prep(4, D)
        PT = prep(KB, D)
        lam = prep(KB, D)
        w1s = R3[:, 0:NX * KB * H].rearrange("p (e k h) -> p e k h", e=NX, k=KB)
        w2s = R3[:, NX * KB * H:].rearrange("p (e k d) -> p e k d", e=NX, k=H // P)

        chunk = Carve(R1)
        ends = chunk(NB)
        junk = chunk(G, NB, dt=BF16)
        rows = chunk(G, BL)
        recs = chunk(G, REC)
        slotmask = chunk(G, P)
        hits = chunk(3 * G, P)
        Lself = chunk(G, P)
        Lnext = chunk(G, P)
        WK = chunk(G, 3 * P)
        Bself = chunk(G, D)
        Bmat = chunk(G, D)
        STm = chunk(G, D)
        GT = chunk(G, KB * P)
        Vs = chunk(D)
        fld = chunk(24, G)
        pos = chunk(3, G)
        cur = chunk(5, G)
        idx = chunk(2, G, dt=U32)
        tb16 = chunk(G, dt=BF16)
        keep = chunk(G, KB)

        moe = Carve(R2)
        b1B = moe(NX, H)
        b2B = moe(NX, D)
        xm = [moe(D) for _ in range(2)]
        xmT = [moe(D) for _ in range(2)]
        hpre = [moe(H) for _ in range(2)]
        hact = [moe(H) for _ in range(2)]
        hT = [moe(H) for _ in range(2)]
        yb = [moe(D) for _ in range(2)]
        ya = [moe(D) for _ in range(2)]
        yc = [moe(D) for _ in range(2)]

        ident = sb("ident", [P, P])
        identb = sb("identb", [P, P], BF16)
        tri = sb("tri", [P, P])
        trib = sb("trib", [P, P], BF16)
        ones = sb("ones", [P, P])
        onesb = sb("onesb", [P, P], BF16)
        col0 = sb("col0", [P, D])
        col1 = sb("col1", [P, P])
        prow = sb("prow", [P, 1])
        prow1 = sb("prow1", [P, 1])
        minsub = sb("minsub", [P, 1])
        maxsub = sb("maxsub", [P, 1])
        slotnum = sb("slotnum", [P, G])
        Mrot = sb("Mrot", [P, KB, D])
        wq = sb("wq", [P, KB, D])
        wk = sb("wk", [P, KB, D])
        wv = sb("wv", [P, KB, D])
        wqT = sb("wqT", [P, KB, D])
        comb = sb("comb", [P, KB, D])
        small = sb("small", [P, 16])
        bq_c = sb("bq_c", [P, KB])
        bk_c = sb("bk_c", [P, KB])
        bng_c = sb("bng_c", [P, KB])
        bnb_c = sb("bnb_c", [P, KB])
        bvB = sb("bvB", [P, D])
        gamB = sb("gamB", [P, D])
        betB = sb("betB", [P, D])
        wr_s = sb("wr_s", [P, KB, NX])
        brB = sb("brB", [P, NX])
        addrow = sb("addrow", [P, D])
        stats = sb("stats", [P, NT, 6])
        mv = sb("mv", [P, NT, 2])
        rstd = sb("rstd", [P, NT])
        nmr = sb("nmr", [P, NT])
        xng = sb("xng", [P, 4, D])
        Pacc = sb("Pacc", [P, KB, D])
        bn = sb("bn", [P, KB, D])
        run_m = sb("run_m", [P, KB])
        grp_m = sb("grp_m", [P, KB])
        new_m = sb("new_m", [P, KB])
        ebias = sb("ebias", [P, KB])
        dm = sb("dm", [P, KB])
        alpha = sb("alpha", [P, KB])
        gsum = sb("gsum", [P, KB])
        ssum = sb("ssum", [P, KB])
        rsum = sb("rsum", [P, KB])
        n_groups_i = sb("n_groups_i", [1, 1], I32)
        total = sb("total", [P, 1])
        poff = sb("poff", [P, 1])

        xt = [sb(f"xt{b}", [P, D]) for b in range(2)]
        stg = [sb(f"stg{b}", [P, D]) for b in range(2)]
        xf = [sb(f"xf{b}", [P, D]) for b in range(2)]
        xfT = sb("xfT", [P, D])
        st2 = sb("st2", [P, 6])
        mv2 = sb("mv2", [P, 2])
        sc2 = sb("sc2", [P, 8])
        lg = sb("lg", [P, NX])
        top = sb("top", [P, 8])
        topi = sb("topi", [P, 8], U32)
        topf = sb("topf", [P, 8])
        oh = sb("oh", [P, 2, NX])
        msk = sb("msk", [P, NX])
        mskb = sb("mskb", [P, NX], BF16)
        slot8 = sb("slot8", [P, NX])
        base8 = sb("base8", [P, NX])
        reg8 = sb("reg8", [P, NX])
        junk8 = sb("junk8", [P, NX])
        sl2 = sb("sl2", [P, 2])
        slots_f = sb("slots_f", [P, 2, NT])
        experts_f = sb("experts_f", [P, 2, NT])
        moved = sb("moved", [P, 2, NT])
        slots_u = sb("slots_u", [P, 2, NT], U32)
        slot_now = [sb(f"slot_now{b}", [P, 2], U32) for b in range(2)]
        padf = sb("padf", [P, NX])
        padu = sb("padu", [P, NX], U32)
        topd = sb("topd", [P, NT])
        wexp = sb("wexp", [P, NT])
        w_a = sb("w_a", [P, NT])
        w_b = sb("w_b", [P, NT])
        zrow = sb("zrow", [P, D])
        ntile = sb("ntile", [P, 4, NX])
        tnum = sb("tnum", [1, MT])
        tacc = sb("tacc", [1, 3, MT])
        ttab = sb("ttab", [1, 2, MT], I32)
        tint = sb("tint", [1, NX], I32)

        bank = [ctx.enter_context(nc.psum_tensor(f"bank{i}", [P, 512], F32)) for i in range(8)]
        pw = [bank[h][:, :].rearrange("p (c n) -> p c n", c=2) for h in range(2)]
        jb = [bank[2 + h][:, 0:2 * P].rearrange("p (c n) -> p c n", c=2) for h in range(2)]
        TB, apV, apM, misc = bank[4:8]

        S = {}
        for n in ("const consts edges wload prow_ld xld dve act pool pe recs_out ends_in "
                  "xn_ready xT_psum xT_done keys_psum kmax_done ebias_ready alpha_ready exp_done exT_psum exT_done "
                  "mix_psum mix_acc lam_in Lready LT_psum WK_act WK_dve sq_psum J_done V_psum V_done M_psum M_done "
                  "blk_ready rows_in pos_ready recs_in flds_ready TB_psum B_ready J_last GT_psum GT_done ST_ready D_psum D_done "
                  "reserve ngroups comb_pe comb_dve addrow_done x2_psum stg_done x2_done "
                  "std_need std_done xf_ready xfT_psum xfT_done lg_psum msk_ready rank_psum slot_ready "
                  "w_loaded bias_loaded pads zeros_out tiles_ready sc0 sc1 xt0 xt1 xm0 xm1 "
                  "xmT_psum xmT_done h_psum hpre_done hact_done hT_psum hT_done y_psum y_done yst0 yst1 "
                  "ya0 ya1 out0 out1 fin_done wexp_need wexp_done w_ready scan_ok angles_ok xstats_ok pn_ok pT_ok lamstats_ok "
                  "bn_ok chunk_init_ok dve_settled pool_settled slot8 tl back_slots ya_sum mskb_zero").split():
            S[n] = sem("s_" + n)
        block = ctx.enter_context(nc.Block())

        def chain(eng, s):
            n = [0]

            def link(ins):
                n[0] += 1
                ins.then_inc(s, 1)
                eng.wait_ge(s, n[0])
            link.n = n
            return link

        def settle(eng):
            eng.sem_inc(S["dve_settled"] if eng is nc.vector else S["pool_settled"], 1)

        def bcast_row(ap, n):
            return ap.rearrange("(a n) -> a n", a=1).broadcast_to([P, n])

        NG12 = FULL // 4
        xg_src = x[0:FULL * P, :].rearrange("(t p) d -> p t d", p=P)

        @block.sync
        def _(sp):
            sp.dma_start(i_raw, src.rearrange("(p l) -> p l", p=EP)).then_inc(S["edges"], 16)
            sp.dma_start(j_raw, dst.rearrange("(p l) -> p l", p=EP)).then_inc(S["edges"], 16)
            sp.dma_start(theta, edge_weight.rearrange("(p l) -> p l", p=EP)).then_inc(S["edges"], 16)
            for c in range(0, FULL, 8):
                sp.dma_start(x_all[:, c:c + 8, :], xg_src[:, c:c + 8, :]).then_inc(S["xld"], 16)
            sp.dma_start(x_all[0:TAIL, FULL, :], x[FULL * P:N, :]).then_inc(S["xld"], 16)
            for dstt, s in ((wq, W_qk[0]), (wk, W_qk[1]), (wv, W_v)):
                sp.dma_start(dstt[:, :, :], s.rearrange("(k p) e -> p k e", p=P)).then_inc(S["wload"], 16)
            sp.dma_start(wr_s[:, :, :], Wr.rearrange("(k p) e -> p k e", p=P)).then_inc(S["wload"], 16)
            for dstt, s in ((bq_c, b_qk[0]), (bk_c, b_qk[1]), (bng_c, bn_gamma), (bnb_c, bn_beta)):
                with nc.allow_non_contiguous_dma(reason="one column of a small vector"):
                    sp.dma_start(dstt[:, :], s.rearrange("(k p) -> p k", p=P)).then_inc(S["wload"], 16)
            for dstt, s, n in ((bvB, b_v, D), (gamB, gamma, D), (betB, beta, D), (brB, br, NX)):
                sp.dma_start(dstt[:, :], bcast_row(s, n)).then_inc(S["wload"], 16)
            sp.wait_ge(S["recs_out"], 1)
            sp.dma_start(incl_out, incl[:, :]).then_inc(S["reserve"], 16)
            with nc.allow_non_contiguous_dma(reason="four words per partition"):
                sp.dma_start(ends_d, incl.rearrange("p (c l) -> p c l", l=BL)[:, :, BL - 1]).then_inc(S["reserve"], 16)
            sp.wait_ge(S["recs_out"], 2)
            sp.dma_start(rec_d.rearrange("(p l) r -> p (l r)", p=EP), rec.rearrange("p l r -> p (l r)")).then_inc(S["reserve"], 16)
            sp.wait_ge(S["reserve"], 48)
            sp.wait_ge(S["mix_acc"], NG12 + 2)
            sp.dma_start(ends, ends_d.rearrange("a b -> (a b)").rearrange("(o n) -> o n", o=1).broadcast_to([P, NB])).then_inc(S["ends_in"], 16)
            sp.wait_ge(S["bn_ok"], 1)
            for e in range(NX):
                sp.dma_start(w1s[:, e], W1[e].rearrange("(k p) h -> p k h", p=P)).then_inc(S["w_loaded"], 16)
                sp.dma_start(w2s[:, e], W2[e].rearrange("(k p) d -> p k d", p=P)).then_inc(S["w_loaded"], 16)
            sp.wait_ge(S["consts"], 1)
            for t in range(SPARE):
                r = NX * STRIDE + t * P
                sp.dma_start(send_d[r:r + P, :], zrow[:, :]).then_inc(S["zeros_out"], 16)

            def load_x(t, b, uses, rows_=P):
                sp.wait_ge(S["x2_done"], uses)
                if rows_ == P:
                    sp.dma_start(xt[b][:, :], x[bass.ds(t * P, P), :]).then_inc(S[f"xt{b}"], 16)
                else:
                    sp.dma_start(xt[b][0:rows_, :], x[FULL * P:N, :]).then_inc(S[f"xt{b}"], 16)
            sp.wait_ge(S["consts"], 1)
            for b in range(2):
                sp.dma_start(xt[b][:, :], x[b * P:b * P + P, :]).then_inc(S[f"xt{b}"], 16)
            with sp.Fori(1, FULL // 2) as k:
                for b in range(2):
                    load_x(k * 2 + b, b, k * 2 + (b - 1))
            load_x(FULL, 0, FULL - 1, TAIL)

            sp.wait_ge(S["x2_psum"], NT)
            sp.dma_start(b1B, b1.rearrange("e h -> (e h)").rearrange("(o n) -> o n", o=1).broadcast_to([P, NX * H]).rearrange("p (e h) -> p e h", e=NX)).then_inc(S["bias_loaded"], 16)
            sp.dma_start(b2B, b2.rearrange("e h -> (e h)").rearrange("(o n) -> o n", o=1).broadcast_to([P, NX * D]).rearrange("p (e h) -> p e h", e=NX)).then_inc(S["bias_loaded"], 16)

            sp.wait_ge(S["tiles_ready"], 1)
            sp.wait_ge(S["sc0"], 32 * (FULL // 2 + 1))
            sp.wait_ge(S["sc1"], 32 * (FULL // 2))
            sp.wait_ge(S["pads"], 16 * NX)
            sp.wait_ge(S["zeros_out"], 16 * SPARE)

            def load_tile(i, b):
                r = sp.value_load(ttab[0:1, 1, bass.ds(i, 1)], min_val=0, max_val=(NX + 1) * STRIDE - P)
                sp.dma_start(xm[b], send_d[bass.ds(r, P), :]).then_inc(S[f"xm{b}"], 16)
            for b in range(2):
                load_tile(b, b)
            with sp.Fori(1, MT // 2) as k:
                for b in range(2):
                    sp.wait_ge(S["xmT_psum"], k * 2 + (b - 1))
                    load_tile(k * 2 + b, b)

        @block.gpsimd
        def _(pool):
            link = chain(pool, S["pool"])
            nc.gpsimd.memset(ones[:, :], 1.0).then_inc(S["const"], 1)
            nc.gpsimd.memset(onesb[:, :], 1.0).then_inc(S["const"], 1)
            nc.gpsimd.memset(zrow[:, :], 0.0).then_inc(S["const"], 1)
            link(nc.gpsimd.memset(ident[:, :], 0.0))
            link(nc.gpsimd.affine_select(out=ident[:, :], in_=ident[:, :], compare_op=ALU.not_equal, fill=1.0,
                                         base=0, pattern=[[-1, P]], channel_multiplier=1))
            link(nc.gpsimd.tensor_copy(identb[:, :], ident[:, :]))
            link(nc.gpsimd.memset(tri[:, :], 0.0))
            link(nc.gpsimd.affine_select(out=tri[:, :], in_=tri[:, :], compare_op=ALU.is_ge, fill=1.0,
                                         base=0, pattern=[[-1, P]], channel_multiplier=1))
            link(nc.gpsimd.tensor_copy(trib[:, :], tri[:, :]))
            for ap, pat, base, mult in ((col0[:, :], [[1, D]], 0, 0), (col1[:, :], [[1, P]], 1, 0),
                                        (prow[:, :], [[0, 1]], 0, 1), (prow1[:, :], [[0, 1]], 1, 1),
                                        (slotnum[:, :], [[CAP, G]], 0, 1), (reg8[:, :], [[STRIDE, NX]], 0, 0),
                                        (tnum[:, :], [[1, MT]], 0, 0)):
                link(nc.gpsimd.iota(ap, pattern=pat, base=base, channel_multiplier=mult,
                                    allow_small_or_imprecise_dtypes=True))
            link(nc.gpsimd.tensor_scalar(minsub[:, :], prow[:, :], float(P - 1), None, ALU.is_ge))
            link(nc.gpsimd.tensor_scalar(maxsub[:, :], prow[:, :], 1.0, None, ALU.is_ge))
            pool.wait_ge(S["const"], 3)
            nc.gpsimd.memset(small[:, :], EPS).then_inc(S["consts"], 1)

            def gather_group(k):
                pool.wait_ge(S["blk_ready"], k + 1)
                settle(pool)
                for g in range(G):
                    nc.gpsimd.indirect_dma_start(
                        out=rows[:, g, :], out_offset=None, in_=incl_d,
                        in_offset=bass.IndirectOffsetOnAxis(ap=idx[:, 0, g:g + 1], axis=0)).then_inc(S["rows_in"], 16)
                pool.wait_ge(S["pos_ready"], k + 1)
                settle(pool)
                for g in range(G):
                    nc.gpsimd.indirect_dma_start(
                        out=recs[:, g, :], out_offset=None, in_=rec_d,
                        in_offset=bass.IndirectOffsetOnAxis(ap=idx[:, 1, g:g + 1], axis=0)).then_inc(S["recs_in"], 16)
            pool.wait_ge(S["ngroups"], 1)
            pool.wait_ge(S["reserve"], 48)
            n = pool.value_load(n_groups_i[0:1, 0:1], min_val=1, max_val=4 * NE)
            gather_group(0)
            with pool.Fori(0, n) as k:
                gather_group(k + 1)

            def scatter(t, b, rows_=P):
                pool.wait_ge(S["slot_ready"], t + 1)
                settle(pool)
                for c in range(2):
                    nc.gpsimd.indirect_dma_start(
                        out=send_d, out_offset=bass.IndirectOffsetOnAxis(ap=slot_now[b][0:rows_, c:c + 1], axis=0),
                        in_=xf[b][0:rows_, :], in_offset=None).then_inc(S[f"sc{b}"], 16)
            with pool.Fori(0, FULL // 2) as k:
                for b in range(2):
                    scatter(k * 2 + b, b)
            scatter(FULL, 0, TAIL)
            pool.wait_ge(S["tiles_ready"], 1)
            for e in range(NX):
                nc.gpsimd.indirect_dma_start(
                    out=send_d, out_offset=bass.IndirectOffsetOnAxis(ap=padu[:, e:e + 1], axis=0),
                    in_=zrow[:, :], in_offset=None).then_inc(S["pads"], 16)

            pool.wait_ge(S["back_slots"], 1)
            pool.wait_ge(S["yst0"], 16 * (MT // 2))
            pool.wait_ge(S["yst1"], 16 * (MT // 2))
            base = link.n[0]

            def gather_back(t, b, rows_=P):
                for c in range(2):
                    nc.gpsimd.tensor_copy(slot_now[b][0:rows_, c:c + 1], slots_u[0:rows_, c, bass.ds(t, 1)]).then_inc(S["pool"], 1)
                pool.wait_ge(S["pool"], t * 2 + (base + 2))
                settle(pool)
                for c, y in ((0, ya), (1, yc)):
                    nc.gpsimd.indirect_dma_start(
                        out=y[b][0:rows_], out_offset=None, in_=back_d,
                        in_offset=bass.IndirectOffsetOnAxis(ap=slot_now[b][0:rows_, c:c + 1], axis=0)).then_inc(S[f"ya{b}"], 16)
            for b in range(2):
                gather_back(b, b)
            with pool.Fori(1, FULL // 2) as k:
                for b in range(2):
                    pool.wait_ge(S["fin_done"], k * 2 + (b - 1))
                    gather_back(k * 2 + b, b)
            pool.wait_ge(S["fin_done"], FULL - 1)
            gather_back(FULL, 0, TAIL)

        @block.scalar
        def _(act):
            eps = small[:, 0:1]
            act.wait_ge(S["angles_ok"], 1)
            nc.scalar.activation(rec[:, :, 4], theta[:, :], ACT.Sin).then_inc(S["act"], 1)
            nc.scalar.activation(rec[:, :, 3], turn[:, :], ACT.Sin).then_inc(S["act"], 1)
            act.wait_ge(S["xstats_ok"], 1)
            act.wait_ge(S["consts"], 1)
            nc.scalar.activation(rstd[:, :], mv[:, :, 1], ACT.Sqrt, bias=eps).then_inc(S["act"], 1)

            def mix_act(q, W):
                nt = (W + P - 1) // P
                act.wait_ge(S["xT_psum"], q + 1)
                for kb in range(KB):
                    last = nc.scalar.activation(xnT[:, kb, bass.ds(q * GRP, W)], bank[kb][:, 0:W], ACT.Copy)
                last.then_inc(S["xT_done"], 1)
                act.wait_ge(S["ebias_ready"], q + 1)
                nc.scalar.activation(alpha[:, :], dm[:, :], ACT.Exp).then_inc(S["alpha_ready"], 1)
                for kb in range(KB):
                    last = nc.scalar.activation(ex[:, kb, 0:W], bank[2 + kb][:, 0:W], ACT.Exp,
                                                bias=ebias[:, kb:kb + 1], accum_out=gsum[:, kb:kb + 1])
                last.then_inc(S["exp_done"], 1)
            with act.Fori(0, NG12) as q:
                mix_act(q, GRP)
            mix_act(NG12, TAIL)
            act.wait_ge(S["lamstats_ok"], 1)
            nc.scalar.activation(small[:, 4:6], small[:, 6:8], ACT.Sqrt, bias=eps).then_inc(S["act"], 1)

            act.wait_ge(S["ngroups"], 1)
            n = act.value_load(n_groups_i[0:1, 0:1], min_val=1, max_val=4 * NE)

            def apply_v(k, g):
                act.wait_ge(S["V_psum"], k * G + (g + 1))
                nc.scalar.activation(Vs[:, :], apV[:, 0:D], ACT.Copy).then_inc(S["V_done"], 1)

            act.sem_inc(S["GT_done"], 1)
            with act.Fori(0, n) as k:
                act.wait_ge(S["LT_psum"], k + 1)
                nc.scalar.activation(WK[:, :, 0:P], Lnext[:, :, :], ACT.Copy)
                for h in range(2):
                    last = nc.scalar.activation(WK[:, 2 * h:2 * h + 2, P:2 * P], pw[h][:, :, P:2 * P], ACT.Copy)
                last.then_inc(S["WK_act"], 1)
                for s in range(2 * LEVELS):
                    lv, hf = s // 2, s % 2
                    if lv < LEVELS - 1:
                        act.wait_ge(S["sq_psum"], k * (2 * LEVELS) + (s + 1))
                        nc.scalar.activation(WK[:, 2 * hf:2 * hf + 2, 0:2 * P], pw[hf], ACT.Copy).then_inc(S["WK_act"], 1)
                    if 1 <= s <= 2 * G and s % 2 == 1:
                        apply_v(k, s // 2)
                act.wait_ge(S["GT_psum"], k + 1)
                for h in range(2):
                    last = nc.scalar.activation(GT[:, 2 * h:2 * h + 2, :], pw[h], ACT.Copy)
                last.then_inc(S["GT_done"], 1)
            for g in range(G):
                apply_v(n, g)

            def tile_act(t, b, rows_=P):
                if not isinstance(t, int) or t >= 2:
                    act.wait_ge(S["x2_psum"], t - 1)
                nc.scalar.activation(stg[b][:, :].rearrange("p (k n) -> p k n", k=KB)[:, :, 0:rows_], xnT[:, :, bass.ds(t * P, rows_)],
                                     ACT.Copy).then_inc(S["stg_done"], 1)

            def std_act(t):
                act.wait_ge(S["std_need"], t * 2 + 1)
                nc.scalar.activation(sc2[:, 0:1], mv2[:, 1:2], ACT.Sqrt, bias=eps).then_inc(S["std_done"], 1)
                act.wait_ge(S["std_need"], t * 2 + 2)
                nc.scalar.activation(sc2[:, 3:4], sc2[:, 2:3], ACT.Sqrt, bias=eps).then_inc(S["std_done"], 1)
                act.wait_ge(S["xfT_psum"], t + 1)
                nc.scalar.activation(xfT[:, :], bank[1][:, 0:D], ACT.Copy).then_inc(S["xfT_done"], 1)
            tile_act(0, 0)
            tile_act(1, 1)
            with act.Fori(0, FULL // 2 - 1) as k:
                for b in range(2):
                    std_act(k * 2 + b)
                    tile_act(k * 2 + (b + 2), b)
            std_act(FULL - 2)
            tile_act(FULL, 0, TAIL)
            std_act(FULL - 1)
            std_act(FULL)
            act.wait_ge(S["wexp_need"], 1)
            nc.scalar.activation(wexp[:, :], topd[:, :], ACT.Exp).then_inc(S["wexp_done"], 1)

            def moe_act(i, b):
                act.wait_ge(S["xmT_psum"], i + 1)
                nc.scalar.activation(xmT[b], bank[b][:, 0:D], ACT.Copy).then_inc(S["xmT_done"], 1)

            def moe_gelu(i, b):
                act.wait_ge(S["hpre_done"], i + 2)
                nc.scalar.activation(hact[b], hpre[b], ACT.Gelu).then_inc(S["hact_done"], 1)

            def moe_store(i, b):
                act.wait_ge(S["y_done"], i + 2)
                act.dma_start(back_d[bass.ds(i * P, P), :], yb[b]).then_inc(S[f"yst{b}"], 16)
            act.wait_ge(S["tiles_ready"], 1)
            act.sem_inc(S["xmT_done"], 1)
            moe_act(0, 0)
            with act.Fori(0, MT // 2 - 1) as k:
                for b in range(2):
                    moe_act(k * 2 + (b + 1), 1 - b)
                    moe_gelu(k * 2 + b, b)
                    moe_store(k * 2 + b, b)
            moe_act(MT - 1, 1)
            for i in (MT - 2, MT - 1):
                moe_gelu(i, i % 2)
                moe_store(i, i % 2)

            def store_out(t, b, rows_=P):
                act.wait_ge(S["fin_done"], t + 1)
                if rows_ == P:
                    act.dma_start(out[bass.ds(t * P, P), :], xt[b][:, :]).then_inc(S[f"out{b}"], 16)
                else:
                    act.dma_start(out[FULL * P:N, :], xt[b][0:rows_, :]).then_inc(S[f"out{b}"], 16)
            with act.Fori(0, FULL // 2) as k:
                for b in range(2):
                    store_out(k * 2 + b, b)
            store_out(FULL, 0, TAIL)
            act.wait_ge(S["out0"], 16 * (FULL // 2 + 1))
            act.wait_ge(S["out1"], 16 * (FULL // 2))

        @block.vector
        def _(dve):
            link = chain(dve, S["dve"])
            TT, TS, STT = nc.vector.tensor_tensor, nc.vector.tensor_scalar, nc.vector.scalar_tensor_tensor

            dve.wait_ge(S["consts"], 1)
            link(nc.vector.memset(mv[:, :, :], 0.0))
            link(nc.vector.memset(Mrot[:, :, :], 0.0))
            dve.wait_ge(S["edges"], 48)
            link(nc.vector.tensor_copy(i_f, i_raw))
            link(nc.vector.tensor_copy(j_f, j_raw))
            TS(g_i, i_f, float(D), None, ALU.is_ge)
            link(TS(g_j, j_f, float(D), None, ALU.is_ge))
            link(TT(incl, g_i, g_j, ALU.add))
            link(TS(cnt, incl, -1.0, 2.0, ALU.mult, ALU.add))
            TS(rec[:, :, 0], i_f, float(D - 1), None, ALU.min)
            TS(rec[:, :, 2], j_f, float(D - 1), None, ALU.min)
            nc.vector.tensor_copy(rec[:, :, 6], g_i)
            link(nc.vector.tensor_tensor_scan(incl, ones[0:EP, 0:1].broadcast_to([EP, EL]), cnt, 0.0, ALU.mult, ALU.add))
            dve.sem_inc(S["scan_ok"], 1)
            link(TT(rec[:, :, 1], rec[:, :, 2], rec[:, :, 0], ALU.subtract))
            dve.wait_ge(S["pe"], 1)
            nc.vector.tensor_copy(poff[:, :], misc[:, 0:1])
            link(nc.vector.tensor_copy(total[:, :], misc[:, 1:2]))
            link(TS(incl, incl, poff[0:EP, :], None, ALU.add))
            link(TS(small[0:1, 1:2], total[0:1, :], CAP * G - 0.5, 1.0 / (CAP * G), ALU.add, ALU.mult))
            link(TS(small[0:1, 1:2], small[0:1, 1:2], 1.0, None, ALU.max))
            nc.vector.tensor_copy(n_groups_i[:, :], small[0:1, 1:2]).then_inc(S["ngroups"], 1)
            link(TT(rec[:, :, 5], incl, cnt, ALU.subtract))
            nc.vector.memset(rec[:, :, 7], 0.0).then_inc(S["recs_out"], 1)
            link(TS(turn, theta, 1.0 / (2 * PI), MAGIC, ALU.mult, ALU.add))
            link(TS(turn, turn, -MAGIC, None, ALU.add))
            for part in (TURN_HI, TURN_MID, TURN_LO):
                link(STT(theta, turn, -part, theta, ALU.mult, ALU.add))
            link(TS(theta, theta, 3.1415925, -3.1415925, ALU.min, ALU.max))
            link(STT(turn, theta, -1.0, theta, ALU.mult, ALU.max))
            link(TS(turn, turn, -1.0, PI / 2, ALU.mult, ALU.add))
            dve.sem_inc(S["angles_ok"], 1)
            for c in range(0, FULL, 8):
                for t in range(c, c + 8):
                    if t == c:
                        dve.wait_ge(S["xld"], 16 * (NT // 8 + 1))
                    nc.vector.bn_stats(stats[:, t, :], x_all[:, t, :])
            link(nc.vector.bn_stats(stats[0:TAIL, FULL, :], x_all[0:TAIL, FULL, :]))
            for t in range(FULL):
                nc.vector.bn_aggr(mv[:, t, :], stats[:, t, :])
            link(nc.vector.bn_aggr(mv[0:TAIL, FULL, :], stats[0:TAIL, FULL, :]))
            dve.sem_inc(S["xstats_ok"], 1)
            dve.wait_ge(S["act"], 2)
            nc.vector.memset(run_m[:, :], -1e30).then_inc(S["recs_out"], 1)
            nc.vector.memset(ssum[:, :], 0.0)
            link(nc.vector.memset(Pacc[:, :, :], 0.0))
            dve.wait_ge(S["act"], 3)
            link(nc.vector.reciprocal(rstd[:, :], rstd[:, :]))
            link(STT(nmr[:, :], mv[:, :, 0], -1.0, rstd[:, :], ALU.mult, ALU.mult))
            base = link.n[0]
            PERM = 5

            def mix_dve(q, W):
                nt, tail = (W + P - 1) // P, W % P
                r = tail or P
                dve.wait_ge(S["mix_psum"], q + 1)
                for t in range(nt):
                    tt = q * 4 + t
                    last = TS(xng[0:r, t, :], x_all[0:r, bass.ds(tt, 1), :].rearrange("p a d -> p (a d)"),
                              rstd[0:r, bass.ds(tt, 1)], nmr[0:r, bass.ds(tt, 1)], ALU.mult, ALU.add)
                last.then_inc(S["xn_ready"], 1)
                n0 = q * PERM + base
                dve.wait_ge(S["keys_psum"], q + 1)
                for kb in range(KB):
                    last = nc.vector.reduce_max(grp_m[:, kb:kb + 1], bank[2 + kb][:, 0:W], AX_X)
                last.then_inc(S["dve"], 1)
                dve.wait_ge(S["dve"], n0 + 1)
                TT(new_m[:, :], run_m[:, :], grp_m[:, :], ALU.max).then_inc(S["dve"], 1)
                dve.wait_ge(S["dve"], n0 + 2)
                TT(dm[:, :], run_m[:, :], new_m[:, :], ALU.subtract)
                TT(ebias[:, :], bk_c[:, :], new_m[:, :], ALU.subtract).then_inc(S["dve"], 1)
                dve.wait_ge(S["dve"], n0 + 3)
                TT(ebias[:, :], ebias[:, :], bk_c[:, :], ALU.subtract).then_inc(S["ebias_ready"], 1)
                nc.vector.tensor_copy(run_m[:, :], new_m[:, :])
                dve.wait_ge(S["exT_psum"], q + 1)
                for kb in range(KB):
                    last = nc.vector.tensor_copy(exT[0:r, 0:nt, kb * P:(kb + 1) * P],
                                                 bank[4 + kb][0:r, 0:nt * P].rearrange("p (t d) -> p t d", d=P))
                last.then_inc(S["exT_done"], 1)
                dve.wait_ge(S["alpha_ready"], q + 1)
                TT(ssum[:, :], ssum[:, :], alpha[:, :], ALU.mult).then_inc(S["dve"], 1)
                dve.wait_ge(S["dve"], n0 + 4)
                dve.wait_ge(S["exp_done"], q + 1)
                TT(ssum[:, :], ssum[:, :], gsum[:, :], ALU.add).then_inc(S["dve"], 1)
                dve.wait_ge(S["dve"], n0 + 5)
                dve.wait_ge(S["mix_psum"], q + 2)
                for kb in range(KB):
                    last = STT(Pacc[:, kb, :], Pacc[:, kb, :], alpha[:, kb:kb + 1], bank[6][:, kb * D:(kb + 1) * D],
                               ALU.mult, ALU.add)
                last.then_inc(S["mix_acc"], 1)
            dve.wait_ge(S["wload"], 16 * 12)
            dve.wait_ge(S["consts"], 1)
            dve.sem_inc(S["mix_acc"], 1)
            with dve.Fori(0, NG12) as q:
                mix_dve(q, GRP)
            mix_dve(NG12, TAIL)
            link.n[0] = base + PERM * (NG12 + 1)
            link(nc.vector.reciprocal(rsum[:, :], ssum[:, :]))
            dve.wait_ge(S["mix_acc"], NG12 + 2)
            for kb in range(KB):
                last = TS(Pacc[:, kb, :], Pacc[:, kb, :], rsum[:, kb:kb + 1], None, ALU.mult)
            link(last)
            dve.sem_inc(S["pn_ok"], 1)
            dve.wait_ge(S["pe"], 2)
            link(nc.vector.tensor_copy(PT, bank[0][:, :].rearrange("p (a b) -> p a b", a=KB)))
            dve.sem_inc(S["pT_ok"], 1)
            link(nc.vector.tensor_copy(wqT[:, :, :], bank[1][:, :].rearrange("p (a b) -> p a b", a=KB)))
            dve.wait_ge(S["pe"], 3)
            for kb in range(KB):
                last = TT(lam[:, kb, :], bank[2][:, kb * D:(kb + 1) * D], bvB[:, :], ALU.add)
            link(last)
            for kb in range(KB):
                last = nc.vector.bn_stats(stats[:, kb, :], lam[:, kb, :])
            link(last)
            for kb in range(KB):
                last = nc.vector.bn_aggr(mv[:, kb, :], stats[:, kb, :])
            link(last)
            link(nc.vector.tensor_copy(small[:, 6:8], mv[:, 0:KB, 1]))
            dve.sem_inc(S["lamstats_ok"], 1)
            dve.wait_ge(S["act"], 4)
            link(nc.vector.reciprocal(small[:, 8:10], small[:, 4:6]))
            link(TT(small[:, 8:10], small[:, 8:10], bng_c[:, :], ALU.mult))
            for kb in range(KB):
                last = TS(lam[:, kb, :], lam[:, kb, :], mv[:, kb, 0:1], small[:, 8 + kb:9 + kb], ALU.subtract, ALU.mult)
            link(last)
            for kb in range(KB):
                last = TS(bn[:, kb, :], lam[:, kb, :], bnb_c[:, kb:kb + 1], None, ALU.add)
            link(last)
            dve.sem_inc(S["bn_ok"], 1)

            for kb in range(KB):
                last = nc.vector.tensor_copy(Mrot[:, kb, kb * P:(kb + 1) * P], ident[:, :])
            nc.vector.memset(GT[:, :, :], 0.0)
            nc.vector.memset(STm[:, :, :], 0.0)
            link(nc.vector.memset(keep[:, :, :], 1.0))
            dve.sem_inc(S["chunk_init_ok"], 1)
            dve.sem_inc(S["M_done"], 1)
            dve.wait_ge(S["ends_in"], 16)
            n = dve.value_load(n_groups_i[0:1, 0:1], min_val=1, max_val=4 * NE)
            base2 = link.n[0]
            sub, v1, v2, valid, isj, dj, tgt, tn, oth, cs, sg, co, lim, csb, cob, lastw = [fld[:, i, :] for i in range(16)]
            f_blk, f_pos, f_edge = [fld[:, i, :] for i in range(16, 19)]
            posA, posB, posL = [pos[:, i, :] for i in range(3)]
            c_t, c_o, c_cs, c_co, c_last = [cur[:, i, :] for i in range(5)]
            count = {}

            def steps(name, per, order=[0]):
                count[name] = order[0]
                order[0] += per
                return order[0]
            steps("search", 2)
            steps("pos", 3)
            steps("fields", 7)
            steps("L", 5)
            PER = steps("swap", 1)

            def after(k, name, i):
                dve.wait_ge(S["dve"], k * PER + (base2 + count[name] + i))

            def sig(ins):
                ins.then_inc(S["dve"], 1)

            def search(k):
                for g in range(G):
                    last = TS(junk[:, g, :], ends, slotnum[:, g:g + 1], 0.0, ALU.is_le, ALU.add, accum_out=f_blk[:, g:g + 1])
                sig(last)
                after(k, "search", 1)
                sig(TS(f_blk, f_blk, float(NB - 1), None, ALU.min))
                after(k, "search", 2)
                nc.vector.tensor_copy(idx[:, 0, :], f_blk).then_inc(S["blk_ready"], 1)

            def search_in(k):
                dve.wait_ge(S["rows_in"], k * (16 * G) + 16 * G)
                for g in range(G):
                    last = TS(junk[:, g, 0:BL], rows[:, g, :], slotnum[:, g:g + 1], 0.0, ALU.is_le, ALU.add,
                              accum_out=f_pos[:, g:g + 1])
                sig(last)
                after(k, "pos", 1)
                sig(STT(f_edge, f_blk, float(BL), f_pos, ALU.mult, ALU.add))
                after(k, "pos", 2)
                sig(TS(f_edge, f_edge, float(NE - 1), None, ALU.min))
                after(k, "pos", 3)
                nc.vector.tensor_copy(idx[:, 1, :], f_edge).then_inc(S["pos_ready"], 1)

            def fields(k):
                dve.wait_ge(S["recs_in"], k * (16 * G) + 16 * G)
                r_i, r_d, r_j, r_c, r_s, r_n, r_g = [recs[:, :, i] for i in range(7)]
                sig(TT(sub, slotnum[:, :], r_n, ALU.subtract))
                after(k, "fields", 1)
                TS(v1, sub, minsub[:, :], None, ALU.is_ge)
                TS(lim, sub, -1.0, prow[:, :], ALU.mult, ALU.add)
                sig(TT(isj, sub, r_g, ALU.add))
                after(k, "fields", 2)
                STT(v2, sub, maxsub[:, :], v1, ALU.is_le, ALU.mult)
                TS(sg, isj, 2.0, -1.0, ALU.mult, ALU.add)
                sig(TT(dj, isj, r_d, ALU.mult))
                after(k, "fields", 3)
                STT(valid, slotnum[:, :], total[:, :], v2, ALU.is_lt, ALU.mult)
                TT(tgt, dj, r_i, ALU.add)
                TT(oth, r_j, dj, ALU.subtract)
                sig(TT(co, r_s, sg, ALU.mult))
                after(k, "fields", 4)
                STT(tn, tgt, NOROW, valid, ALU.subtract, ALU.mult)
                TT(cs, r_c, valid, ALU.mult)
                sig(TT(co, co, valid, ALU.mult))
                after(k, "fields", 5)
                sig(TS(tgt, tn, NOROW, None, ALU.add))
                after(k, "fields", 6)
                sig(TS(slotnum[:, :], slotnum[:, :], float(CAP * G), None, ALU.add))
                after(k, "fields", 7)
                nc.vector.tensor_copy(tb16, tgt).then_inc(S["flds_ready"], 1)

            def build_L(k):
                dve.wait_ge(S["TB_psum"], k + 1)
                for g in range(G):
                    last = STT(slotmask[:, g, :], col0[:, 0:P], lim[:, g:g + 1], col1[:, :], ALU.is_lt, ALU.mult)
                sig(last)
                after(k, "L", 1)
                for g in range(G):
                    tb = TB[:, g * P:(g + 1) * P]
                    STT(hits[:, g, :], tb, tgt[:, g:g + 1], slotmask[:, g, :], ALU.is_equal, ALU.mult)
                    STT(hits[:, G + g, :], tb, oth[:, g:g + 1], slotmask[:, g, :], ALU.is_equal, ALU.mult)
                    last = STT(hits[:, 2 * G + g, :], tb, tgt[:, g:g + 1], col1[:, :], ALU.is_equal, ALU.mult)
                sig(last)
                after(k, "L", 2)
                sig(nc.vector.tensor_reduce(pos[:, :, :].rearrange("p a g -> p (a g)"), hits[:, :, :], AX_X, ALU.max))
                after(k, "L", 3)
                for g in range(G):
                    TS(Lself[:, g, :], col1[:, :], posA[:, g:g + 1], cs[:, g:g + 1], ALU.is_equal, ALU.mult)
                    TS(hits[:, g, :], col1[:, :], posB[:, g:g + 1], co[:, g:g + 1], ALU.is_equal, ALU.mult)
                STT(csb, posA, 0.0, cs, ALU.is_equal, ALU.mult)
                STT(cob, posB, 0.0, co, ALU.is_equal, ALU.mult)
                sig(TS(lastw, posL, prow1[:, :], None, ALU.is_equal))
                after(k, "L", 4)
                sig(TT(Lnext[:, :, :], Lself[:, :, :], hits[:, 0:G, :], ALU.add))
                after(k, "L", 5)

            def swap(k):
                for dst_, s_ in ((c_t, tgt), (c_o, oth), (c_cs, csb), (c_co, cob), (c_last, lastw)):
                    last = nc.vector.tensor_copy(dst_, s_)
                sig(last)
                after(k, "swap", 1)

            def apply_m(k, g):
                dve.wait_ge(S["M_psum"], k * G + (g + 1))
                for kb in range(KB):
                    last = STT(Mrot[:, kb, :], Mrot[:, kb, :], keep[:, g, kb:kb + 1], apM[:, kb * D:(kb + 1) * D],
                               ALU.mult, ALU.add)
                last.then_inc(S["M_done"], 1)

            search(0)
            search_in(0)
            fields(0)
            build_L(0)
            dve.sem_inc(S["Lready"], 1)
            with dve.Fori(0, n) as k:
                k1 = k + 1
                swap(k)
                dve.wait_ge(S["WK_act"], k * (1 + 2 * (LEVELS - 1)) + 1)
                for g in range(G):
                    last = TT(WK[:, g, 2 * P:3 * P], ident[:, :], WK[:, g, P:2 * P], ALU.add)
                last.then_inc(S["WK_dve"], 1)
                for s in range(2 * LEVELS):
                    lv, hf = s // 2, s % 2
                    if lv >= 1:
                        dve.wait_ge(S["sq_psum"], k * (2 * LEVELS) + (s + 1))
                        TT(WK[:, 2 * hf:2 * hf + 2, 2 * P:3 * P], WK[:, 2 * hf:2 * hf + 2, 2 * P:3 * P], jb[hf],
                           ALU.add).then_inc(S["WK_dve"], 1)
                    if s == 0:
                        search(k1)
                    if s in (2, 4, 6, 8):
                        apply_m(k, s // 2 - 1)
                    if s in (1, 3):
                        for g in (s - 1, s):
                            TS(Bself[:, g, :], col0[:, :], c_t[:, g:g + 1], c_cs[:, g:g + 1], ALU.is_equal, ALU.mult)
                            last = TS(Bmat[:, g, :], col0[:, :], c_o[:, g:g + 1], c_co[:, g:g + 1], ALU.is_equal, ALU.mult)
                        last.then_inc(S["B_ready"], 1)
                    if s == 5:
                        dve.wait_ge(S["B_ready"], k * 3 + 2)
                        TT(Bmat[:, :, :], Bmat[:, :, :], Bself[:, :, :], ALU.add).then_inc(S["B_ready"], 1)
                        search_in(k1)
                    if s == 9:
                        for g in range(G):
                            last = TS(STm[:, g, :], col0[:, :], c_t[:, g:g + 1], c_last[:, g:g + 1], ALU.is_equal, ALU.mult)
                        last.then_inc(S["ST_ready"], 1)
                        fields(k1)
                    if s == 11:
                        build_L(k1)
                        dve.sem_inc(S["Lready"], 1)
                dve.wait_ge(S["D_psum"], k + 1)
                TS(keep[:, :, :], misc[:, 0:G * KB].rearrange("p (g k) -> p g k", g=G), -1.0, 1.0, ALU.mult,
                   ALU.add).then_inc(S["D_done"], 1)
                dve.wait_ge(S["D_done"], k + 1)
            for g in range(G):
                apply_m(n, g)
            dve.wait_ge(S["comb_pe"], 1)
            nc.vector.tensor_copy(comb[:, :, :], bank[0][:, :].rearrange("p (a b) -> p a b", a=KB)).then_inc(S["comb_dve"], 1)
            nc.vector.tensor_copy(addrow[:, :], bank[2][:, 0:D]).then_inc(S["comb_dve"], 1)
            dve.wait_ge(S["comb_dve"], 2)
            TT(comb[:, :, :], comb[:, :, :], bank[1][:, :].rearrange("p (a b) -> p a b", a=KB), ALU.add)\
                .then_inc(S["comb_dve"], 1)
            nc.vector.memset(msk[:, :], 0.0)
            nc.vector.memset(mskb[:, :], 0.0)
            nc.vector.memset(topd[:, :], 0.0)
            nc.vector.memset(slots_f[:, :, :], 0.0)
            nc.vector.memset(experts_f[:, :, :], 0.0)
            nc.vector.tensor_copy(base8[:, :], reg8[:, :]).then_inc(S["comb_dve"], 1)
            dve.wait_ge(S["comb_dve"], 4)

            PT_ = 13

            def tile_dve(t, b, rows_=P):
                r = slice(0, rows_)

                def own(i):
                    dve.wait_ge(S["x2_done"] if i == 0 else S["w_ready"], (t + 1) if i == 0 else t * PT_ + i)
                    settle(dve)

                def mark(ins):
                    ins.then_inc(S["w_ready"], 1)
                half = (t // 2) if isinstance(t, int) else None
                dve.wait_ge(S["x2_psum"], t + 1)
                x2 = x2_all[r, bass.ds(t, 1), :].rearrange("p a d -> p (a d)")
                mark(TT(x2, bank[0][r, 0:D], addrow[r, :], ALU.add))
                own(1)
                TT(x2, x2, xt[b][r, :], ALU.add).then_inc(S["x2_done"], 1)
                own(0)
                mark(nc.vector.bn_stats(st2[r, :], x2))
                own(2)
                nc.vector.bn_aggr(mv2[r, :], st2[r, :]).then_inc(S["std_need"], 1)
                dve.wait_ge(S["std_done"], t * 2 + 1)
                mark(nc.vector.reciprocal(sc2[:, 1:2], sc2[:, 0:1]))
                own(3)
                mark(TT(sc2[:, 2:3], sc2[:, 1:2], mv2[:, 1:2], ALU.mult))
                own(4)
                TT(sc2[:, 2:3], sc2[:, 2:3], sc2[:, 1:2], ALU.mult).then_inc(S["std_need"], 1)
                dve.wait_ge(S["std_done"], t * 2 + 2)
                mark(nc.vector.reciprocal(sc2[:, 4:5], sc2[:, 3:4]))
                own(5)
                mark(TT(sc2[:, 5:6], sc2[:, 4:5], sc2[:, 1:2], ALU.mult))
                own(6)
                xw = xf[b]
                mark(TS(xw[r, :], x2, mv2[r, 0:1], sc2[r, 5:6], ALU.subtract, ALU.mult))
                own(7)
                mark(TT(xw[r, :], xw[r, :], gamB[r, :], ALU.mult))
                own(8)
                TT(xw[r, :], xw[r, :], betB[r, :], ALU.add).then_inc(S["xf_ready"], 1)
                dve.wait_ge(S["lg_psum"], t + 1)
                mark(TT(lg[r, :], bank[2][r, 0:NX], brB[r, :], ALU.add))
                own(9)
                mark(nc.vector.max(top[r, :], lg[r, :]))
                own(10)
                TT(topd[r, bass.ds(t, 1)], top[r, 1:2], top[r, 0:1], ALU.subtract)
                mark(nc.vector.max_index(topi[r, :], top[r, :], lg[r, :]))
                own(11)
                mark(nc.vector.tensor_copy(topf[r, :], topi[r, :]))
                own(12)
                for c in range(2):
                    last = TS(oh[r, c, :], col0[r, 0:NX], topf[r, c:c + 1], None, ALU.is_equal)
                mark(last)
                own(13)
                if rows_ < P:
                    nc.vector.memset(mskb[:, :], 0.0).then_inc(S["mskb_zero"], 1)
                    dve.wait_ge(S["mskb_zero"], 1)
                TT(mskb[r, :], oh[r, 0, :], oh[r, 1, :], ALU.add).then_inc(S["msk_ready"], 1)
                dve.wait_ge(S["rank_psum"], t + 1)
                TT(slot8[:, :], misc[:, 0:NX], base8[:, :], ALU.add).then_inc(S["slot8"], 1)
                dve.wait_ge(S["slot8"], t * 4 + 1)
                TT(base8[:, :], misc[:, NX:2 * NX], base8[:, :], ALU.add)
                for c in range(2):
                    last = nc.vector.tensor_tensor_reduce(junk8[r, :], oh[r, c, :], slot8[r, :], 1.0, 0.0, ALU.mult,
                                                          ALU.add, sl2[r, c:c + 1])
                    last.then_inc(S["slot8"], 1)
                    dve.wait_ge(S["slot8"], t * 4 + (2 + c))
                nc.vector.tensor_copy(slots_f[r, :, bass.ds(t, 1)], sl2[r, :].rearrange("p (a b) -> p a b", b=1))
                nc.vector.tensor_copy(experts_f[r, :, bass.ds(t, 1)], topf[r, 0:2].rearrange("p (a b) -> p a b", b=1))
                nc.vector.tensor_copy(slot_now[b][r, :], sl2[r, :])\
                    .then_inc(S["slot8"], 1)
                dve.wait_ge(S["slot8"], t * 4 + 4)
                dve.sem_inc(S["slot_ready"], 1)

            dve.wait_ge(S["wload"], 16 * 12)
            first = [True]

            def tile_wait(k, b):
                dve.wait_ge(S[f"xt{b}"], k * 16 + 16)
            tile_wait(0, 0)
            tile_dve(0, 0)
            tile_wait(0, 1)
            tile_dve(1, 1)
            with dve.Fori(1, FULL // 2) as k:
                for b in range(2):
                    dve.wait_ge(S[f"xt{b}"], k * 16 + 16)
                    dve.wait_ge(S[f"sc{b}"], k * 32)
                    tile_dve(k * 2 + b, b)
            dve.wait_ge(S["xt0"], (FULL // 2) * 16 + 16)
            dve.wait_ge(S["sc0"], (FULL // 2) * 32)
            tile_dve(FULL, 0, TAIL)
            dve.sem_inc(S["wexp_need"], 1)
            tl = chain(dve, S["tl"])
            tl(TT(padf[:, :], base8[:, :], ones[:, 0:NX], ALU.mult))
            tl(TS(padf[:, :], padf[:, :], prow[:, :], None, ALU.add))
            nc.vector.tensor_copy(padu[:, :], padf[:, :])
            tl(TT(ntile[:, 0, :], base8[:, :], reg8[:, :], ALU.subtract))
            tl(TS(ntile[:, 0, :], ntile[:, 0, :], 1.0 / P, 0.5 - 1.0 / (2 * P), ALU.mult, ALU.add))
            tl(TS(ntile[:, 0, :], ntile[:, 0, :], MAGIC, None, ALU.add))
            tl(TS(ntile[:, 0, :], ntile[:, 0, :], -MAGIC, None, ALU.add))
            tl(nc.vector.tensor_tensor_scan(ntile[:, 1, :], ones[:, 0:NX], ntile[:, 0, :], 0.0, ALU.mult, ALU.add))
            tl(TS(ntile[:, 2, :], ntile[:, 0, :], -float(P), float(STRIDE), ALU.mult, ALU.add))
            tl(nc.vector.memset(tacc[:, 0, :], 0.0))
            tl(TS(tacc[:, 1, :], tnum[:, :], float(P), None, ALU.mult))
            for e in range(NX):
                tl(TS(tacc[:, 2, :], tnum[:, :], ntile[0:1, 1, e:e + 1], None, ALU.is_ge))
                tl(TT(tacc[:, 0, :], tacc[:, 0, :], tacc[:, 2, :], ALU.add))
                tl(STT(tacc[:, 1, :], tacc[:, 2, :], ntile[0:1, 2, e:e + 1], tacc[:, 1, :], ALU.mult, ALU.add))
            tl(TS(tacc[:, 0, :], tacc[:, 0, :], float(NX - 1), None, ALU.min))
            tl(nc.vector.tensor_copy(ttab[:, :, :], tacc[:, 0:2, :]))
            dve.sem_inc(S["tiles_ready"], 1)
            tl(TT(ntile[:, 3, :], ntile[:, 1, :], ntile[:, 0, :], ALU.subtract))
            tl(TS(ntile[:, 3, :], ntile[:, 3, :], float(P), None, ALU.mult))
            tl(TT(ntile[:, 3, :], ntile[:, 3, :], reg8[:, :], ALU.subtract))
            for e in range(NX):
                tl(TS(moved[:, :, :], experts_f[:, :, :], float(e), ntile[:, 3, e:e + 1], ALU.is_equal, ALU.mult))
                tl(TT(slots_f[:, :, :], slots_f[:, :, :], moved[:, :, :], ALU.add))
            nc.vector.tensor_copy(slots_u[:, :, :], slots_f[:, :, :]).then_inc(S["back_slots"], 1)
            dve.wait_ge(S["wexp_done"], 1)
            tl(TS(w_a[:, :], wexp[:, :], 1.0, None, ALU.add))
            tl(nc.vector.reciprocal(w_a[:, :], w_a[:, :]))
            tl(TT(w_b[:, :], w_a[:, :], wexp[:, :], ALU.mult))

            dve.wait_ge(S["bias_loaded"], 32)

            def moe_h(i, b):
                e = dve.value_load(ttab[0:1, 0, bass.ds(i, 1)], min_val=0, max_val=NX - 1)
                dve.wait_ge(S["h_psum"], i + 1)
                TT(hpre[b], bank[2 + b][:, 0:H], b1B[:, bass.ds(e, 1), :].rearrange("p a h -> p (a h)"),
                   ALU.add).then_inc(S["hpre_done"], 1)
                return e

            def moe_hT(i, b):
                dve.wait_ge(S["hT_psum"], i + 1)
                nc.vector.tensor_copy(hT[b], bank[4 + b][:, 0:H]).then_inc(S["hT_done"], 1)

            def moe_y(i, b, e):
                dve.wait_ge(S["y_psum"], i + 1)
                TT(yb[b], bank[6 + b][:, 0:D], b2B[:, bass.ds(e, 1), :].rearrange("p a h -> p (a h)"),
                   ALU.add).then_inc(S["y_done"], 1)

            def moe_dve(i, b, k, more=True):
                e = dve.value_load(ttab[0:1, 0, bass.ds(i, 1)], min_val=0, max_val=NX - 1)
                if more:
                    moe_h(i + 1, 1 - b)
                moe_hT(i, b)
                if not isinstance(k, int) or k > 0:
                    dve.wait_ge(S[f"yst{b}"], k * 16)
                moe_y(i, b, e)
            dve.sem_inc(S["hpre_done"], 1)
            dve.sem_inc(S["y_done"], 1)
            moe_h(0, 0)
            moe_dve(0, 0, 0)
            moe_dve(1, 1, 0)
            with dve.Fori(1, MT // 2 - 1) as k:
                for b in range(2):
                    moe_dve(k * 2 + b, b, k)
            moe_dve(MT - 2, 0, MT // 2 - 1)
            moe_dve(MT - 1, 1, MT // 2 - 1, more=False)

            def final(t, b, k, rows_=P):
                r = slice(0, rows_)
                dve.wait_ge(S[f"ya{b}"], k * 32 + 32)
                if not isinstance(k, int) or k > 0:
                    dve.wait_ge(S[f"out{b}"], k * 16)
                STT(ya[b][r], ya[b][r], w_a[r, bass.ds(t, 1)],
                    x2_all[r, bass.ds(t, 1), :].rearrange("p a d -> p (a d)"), ALU.mult, ALU.add).then_inc(S["ya_sum"], 1)
                dve.wait_ge(S["ya_sum"], t + 1)
                STT(xt[b][r, :], yc[b][r], w_b[r, bass.ds(t, 1)], ya[b][r], ALU.mult, ALU.add)\
                    .then_inc(S["fin_done"], 1)
            final(0, 0, 0)
            final(1, 1, 0)
            with dve.Fori(1, FULL // 2) as k:
                for b in range(2):
                    final(k * 2 + b, b, k)
            final(FULL, 0, FULL // 2, TAIL)

        @block.tensor
        def _(pe):
            link = chain(pe, S["pe"])
            mm, tr = nc.tensor.matmul, nc.tensor.transpose
            pe.wait_ge(S["consts"], 1)
            pe.wait_ge(S["scan_ok"], 1)
            mm(misc[:, 0:1], tri[0:EP, :], incl[:, EL - 1:EL], start=True, stop=True)
            mm(misc[:, 1:2], ones[0:EP, :], incl[:, EL - 1:EL], start=True, stop=True).then_inc(S["pe"], 1)

            pe.wait_ge(S["wload"], 16 * 12)

            def mix_pe(q, W):
                nt, tail = (W + P - 1) // P, W % P
                r = tail or P
                first = isinstance(q, int) and q == 0
                pe.wait_ge(S["xn_ready"], q + 1)
                for kb in range(KB):
                    for t in range(nt):
                        last = tr(bank[kb][:, t * P:t * P + r], xng[0:r, t, kb * P:(kb + 1) * P], ident[0:r, 0:r])
                last.then_inc(S["xT_psum"], 1)
                pe.wait_ge(S["xT_done"], q + 1)
                for db in range(KB):
                    for kb in range(KB):
                        last = mm(bank[2 + db][:, 0:W], wk[:, kb, db * P:(db + 1) * P],
                                  xnT[:, kb, bass.ds(q * GRP, W)], start=(kb == 0), stop=(kb == KB - 1))
                last.then_inc(S["keys_psum"], 1)
                pe.wait_ge(S["exp_done"], q + 1)
                for kb in range(KB):
                    for t in range(nt):
                        last = tr(bank[4 + kb][0:r, t * P:(t + 1) * P], ex[:, kb, t * P:t * P + r], ident[:, :])
                last.then_inc(S["exT_psum"], 1)
                pe.wait_ge(S["exT_done"], q + 1)
                pe.wait_ge(S["mix_acc"], q + 1)
                for kb in range(KB):
                    for t in range(nt):
                        last = mm(bank[6][:, kb * D:(kb + 1) * D], exT[0:r, t, kb * P:(kb + 1) * P], xng[0:r, t, :],
                                  start=(t == 0), stop=(t == nt - 1))
                last.then_inc(S["mix_psum"], 1)
            pe.sem_inc(S["mix_psum"], 1)
            with pe.Fori(0, NG12) as q:
                mix_pe(q, GRP)
            mix_pe(NG12, TAIL)

            pe.wait_ge(S["pn_ok"], 1)
            for src_, bk in ((Pacc, 0), (wq, 1)):
                for a in range(KB):
                    for b in range(KB):
                        last = tr(bank[bk][:, b * D + a * P:b * D + (a + 1) * P], src_[:, a, b * P:(b + 1) * P], ident[:, :])
            last.then_inc(S["pe"], 1)
            pe.wait_ge(S["pT_ok"], 1)
            for db in range(KB):
                for kb in range(KB):
                    last = mm(bank[2][:, db * D:(db + 1) * D], PT[:, kb, db * P:(db + 1) * P], wv[:, kb, :],
                              start=(kb == 0), stop=(kb == KB - 1))
            last.then_inc(S["pe"], 1)
            pe.wait_ge(S["chunk_init_ok"], 1)

            n = pe.value_load(n_groups_i[0:1, 0:1], min_val=1, max_val=4 * NE)

            def spread_targets(k):
                pe.wait_ge(S["flds_ready"], k + 1)
                for g in range(G):
                    last = mm(TB[:, g * P:(g + 1) * P], tb16[:, g:g + 1].broadcast_to([P, P]), identb[:, :],
                              start=True, stop=True)
                last.then_inc(S["TB_psum"], 1)

            def apply_v(k, g):
                pe.wait_ge(S["M_done"], k * G + (g + 1))
                for kb in range(KB):
                    last = mm(apV[:, 0:D], GT[:, g, kb * P:(kb + 1) * P], Mrot[:, kb, :], start=(kb == 0), stop=(kb == KB - 1))
                last.then_inc(S["V_psum"], 1)

            def apply_m(k, g):
                pe.wait_ge(S["V_done"], k * G + (g + 1))
                for rb in range(KB):
                    last = mm(apM[:, rb * D:(rb + 1) * D], STm[:, g, rb * P:(rb + 1) * P], Vs[:, :], start=True, stop=True)
                last.then_inc(S["M_psum"], 1)

            spread_targets(0)
            with pe.Fori(0, n) as k:
                pe.wait_ge(S["Lready"], k + 1)
                pe.wait_ge(S["GT_done"], k + 1)
                for g in range(G):
                    last = tr(pw[g // 2][:, g % 2, P:2 * P], Lnext[:, g, :], ident[:, :])
                last.then_inc(S["LT_psum"], 1)
                NACT = 1 + 2 * (LEVELS - 1)
                NDVE = 1 + 2 * (LEVELS - 1)
                for s in range(2 * LEVELS):
                    lv, hf = s // 2, s % 2
                    pe.wait_ge(S["WK_act"], k * NACT + (1 if lv == 0 else 2 * lv + hf))
                    pe.wait_ge(S["WK_dve"], k * NDVE + (1 if lv <= 1 else 2 * (lv - 1) + hf))
                    for g in (2 * hf, 2 * hf + 1):
                        Lk, LkT, J = WK[:, g, 0:P], WK[:, g, P:2 * P], WK[:, g, 2 * P:3 * P]
                        if lv < LEVELS - 1:
                            mm(pw[hf][:, g % 2, 0:P], LkT, Lk, start=True, stop=True)
                            last = mm(pw[hf][:, g % 2, P:2 * P], Lk, LkT, start=True, stop=True)
                        if lv >= 1:
                            last = mm(jb[hf][:, g % 2, :], Lk, J, start=True, stop=True)
                    last.then_inc(S["sq_psum"], 1)
                    if 1 <= s <= 2 * G:
                        (apply_v if s % 2 else apply_m)(k, (s - 1) // 2)
                    if s == 10:
                        spread_targets(k + 1)
                pe.wait_ge(S["WK_dve"], k * NDVE + NDVE)
                pe.wait_ge(S["B_ready"], k * 3 + 3)
                for g in range(G):
                    for kb in range(KB):
                        last = mm(pw[g // 2][:, g % 2, kb * P:(kb + 1) * P], Bmat[:, g, kb * P:(kb + 1) * P], WK[:, g, 2 * P:3 * P],
                                  start=True, stop=True)
                last.then_inc(S["GT_psum"], 1)
                pe.wait_ge(S["ST_ready"], k + 1)
                for g in range(G):
                    for kb in range(KB):
                        last = mm(misc[:, g * KB + kb:g * KB + kb + 1], STm[:, g, kb * P:(kb + 1) * P], ones[:, 0:1],
                                  start=True, stop=True)
                last.then_inc(S["D_psum"], 1)
            pe.wait_ge(S["D_done"], n)
            pe.wait_ge(S["GT_done"], n + 1)
            for g in range(G):
                apply_v(n, g)
                apply_m(n, g)
            pe.wait_ge(S["M_done"], n * G + (G + 1))
            for a in range(KB):
                for b in range(KB):
                    tr(bank[0][:, b * D + a * P:b * D + (a + 1) * P], Mrot[:, a, b * P:(b + 1) * P], ident[:, :])
            for ib in range(KB):
                for kb in range(KB):
                    mm(bank[1][:, ib * D:(ib + 1) * D], wqT[:, kb, ib * P:(ib + 1) * P], bn[:, kb, :],
                       start=(kb == 0), stop=(kb == KB - 1))
            for kb in range(KB):
                last = mm(bank[2][:, 0:D], bq_c[:, kb:kb + 1].broadcast_to([P, P]), bn[:, kb, :],
                          start=(kb == 0), stop=(kb == KB - 1))
            last.then_inc(S["comb_pe"], 1)
            pe.wait_ge(S["comb_dve"], 4)

            def x2_pe(t, b, rows_=P):
                pe.wait_ge(S["stg_done"], t + 1)
                if not isinstance(t, int) or t > 0:
                    pe.wait_ge(S["x2_done"], t)
                for kb in range(KB):
                    last = mm(bank[0][0:rows_, 0:D], stg[b][:, kb * P:kb * P + rows_], comb[:, kb, :],
                              start=(kb == 0), stop=(kb == KB - 1))
                last.then_inc(S["x2_psum"], 1)

            def router_pe(t, b, rows_=P):
                pe.wait_ge(S["xf_ready"], t + 1)
                for kb in range(KB):
                    last = tr(bank[1][:, kb * P:kb * P + rows_], xf[b][0:rows_, kb * P:(kb + 1) * P], ident[0:rows_, 0:rows_])
                last.then_inc(S["xfT_psum"], 1)
                pe.wait_ge(S["xfT_done"], t + 1)
                for kb in range(KB):
                    last = mm(bank[2][:, 0:NX], xfT[:, kb * P:(kb + 1) * P], wr_s[:, kb, :], start=(kb == 0), stop=(kb == KB - 1))
                last.then_inc(S["lg_psum"], 1)
                pe.wait_ge(S["msk_ready"], t + 1)
                mm(misc[:, 0:NX], trib[:, :], mskb[:, :], start=True, stop=True)
                mm(misc[:, NX:2 * NX], onesb[:, :], mskb[:, :], start=True, stop=True).then_inc(S["rank_psum"], 1)
            x2_pe(0, 0)
            with pe.Fori(0, FULL // 2 - 1) as k:
                for b in range(2):
                    x2_pe(k * 2 + (b + 1), 1 - b)
                    router_pe(k * 2 + b, b)
            x2_pe(FULL - 1, 1)
            router_pe(FULL - 2, 0)
            x2_pe(FULL, 0, TAIL)
            router_pe(FULL - 1, 1)
            router_pe(FULL, 0, TAIL)

            pe.wait_ge(S["tiles_ready"], 1)
            pe.wait_ge(S["w_loaded"], 16 * 2 * NX)

            def turn_x(i, b, k):
                pe.wait_ge(S[f"xm{b}"], k * 16 + 16)
                pe.wait_ge(S["xmT_done"], max(i, 1) if isinstance(i, int) else i)
                for kb in range(KB):
                    last = tr(bank[b][:, kb * P:(kb + 1) * P], xm[b][:, kb * P:(kb + 1) * P], ident[:, :])
                last.then_inc(S["xmT_psum"], 1)

            def first_product(i, b):
                e = pe.value_load(ttab[0:1, 0, bass.ds(i, 1)], min_val=0, max_val=NX - 1)
                pe.wait_ge(S["xmT_done"], i + 2)
                pe.wait_ge(S["hpre_done"], max(i, 1) if isinstance(i, int) else i)
                for kb in range(KB):
                    last = mm(bank[2 + b][:, 0:H], xmT[b][:, kb * P:(kb + 1) * P],
                              w1s[:, bass.ds(e, 1), kb, :].rearrange("p a h -> p (a h)"), start=(kb == 0), stop=(kb == KB - 1))
                last.then_inc(S["h_psum"], 1)

            def second_product(i, b):
                e = pe.value_load(ttab[0:1, 0, bass.ds(i, 1)], min_val=0, max_val=NX - 1)
                pe.wait_ge(S["hact_done"], i + 1)
                for kb in range(H // P):
                    last = tr(bank[4 + b][:, kb * P:(kb + 1) * P], hact[b][:, kb * P:(kb + 1) * P], ident[:, :])
                last.then_inc(S["hT_psum"], 1)
                pe.wait_ge(S["hT_done"], i + 1)
                pe.wait_ge(S["y_done"], i + 1)
                for kb in range(H // P):
                    last = mm(bank[6 + b][:, 0:D], hT[b][:, kb * P:(kb + 1) * P],
                              w2s[:, bass.ds(e, 1), kb, :].rearrange("p a h -> p (a h)"),
                              start=(kb == 0), stop=(kb == H // P - 1))
                last.then_inc(S["y_psum"], 1)
            turn_x(0, 0, 0)
            first_product(0, 0)
            with pe.Fori(0, MT // 2 - 1) as k:
                for b in range(2):
                    turn_x(k * 2 + (b + 1), 1 - b, k + b)
                    first_product(k * 2 + (b + 1), 1 - b)
                    second_product(k * 2 + b, b)
            turn_x(MT - 1, 1, MT // 2 - 1)
            first_product(MT - 1, 1)
            second_product(MT - 2, 0)
            second_product(MT - 1, 1)


_INS = ["x", "src", "dst", "edge_weight", "L0_mix_W_qk", "L0_mix_b_qk", "L0_mix_W_v", "L0_mix_b_v", "L0_mix_gamma",
        "L0_mix_beta", "L0_ffn_gamma", "L0_ffn_beta", "L0_ffn_Wr", "L0_ffn_br", "L0_ffn_W1", "L0_ffn_b1",
        "L0_ffn_W2", "L0_ffn_b2"]


def kernel(**inputs):
    import numpy as _np
    import concourse.bacc as _bacc
    from concourse import mybir as _mybir
    from concourse.bass_utils import run_bass_kernel_spmd as _run

    nc = _bacc.Bacc("TRN2", target_bir_lowering=False, num_devices=1)
    arrays, args = {}, []
    for name in _INS:
        a = _np.ascontiguousarray(inputs[name])
        arrays[f"in_{name}_dram"] = a
        args.append(nc.dram_tensor(f"in_{name}_dram", a.shape, _mybir.dt.from_np(a.dtype), kind="ExternalInput").ap())
    out = nc.dram_tensor("out_0_dram", inputs["x"].shape, _mybir.dt.from_np(_np.dtype("float32")), kind="ExternalOutput")
    gnn_layer(nc, *args, out.ap())
    r = _run(nc, [arrays], core_ids=[0])
    return r.results[0]["out_0_dram"]
```

```python
from contextlib import ExitStack

import concourse.bass as bass
from concourse import mybir

F32 = mybir.dt.float32
BF16 = mybir.dt.bfloat16
I32 = mybir.dt.int32
U32 = mybir.dt.uint32
ALU = mybir.AluOpType
ACT = mybir.ActivationFunctionType
AX_X = mybir.AxisListType.X

P = 128
PI = 3.141592653589793
MAGIC = 12582912.0
TURN_HI = 6.28125
TURN_MID = 0.0019350051879882812
TURN_LO = 2.0 * PI - TURN_HI - TURN_MID


def gnn_layer(nc, x, src, dst, edge_weight, W_qk, b_qk, W_v, b_v, bn_gamma, bn_beta,
              gamma, beta, Wr, br, W1, b1, W2, b2, out):
    N, D = x.shape
    NE = src.shape[0]
    NX, _, H = W1.shape
    KB = D // P
    NT = (N + P - 1) // P
    FULL = N // P
    TAIL = N - FULL * P
    EPS = 1e-5

    EP = 125
    EL = NE // EP
    BL = 200
    NB = NE // BL
    REC = 8
    CAP = P - 1
    G = 4
    NOROW = 512.0
    LEVELS = 7

    GRP = 4 * P
    STRIDE = N + P + 22
    MT = (2 * N + P - 1) // P + NX
    MT += MT % 2
    DM = D + 2
    SPARE = MT - (2 * N) // P
    assert EP * EL == NE and EL % BL == 0 and TAIL and D == 2 * P and H % P == 0

    ctx = ExitStack()
    with ctx:
        def sb(name, shape, dt=F32):
            return ctx.enter_context(nc.sbuf_tensor(name, shape, dt))

        def sem(name):
            return ctx.enter_context(nc.semaphore(name))

        def dram(name, shape, dt=F32):
            return nc.dram_tensor(name, shape, dt).ap()

        incl_d = dram("incl_d", [NB, BL])
        incl_out = incl_d.rearrange("(p c) l -> p (c l)", p=EP)
        ends_d = dram("ends_d", [EP, NB // EP])
        rec_d = dram("rec_d", [NE, REC])
        send_d = dram("send_d", [(NX + 1) * STRIDE, DM])
        back_d = dram("back_d", [2 * N, D])

        R1 = sb("R1", [P, NT * D])
        R2 = sb("R2", [P, KB * NT * P])
        R3 = sb("R3", [P, NX * (KB * H + (H // P) * D)])

        R4 = sb("R4", [P, 8 * D + 2 * KB * GRP + 8 * DM + KB * GRP])

        class Carve:
            def __init__(self, region):
                self.region, self.at = region, 0

            def __call__(self, *shape, dt=F32, parts=P):
                n = 1
                for s in shape:
                    n *= s
                words = n if dt in (F32, I32, U32) else (n + 1) // 2
                v = self.region[0:parts, self.at:self.at + words]
                self.at += words
                assert self.at <= self.region.shape[1]
                if dt != F32:
                    v = v.bitcast(dt)
                if len(shape) == 2:
                    v = v.rearrange("p (a b) -> p a b", a=shape[0])
                if len(shape) == 3:
                    v = v.rearrange("p (a b c) -> p a b c", a=shape[0], b=shape[1])
                return v

        x_all = R1[:, :].rearrange("p (t d) -> p t d", t=NT)
        x2_all = x_all
        xnT = R2[:, :].rearrange("p (k n) -> p k n", k=KB)

        prep = Carve(R3)
        i_f, j_f, g_i, g_j, cnt, incl, theta, turn = [prep(EL, parts=EP) for _ in range(8)]
        i_raw, j_raw = incl.bitcast(I32), cnt.bitcast(I32)
        rec = prep(EL, REC, parts=EP)
        ex = prep(KB, GRP)
        exT = prep(4, D)
        PT = prep(KB, D)
        lam = prep(KB, D)
        stats = prep(NT, 6)
        w1s = R3[:, 0:NX * KB * H].rearrange("p (e k h) -> p e k h", e=NX, k=KB)
        w2s = R3[:, NX * KB * H:].rearrange("p (e k d) -> p e k d", e=NX, k=H // P)

        chunk = Carve(R1)
        ends = chunk(NB)
        junk = chunk(G, NB, dt=BF16)
        rows = chunk(G, BL)
        recs = chunk(G, REC)
        slotmask = chunk(G, P)
        hits = chunk(3 * G, P)
        Lself = chunk(G, P)
        Lnext = chunk(G, P)
        WK = chunk(G, 3 * P)
        Bself = chunk(G, D)
        Bmat = chunk(G, D)
        STm = chunk(G, D)
        GT = chunk(G, KB * P)
        Vs = chunk(D)
        fld = chunk(24, G)
        pos = chunk(3, G)
        cur = chunk(5, G)
        idx = chunk(2, G, dt=U32)
        tb16 = chunk(G, dt=BF16)
        keep = chunk(G, KB)

        soft = Carve(R4)
        xng = [soft(4, D) for _ in range(2)]
        Pacc, wk, wv, wq, wqT, bn = [soft(KB, D) for _ in range(6)]
        bvB = soft(D)
        late = Carve(R4)
        xt = [late(4, D) for _ in range(2)]
        stg = [late(KB, GRP) for _ in range(2)]
        xf = [late(4, DM) for _ in range(2)]
        xfT = late(KB, GRP)
        fin = Carve(R3)
        ya = [fin(4, D) for _ in range(2)]
        yc = [fin(4, D) for _ in range(2)]

        moe = Carve(R2)
        b1B = moe(NX, H)
        b2B = moe(NX, D)
        xm = [moe(DM) for _ in range(2)]
        xmT = [moe(D) for _ in range(2)]
        hpre = [moe(H) for _ in range(2)]
        hact = [moe(H) for _ in range(2)]
        hT = [moe(H) for _ in range(2)]
        yb = [moe(D) for _ in range(2)]
        tacc = moe(3, MT)
        dest_u = moe(MT, dt=U32)

        ident = sb("ident", [P, P])
        identb = sb("identb", [P, P], BF16)
        tri = sb("tri", [P, P])
        trib = sb("trib", [P, P], BF16)
        ones = sb("ones", [P, P])
        onesb = sb("onesb", [P, P], BF16)
        col0 = sb("col0", [P, D])
        col1 = sb("col1", [P, P])
        prow = sb("prow", [P, 1])
        prow1 = sb("prow1", [P, 1])
        minsub = sb("minsub", [P, 1])
        maxsub = sb("maxsub", [P, 1])
        slotnum = sb("slotnum", [P, G])
        Mrot = sb("Mrot", [P, KB, D])
        comb = sb("comb", [P, KB, D])
        small = sb("small", [P, 16])
        bq_c = sb("bq_c", [P, KB])
        bk_c = sb("bk_c", [P, KB])
        bng_c = sb("bng_c", [P, KB])
        bnb_c = sb("bnb_c", [P, KB])
        gamB = sb("gamB", [P, D])
        betB = sb("betB", [P, D])
        wr_s = sb("wr_s", [P, KB, NX])
        brB = sb("brB", [P, NX])
        addrow = sb("addrow", [P, D])
        mv = sb("mv", [P, NT, 2])
        rstd = sb("rstd", [P, NT])
        nmr = sb("nmr", [P, NT])
        run_m = sb("run_m", [P, KB])
        grp_m = sb("grp_m", [P, KB])
        new_m = sb("new_m", [P, KB])
        ebias = sb("ebias", [P, KB])
        dm = sb("dm", [P, KB])
        alpha = sb("alpha", [P, KB])
        alpha2 = sb("alpha2", [P, KB])
        gsum = sb("gsum", [P, KB])
        ssum = sb("ssum", [P, KB])
        rsum = sb("rsum", [P, KB])
        n_groups_i = sb("n_groups_i", [1, 1], I32)
        total = sb("total", [P, 1])
        poff = sb("poff", [P, 1])

        st2 = sb("st2", [P, 4, 6])
        mv2 = sb("mv2", [P, 4, 2])
        dev = sb("dev", [P, 4])
        scl = sb("scl", [P, 4])
        lg = sb("lg", [P, 4, NX])
        top = sb("top", [P, 4, 8])
        topi = sb("topi", [P, 4, 8], U32)
        topf = sb("topf", [P, 4, 8])
        oh = sb("oh", [P, 2 * 4, NX])
        slotf = sb("slotf", [P, 2 * 4])
        sel = sb("sel", [P, 2 * 4, NX])
        mskb = sb("mskb", [P, 5, NX], BF16)
        slot8 = sb("slot8", [P, 4, NX])
        base8 = sb("base8", [P, NX])
        reg8 = sb("reg8", [P, NX])
        slot_now = [sb(f"slot_now{b}", [P, 2 * 4], U32) for b in range(2)]
        tokens = sb("tokens", [P, 4])
        padf = sb("padf", [P, NX])
        padu = sb("padu", [P, NX], U32)
        topd = sb("topd", [P, NT])
        wexp = sb("wexp", [P, NT])
        w_a = sb("w_a", [P, NT])
        w_b = sb("w_b", [P, NT])
        zrow = sb("zrow", [P, DM])
        ntile = sb("ntile", [P, 3, NX])
        tnum = sb("tnum", [P, MT])
        second = sb("second", [P, 2])
        dest_now = [sb(f"dest_now{b}", [P, 1], U32) for b in range(2)]
        ttab = sb("ttab", [1, 2, MT], I32)

        bank = [ctx.enter_context(nc.psum_tensor(f"bank{i}", [P, 512], F32)) for i in range(8)]
        pw = [bank[h][:, :].rearrange("p (c n) -> p c n", c=2) for h in range(2)]
        jb = [bank[2 + h][:, 0:2 * P].rearrange("p (c n) -> p c n", c=2) for h in range(2)]
        TB, apV, apM, misc = bank[4:8]

        S = {}
        for n in ("const consts edges wload prow_ld xld dve act pool pe recs_out ends_in "
                  "xn_ready xT_psum xT_done keys_psum kmax_done ebias_ready alpha_ready exp_done exT_psum exT_done "
                  "mix_psum mix_acc lam_in Lready LT_psum WK_act WK_dve sq_psum J_done V_psum V_done M_psum M_done "
                  "blk_ready rows_in pos_ready recs_in flds_ready TB_psum B_ready J_last GT_psum GT_done ST_ready D_psum D_done "
                  "reserve ngroups comb_pe comb_dve x2_psum stg_done x2_done "
                  "std_need std_done xf_ready xfT_psum xfT_done lg_psum top_ready msk_ready rank_psum rank_read slot_ready "
                  "w_loaded bias_loaded pads zeros_out tiles_ready sc0 sc1 xt0 xt1 xm0 xm1 dest_ready dest_copied "
                  "xmT_psum xmT_done h_psum hpre_done hact_done hT_psum hT_done y_psum y_done ysc0 ysc1 "
                  "back0 back1 out0 out1 sum_a fin_done wexp_need wexp_done x_own r_own t_own tail_own tokens_next second_own "
                  "scan_ok angles_ok xstats_ok pn_ok pT_ok lamstats_ok bn_ok chunk_init_ok dve_settled pool_settled").split():
            S[n] = sem("s_" + n)
        block = ctx.enter_context(nc.Block())

        def chain(eng, s):
            n = [0]

            def link(ins):
                n[0] += 1
                ins.then_inc(s, 1)
                eng.wait_ge(s, n[0])
            link.n = n
            return link

        def at_least(eng, s, v):
            if not isinstance(v, int) or v > 0:
                eng.wait_ge(s, v)

        def settle(eng):
            eng.sem_inc(S["dve_settled"] if eng is nc.vector else S["pool_settled"], 1)

        def bcast_row(ap, n):
            return ap.rearrange("(a n) -> a n", a=1).broadcast_to([P, n])

        NG12 = FULL // 4
        xg_src = x[0:FULL * P, :].rearrange("(t p) d -> p t d", p=P)

        @block.sync
        def _(sp):
            sp.dma_start(i_raw, src.rearrange("(p l) -> p l", p=EP)).then_inc(S["edges"], 16)
            sp.dma_start(j_raw, dst.rearrange("(p l) -> p l", p=EP)).then_inc(S["edges"], 16)
            sp.dma_start(theta, edge_weight.rearrange("(p l) -> p l", p=EP)).then_inc(S["edges"], 16)
            for c in range(0, FULL, 8):
                sp.dma_start(x_all[:, c:c + 8, :], xg_src[:, c:c + 8, :]).then_inc(S["xld"], 16)
            sp.dma_start(x_all[0:TAIL, FULL, :], x[FULL * P:N, :]).then_inc(S["xld"], 16)
            for dstt, s in ((wq, W_qk[0]), (wk, W_qk[1]), (wv, W_v)):
                sp.dma_start(dstt, s.rearrange("(k p) e -> p k e", p=P)).then_inc(S["wload"], 16)
            sp.dma_start(wr_s[:, :, :], Wr.rearrange("(k p) e -> p k e", p=P)).then_inc(S["wload"], 16)
            for dstt, s in ((bq_c, b_qk[0]), (bk_c, b_qk[1]), (bng_c, bn_gamma), (bnb_c, bn_beta)):
                with nc.allow_non_contiguous_dma(reason="one column of a small vector"):
                    sp.dma_start(dstt[:, :], s.rearrange("(k p) -> p k", p=P)).then_inc(S["wload"], 16)
            for dstt, s, n in ((bvB, b_v, D), (gamB, gamma, D), (betB, beta, D), (brB, br, NX)):
                sp.dma_start(dstt[:, :], bcast_row(s, n)).then_inc(S["wload"], 16)
            sp.wait_ge(S["recs_out"], 1)
            sp.dma_start(incl_out, incl[:, :]).then_inc(S["reserve"], 16)
            with nc.allow_non_contiguous_dma(reason="four words per partition"):
                sp.dma_start(ends_d, incl.rearrange("p (c l) -> p c l", l=BL)[:, :, BL - 1]).then_inc(S["reserve"], 16)
            sp.wait_ge(S["recs_out"], 2)
            sp.dma_start(rec_d.rearrange("(p l) r -> p (l r)", p=EP), rec.rearrange("p l r -> p (l r)")).then_inc(S["reserve"], 16)
            sp.wait_ge(S["reserve"], 48)
            sp.wait_ge(S["mix_acc"], NG12 + 1)
            sp.dma_start(ends, ends_d.rearrange("a b -> (a b)").rearrange("(o n) -> o n", o=1).broadcast_to([P, NB])).then_inc(S["ends_in"], 16)
            sp.wait_ge(S["bn_ok"], 1)
            for e in range(NX):
                sp.dma_start(w1s[:, e], W1[e].rearrange("(k p) h -> p k h", p=P)).then_inc(S["w_loaded"], 16)
                sp.dma_start(w2s[:, e], W2[e].rearrange("(k p) d -> p k d", p=P)).then_inc(S["w_loaded"], 16)
            sp.wait_ge(S["consts"], 1)
            for t in range(SPARE):
                r = NX * STRIDE + t * P
                sp.dma_start(send_d[r:r + P, :], zrow[:, :]).then_inc(S["zeros_out"], 16)

            def load_x(q, b):
                sp.dma_start(xt[b], x[bass.ds(q * GRP, GRP), :].rearrange("(t p) d -> p t d", p=P)).then_inc(S[f"xt{b}"], 16)
            for b in range(2):
                load_x(b, b)
            with sp.Fori(1, NG12 // 2) as k:
                for b in range(2):
                    sp.wait_ge(S["x2_done"], k * 2 + (b - 1))
                    load_x(k * 2 + b, b)
            sp.wait_ge(S["x2_done"], NG12 - 1)
            sp.dma_start(xt[0][0:TAIL, 0, :], x[FULL * P:N, :]).then_inc(S["xt0"], 16)

            sp.wait_ge(S["x2_psum"], NG12 + 1)
            sp.dma_start(b1B, b1.rearrange("e h -> (e h)").rearrange("(o n) -> o n", o=1).broadcast_to([P, NX * H]).rearrange("p (e h) -> p e h", e=NX)).then_inc(S["bias_loaded"], 16)
            sp.dma_start(b2B, b2.rearrange("e h -> (e h)").rearrange("(o n) -> o n", o=1).broadcast_to([P, NX * D]).rearrange("p (e h) -> p e h", e=NX)).then_inc(S["bias_loaded"], 16)

            sp.wait_ge(S["tiles_ready"], 1)
            sp.wait_ge(S["sc0"], 16 * (8 * (NG12 // 2) + 2))
            sp.wait_ge(S["sc1"], 16 * 8 * (NG12 // 2))
            sp.wait_ge(S["pads"], 16 * NX)
            sp.wait_ge(S["zeros_out"], 16 * SPARE)

            def load_tile(i, b):
                r = sp.value_load(ttab[0:1, 1, bass.ds(i, 1)], min_val=0, max_val=(NX + 1) * STRIDE - P)
                sp.dma_start(xm[b], send_d[bass.ds(r, P), :]).then_inc(S[f"xm{b}"], 16)
            for b in range(2):
                load_tile(b, b)
            with sp.Fori(1, MT // 2) as k:
                for b in range(2):
                    sp.wait_ge(S["xmT_psum"], k * 2 + (b - 1))
                    sp.wait_ge(S["dest_ready"], k * 2 + (b - 1))
                    load_tile(k * 2 + b, b)

            sp.wait_ge(S["y_psum"], MT)
            sp.wait_ge(S["ysc0"], 16 * (MT // 2))
            sp.wait_ge(S["ysc1"], 16 * (MT // 2))

            def load_back(q, b):
                for c, y in ((0, ya), (1, yc)):
                    sp.dma_start(y[b], back_d[bass.ds(q * GRP + c * N, GRP), :].rearrange("(t p) d -> p t d", p=P))\
                        .then_inc(S[f"back{b}"], 16)
            for b in range(2):
                load_back(b, b)
            with sp.Fori(1, NG12 // 2) as k:
                for b in range(2):
                    sp.wait_ge(S[f"out{b}"], k * 16)
                    load_back(k * 2 + b, b)
            sp.wait_ge(S["out0"], (NG12 // 2) * 16)
            for c, y in ((0, ya), (1, yc)):
                sp.dma_start(y[0][0:TAIL, 0, :], back_d[c * N + FULL * P:c * N + N, :]).then_inc(S["back0"], 16)

        @block.gpsimd
        def _(pool):
            link = chain(pool, S["pool"])
            nc.gpsimd.memset(ones[:, :], 1.0).then_inc(S["const"], 1)
            nc.gpsimd.memset(onesb[:, :], 1.0).then_inc(S["const"], 1)
            nc.gpsimd.memset(zrow[:, 0:D], 0.0).then_inc(S["const"], 1)
            nc.gpsimd.memset(zrow[:, D:DM], 3.0 * N).then_inc(S["const"], 1)
            link(nc.gpsimd.memset(ident[:, :], 0.0))
            link(nc.gpsimd.affine_select(out=ident[:, :], in_=ident[:, :], compare_op=ALU.not_equal, fill=1.0,
                                         base=0, pattern=[[-1, P]], channel_multiplier=1))
            link(nc.gpsimd.tensor_copy(identb[:, :], ident[:, :]))
            link(nc.gpsimd.memset(tri[:, :], 0.0))
            link(nc.gpsimd.affine_select(out=tri[:, :], in_=tri[:, :], compare_op=ALU.is_ge, fill=1.0,
                                         base=0, pattern=[[-1, P]], channel_multiplier=1))
            link(nc.gpsimd.tensor_copy(trib[:, :], tri[:, :]))
            for ap, pat, base, mult in ((col0[:, :], [[1, D]], 0, 0), (col1[:, :], [[1, P]], 1, 0),
                                        (prow[:, :], [[0, 1]], 0, 1), (prow1[:, :], [[0, 1]], 1, 1),
                                        (slotnum[:, :], [[CAP, G]], 0, 1), (reg8[:, :], [[STRIDE, NX]], 0, 0),
                                        (tnum[:, :], [[1, MT]], 0, 0),
                                        (tokens[:, :], [[P, 4]], N, 1)):
                link(nc.gpsimd.iota(ap, pattern=pat, base=base, channel_multiplier=mult,
                                    allow_small_or_imprecise_dtypes=True))
            link(nc.gpsimd.tensor_scalar(minsub[:, :], prow[:, :], float(P - 1), None, ALU.is_ge))
            link(nc.gpsimd.tensor_scalar(maxsub[:, :], prow[:, :], 1.0, None, ALU.is_ge))
            pool.wait_ge(S["const"], 4)
            link(nc.gpsimd.memset(small[:, 0:12], EPS))
            nc.gpsimd.memset(small[:, 12:13], EPS * EPS).then_inc(S["consts"], 1)

            def gather_group(k):
                pool.wait_ge(S["blk_ready"], k + 1)
                settle(pool)
                for g in range(G):
                    nc.gpsimd.indirect_dma_start(
                        out=rows[:, g, :], out_offset=None, in_=incl_d,
                        in_offset=bass.IndirectOffsetOnAxis(ap=idx[:, 0, g:g + 1], axis=0)).then_inc(S["rows_in"], 16)
                pool.wait_ge(S["pos_ready"], k + 1)
                settle(pool)
                for g in range(G):
                    nc.gpsimd.indirect_dma_start(
                        out=recs[:, g, :], out_offset=None, in_=rec_d,
                        in_offset=bass.IndirectOffsetOnAxis(ap=idx[:, 1, g:g + 1], axis=0)).then_inc(S["recs_in"], 16)
            pool.wait_ge(S["ngroups"], 1)
            pool.wait_ge(S["reserve"], 48)
            n = pool.value_load(n_groups_i[0:1, 0:1], min_val=1, max_val=4 * NE)
            gather_group(0)
            with pool.Fori(0, n) as k:
                gather_group(k + 1)

            def scatter(q, b, nt=4, rows_=P):
                pool.wait_ge(S["slot_ready"], q + 1)
                settle(pool)
                for t in range(nt):
                    for c in range(2):
                        nc.gpsimd.indirect_dma_start(
                            out=send_d, out_offset=bass.IndirectOffsetOnAxis(ap=slot_now[b][0:rows_, c * 4 + t:c * 4 + t + 1], axis=0),
                            in_=xf[b][0:rows_, t, :], in_offset=None).then_inc(S[f"sc{b}"], 16)
            with pool.Fori(0, NG12 // 2) as k:
                for b in range(2):
                    scatter(k * 2 + b, b)
            scatter(NG12, 0, 1, TAIL)
            pool.wait_ge(S["tiles_ready"], 1)
            for e in range(NX):
                nc.gpsimd.indirect_dma_start(
                    out=send_d, out_offset=bass.IndirectOffsetOnAxis(ap=padu[:, e:e + 1], axis=0),
                    in_=zrow[:, :], in_offset=None).then_inc(S["pads"], 16)

            def send_back(i, b, k):
                at_least(pool, S[f"ysc{b}"], k * 16)
                pool.wait_ge(S["dest_ready"], i + 1)
                nc.gpsimd.tensor_copy(dest_now[b][:, :], dest_u[:, bass.ds(i, 1)]).then_inc(S["dest_copied"], 1)
                pool.wait_ge(S["dest_copied"], i + 1)
                pool.wait_ge(S["y_done"], i + 2)
                settle(pool)
                nc.gpsimd.indirect_dma_start(
                    out=back_d, out_offset=bass.IndirectOffsetOnAxis(ap=dest_now[b][:, :], axis=0),
                    in_=yb[b], in_offset=None, bounds_check=2 * N - 1, oob_is_err=False).then_inc(S[f"ysc{b}"], 16)
            for b in range(2):
                send_back(b, b, 0)
            with pool.Fori(1, MT // 2) as k:
                for b in range(2):
                    send_back(k * 2 + b, b, k)

        @block.scalar
        def _(act):
            eps, eps_sq = small[:, 0:1], small[:, 12:13]
            act.wait_ge(S["angles_ok"], 1)
            nc.scalar.activation(rec[:, :, 4], theta[:, :], ACT.Sin).then_inc(S["act"], 1)
            nc.scalar.activation(rec[:, :, 3], turn[:, :], ACT.Sin).then_inc(S["act"], 1)
            act.wait_ge(S["xstats_ok"], 1)
            act.wait_ge(S["consts"], 1)
            nc.scalar.activation(rstd[:, :], mv[:, :, 1], ACT.Sqrt, bias=eps).then_inc(S["act"], 1)

            def turned_in(q, W=GRP):
                act.wait_ge(S["xT_psum"], q + 1)
                for kb in range(KB):
                    last = nc.scalar.activation(xnT[:, kb, bass.ds(q * GRP, W)], bank[kb][:, 0:W], ACT.Copy)
                last.then_inc(S["xT_done"], 1)

            def exps(q, W=GRP):
                act.wait_ge(S["ebias_ready"], q + 1)
                at_least(act, S["exT_psum"], q)
                nc.scalar.activation(alpha[:, :], dm[:, :], ACT.Exp).then_inc(S["alpha_ready"], 1)
                for kb in range(KB):
                    last = nc.scalar.activation(ex[:, kb, 0:W], bank[2 + kb][:, 0:W], ACT.Exp,
                                                bias=ebias[:, kb:kb + 1], accum_out=gsum[:, kb:kb + 1])
                last.then_inc(S["exp_done"], 1)
            turned_in(0)
            exps(0)
            with act.Fori(0, NG12 - 1) as q:
                turned_in(q + 1)
                exps(q + 1)
            turned_in(NG12, TAIL)
            exps(NG12, TAIL)
            act.wait_ge(S["lamstats_ok"], 1)
            nc.scalar.activation(small[:, 4:6], small[:, 6:8], ACT.Sqrt, bias=eps).then_inc(S["act"], 1)

            act.wait_ge(S["ngroups"], 1)
            n = act.value_load(n_groups_i[0:1, 0:1], min_val=1, max_val=4 * NE)

            def apply_v(k, g):
                act.wait_ge(S["V_psum"], k * G + (g + 1))
                nc.scalar.activation(Vs[:, :], apV[:, 0:D], ACT.Copy).then_inc(S["V_done"], 1)

            act.sem_inc(S["GT_done"], 1)
            with act.Fori(0, n) as k:
                act.wait_ge(S["LT_psum"], k + 1)
                nc.scalar.activation(WK[:, :, 0:P], Lnext[:, :, :], ACT.Copy)
                for h in range(2):
                    last = nc.scalar.activation(WK[:, 2 * h:2 * h + 2, P:2 * P], pw[h][:, :, P:2 * P], ACT.Copy)
                last.then_inc(S["WK_act"], 1)
                for s in range(2 * LEVELS):
                    lv, hf = s // 2, s % 2
                    if lv < LEVELS - 1:
                        act.wait_ge(S["sq_psum"], k * (2 * LEVELS) + (s + 1))
                        nc.scalar.activation(WK[:, 2 * hf:2 * hf + 2, 0:2 * P], pw[hf], ACT.Copy).then_inc(S["WK_act"], 1)
                    if 1 <= s <= 2 * G and s % 2 == 1:
                        apply_v(k, s // 2)
                act.wait_ge(S["GT_psum"], k + 1)
                for h in range(2):
                    last = nc.scalar.activation(GT[:, 2 * h:2 * h + 2, :], pw[h], ACT.Copy)
                last.then_inc(S["GT_done"], 1)
            for g in range(G):
                apply_v(n, g)

            def stage(q, b, W=GRP):
                at_least(act, S["x2_psum"], q - 1)
                nc.scalar.activation(stg[b][:, :, 0:W], xnT[:, :, bass.ds(q * GRP, W)], ACT.Copy).then_inc(S["stg_done"], 1)

            def norms(q):
                act.wait_ge(S["std_need"], q + 1)
                nc.scalar.activation(dev[:, :], mv2[:, :, 1], ACT.Sqrt, bias=eps_sq, scale=1.0 + EPS).then_inc(S["std_done"], 1)

            def turned_xf(q, W=GRP):
                act.wait_ge(S["xfT_psum"], q + 1)
                for kb in range(KB):
                    last = nc.scalar.activation(xfT[:, kb, 0:W], bank[2 + kb][:, 0:W], ACT.Copy)
                last.then_inc(S["xfT_done"], 1)
            act.wait_ge(S["comb_dve"], 4)
            stage(0, 0)
            stage(1, 1)
            norms(0)
            stage(2, 0)
            with act.Fori(0, NG12 // 2 - 2) as k:
                for b in range(2):
                    turned_xf(k * 2 + b)
                    norms(k * 2 + (b + 1))
                    stage(k * 2 + (b + 3), 1 - b)
            for q in range(NG12 - 4, NG12 + 1):
                turned_xf(q, GRP if q < NG12 else TAIL)
                if q < NG12:
                    norms(q + 1)
                if q + 3 <= NG12:
                    stage(q + 3, (q + 3) % 2, GRP if q + 3 < NG12 else TAIL)
            act.wait_ge(S["wexp_need"], 1)
            nc.scalar.activation(wexp[:, :], topd[:, :], ACT.Exp).then_inc(S["wexp_done"], 1)

            def moe_in(i, b):
                act.wait_ge(S["xmT_psum"], i + 1)
                nc.scalar.activation(xmT[b], bank[b][:, 0:D], ACT.Copy).then_inc(S["xmT_done"], 1)

            def moe_gelu(i, b):
                act.wait_ge(S["hpre_done"], i + 1)
                nc.scalar.activation(hact[b], hpre[b], ACT.Gelu).then_inc(S["hact_done"], 1)

            def moe_step(i, b):
                if not isinstance(i, int) or i + 3 < MT:
                    moe_in(i + 3, 1 - b)
                if not isinstance(i, int) or 0 <= i + 2 < MT:
                    moe_gelu(i + 2, b)
            act.wait_ge(S["tiles_ready"], 1)
            for i in range(-3, 0):
                moe_step(i, i % 2)
            with act.Fori(0, MT // 2 - 2) as k:
                for b in range(2):
                    moe_step(k * 2 + b, b)
            for i in range(MT - 4, MT):
                moe_step(i, i % 2)

            def store_out(q, b):
                act.wait_ge(S["fin_done"], q + 1)
                act.dma_start(out[bass.ds(q * GRP, GRP), :].rearrange("(t p) d -> p t d", p=P), yc[b]).then_inc(S[f"out{b}"], 16)
            with act.Fori(0, NG12 // 2) as k:
                for b in range(2):
                    store_out(k * 2 + b, b)
            act.wait_ge(S["fin_done"], NG12 + 1)
            act.dma_start(out[FULL * P:N, :], yc[0][0:TAIL, 0, :]).then_inc(S["out0"], 16)
            act.wait_ge(S["out0"], 16 * (NG12 // 2 + 1))
            act.wait_ge(S["out1"], 16 * (NG12 // 2))

        @block.vector
        def _(dve):
            link = chain(dve, S["dve"])
            TT, TS, STT = nc.vector.tensor_tensor, nc.vector.tensor_scalar, nc.vector.scalar_tensor_tensor

            dve.wait_ge(S["consts"], 1)
            link(nc.vector.memset(mv[:, :, :], 0.0))
            link(nc.vector.memset(Mrot[:, :, :], 0.0))
            dve.wait_ge(S["edges"], 48)
            link(nc.vector.tensor_copy(i_f, i_raw))
            link(nc.vector.tensor_copy(j_f, j_raw))
            TS(g_i, i_f, float(D), None, ALU.is_ge)
            link(TS(g_j, j_f, float(D), None, ALU.is_ge))
            link(TT(incl, g_i, g_j, ALU.add))
            link(TS(cnt, incl, -1.0, 2.0, ALU.mult, ALU.add))
            TS(rec[:, :, 0], i_f, float(D - 1), None, ALU.min)
            TS(rec[:, :, 2], j_f, float(D - 1), None, ALU.min)
            nc.vector.tensor_copy(rec[:, :, 6], g_i)
            link(nc.vector.tensor_tensor_scan(incl, ones[0:EP, 0:1].broadcast_to([EP, EL]), cnt, 0.0, ALU.mult, ALU.add))
            dve.sem_inc(S["scan_ok"], 1)
            link(TT(rec[:, :, 1], rec[:, :, 2], rec[:, :, 0], ALU.subtract))
            dve.wait_ge(S["pe"], 1)
            nc.vector.tensor_copy(poff[:, :], misc[:, 0:1])
            link(nc.vector.tensor_copy(total[:, :], misc[:, 1:2]))
            link(TS(incl, incl, poff[0:EP, :], None, ALU.add))
            link(TS(small[0:1, 1:2], total[0:1, :], CAP * G - 0.5, 1.0 / (CAP * G), ALU.add, ALU.mult))
            link(TS(small[0:1, 1:2], small[0:1, 1:2], 1.0, None, ALU.max))
            nc.vector.tensor_copy(n_groups_i[:, :], small[0:1, 1:2]).then_inc(S["ngroups"], 1)
            link(TT(rec[:, :, 5], incl, cnt, ALU.subtract))
            nc.vector.memset(rec[:, :, 7], 0.0).then_inc(S["recs_out"], 1)
            link(TS(turn, theta, 1.0 / (2 * PI), MAGIC, ALU.mult, ALU.add))
            link(TS(turn, turn, -MAGIC, None, ALU.add))
            for part in (TURN_HI, TURN_MID, TURN_LO):
                link(STT(theta, turn, -part, theta, ALU.mult, ALU.add))
            link(TS(theta, theta, 3.1415925, -3.1415925, ALU.min, ALU.max))
            link(STT(turn, theta, -1.0, theta, ALU.mult, ALU.max))
            link(TS(turn, turn, -1.0, PI / 2, ALU.mult, ALU.add))
            dve.sem_inc(S["angles_ok"], 1)
            for c in range(0, FULL, 8):
                for t in range(c, c + 8):
                    if t == c:
                        dve.wait_ge(S["xld"], 16 * (NT // 8 + 1))
                    nc.vector.bn_stats(stats[:, t, :], x_all[:, t, :])
            link(nc.vector.bn_stats(stats[0:TAIL, FULL, :], x_all[0:TAIL, FULL, :]))
            for t in range(FULL):
                nc.vector.bn_aggr(mv[:, t, :], stats[:, t, :])
            link(nc.vector.bn_aggr(mv[0:TAIL, FULL, :], stats[0:TAIL, FULL, :]))
            dve.sem_inc(S["xstats_ok"], 1)
            dve.wait_ge(S["act"], 2)
            nc.vector.memset(run_m[:, :], -1e30).then_inc(S["recs_out"], 1)
            nc.vector.memset(ssum[:, :], 0.0)
            link(nc.vector.memset(Pacc, 0.0))
            dve.wait_ge(S["act"], 3)
            link(nc.vector.reciprocal(rstd[:, :], rstd[:, :]))
            link(STT(nmr[:, :], mv[:, :, 0], -1.0, rstd[:, :], ALU.mult, ALU.mult))
            base = link.n[0]
            PERM = 5

            def norm_rows(q, b, W=GRP):
                nt, r = (W + P - 1) // P, W % P or P
                at_least(dve, S["mix_psum"], q - 1)
                for t in range(nt):
                    tt = q * 4 + t
                    last = TS(xng[b][0:r, t, :], x_all[0:r, bass.ds(tt, 1), :].rearrange("p a d -> p (a d)"),
                              rstd[0:r, bass.ds(tt, 1)], nmr[0:r, bass.ds(tt, 1)], ALU.mult, ALU.add)
                last.then_inc(S["xn_ready"], 1)

            def maxima(q, W=GRP):
                n0 = q * PERM + base
                dve.wait_ge(S["keys_psum"], q + 1)
                for kb in range(KB):
                    last = nc.vector.reduce_max(grp_m[:, kb:kb + 1], bank[2 + kb][:, 0:W], AX_X)
                last.then_inc(S["dve"], 1)
                dve.wait_ge(S["dve"], n0 + 1)
                at_least(dve, S["exp_done"], q)
                TT(new_m[:, :], run_m[:, :], grp_m[:, :], ALU.max).then_inc(S["dve"], 1)
                dve.wait_ge(S["dve"], n0 + 2)
                TT(dm[:, :], run_m[:, :], new_m[:, :], ALU.subtract)
                TT(ebias[:, :], bk_c[:, :], new_m[:, :], ALU.subtract).then_inc(S["dve"], 1)
                dve.wait_ge(S["dve"], n0 + 3)
                nc.vector.tensor_copy(run_m[:, :], new_m[:, :])
                TT(ebias[:, :], ebias[:, :], bk_c[:, :], ALU.subtract).then_inc(S["ebias_ready"], 1)

            def turned_exps(q, W=GRP):
                nt, r = (W + P - 1) // P, W % P or P
                dve.wait_ge(S["exT_psum"], q + 1)
                for kb in range(KB):
                    last = nc.vector.tensor_copy(exT[0:r, 0:nt, kb * P:(kb + 1) * P],
                                                 bank[4 + kb][0:r, 0:nt * P].rearrange("p (t d) -> p t d", d=P))
                last.then_inc(S["exT_done"], 1)
                TT(ssum[:, :], ssum[:, :], alpha[:, :], ALU.mult).then_inc(S["dve"], 1)
                dve.wait_ge(S["dve"], q * PERM + (base + 4))
                TT(ssum[:, :], ssum[:, :], gsum[:, :], ALU.add)
                nc.vector.tensor_copy(alpha2[:, :], alpha[:, :]).then_inc(S["dve"], 1)
                dve.wait_ge(S["dve"], q * PERM + (base + 5))

            def weighted_sum(q):
                dve.wait_ge(S["mix_psum"], q + 1)
                for kb in range(KB):
                    last = STT(Pacc[:, kb, :], Pacc[:, kb, :], alpha2[:, kb:kb + 1], bank[6][:, kb * D:(kb + 1) * D],
                               ALU.mult, ALU.add)
                last.then_inc(S["mix_acc"], 1)
            dve.wait_ge(S["wload"], 16 * 12)
            norm_rows(0, 0)
            maxima(0)
            norm_rows(1, 1)
            turned_exps(0)
            maxima(1)
            with dve.Fori(0, NG12 // 2 - 1) as k:
                for b in range(2):
                    q = k * 2 + (b + 1)
                    weighted_sum(q - 1)
                    norm_rows(q + 1, b)
                    turned_exps(q)
                    maxima(q + 1)
            weighted_sum(NG12 - 2)
            norm_rows(NG12, 0, TAIL)
            turned_exps(NG12 - 1)
            maxima(NG12, TAIL)
            weighted_sum(NG12 - 1)
            turned_exps(NG12, TAIL)
            weighted_sum(NG12)
            link.n[0] = base + PERM * (NG12 + 1)
            link(nc.vector.reciprocal(rsum[:, :], ssum[:, :]))
            dve.wait_ge(S["mix_acc"], NG12 + 1)
            for kb in range(KB):
                last = TS(Pacc[:, kb, :], Pacc[:, kb, :], rsum[:, kb:kb + 1], None, ALU.mult)
            link(last)
            dve.sem_inc(S["pn_ok"], 1)
            dve.wait_ge(S["pe"], 2)
            link(nc.vector.tensor_copy(PT, bank[0][:, :].rearrange("p (a b) -> p a b", a=KB)))
            dve.sem_inc(S["pT_ok"], 1)
            link(nc.vector.tensor_copy(wqT, bank[1][:, :].rearrange("p (a b) -> p a b", a=KB)))
            dve.wait_ge(S["pe"], 3)
            for kb in range(KB):
                last = TT(lam[:, kb, :], bank[2][:, kb * D:(kb + 1) * D], bvB[:, :], ALU.add)
            link(last)
            for kb in range(KB):
                last = nc.vector.bn_stats(stats[:, kb, :], lam[:, kb, :])
            link(last)
            for kb in range(KB):
                last = nc.vector.bn_aggr(mv[:, kb, :], stats[:, kb, :])
            link(last)
            link(nc.vector.tensor_copy(small[:, 6:8], mv[:, 0:KB, 1]))
            dve.sem_inc(S["lamstats_ok"], 1)
            dve.wait_ge(S["act"], 4)
            link(nc.vector.reciprocal(small[:, 8:10], small[:, 4:6]))
            link(TT(small[:, 8:10], small[:, 8:10], bng_c[:, :], ALU.mult))
            for kb in range(KB):
                last = TS(lam[:, kb, :], lam[:, kb, :], mv[:, kb, 0:1], small[:, 8 + kb:9 + kb], ALU.subtract, ALU.mult)
            link(last)
            for kb in range(KB):
                last = TS(bn[:, kb, :], lam[:, kb, :], bnb_c[:, kb:kb + 1], None, ALU.add)
            link(last)
            dve.sem_inc(S["bn_ok"], 1)

            for kb in range(KB):
                last = nc.vector.tensor_copy(Mrot[:, kb, kb * P:(kb + 1) * P], ident[:, :])
            nc.vector.memset(GT[:, :, :], 0.0)
            nc.vector.memset(STm[:, :, :], 0.0)
            link(nc.vector.memset(keep[:, :, :], 1.0))
            dve.sem_inc(S["chunk_init_ok"], 1)
            dve.sem_inc(S["M_done"], 1)
            dve.wait_ge(S["ends_in"], 16)
            n = dve.value_load(n_groups_i[0:1, 0:1], min_val=1, max_val=4 * NE)
            base2 = link.n[0]
            sub, v1, v2, valid, isj, dj, tgt, tn, oth, cs, sg, co, lim, csb, cob, lastw = [fld[:, i, :] for i in range(16)]
            f_blk, f_pos, f_edge = [fld[:, i, :] for i in range(16, 19)]
            posA, posB, posL = [pos[:, i, :] for i in range(3)]
            c_t, c_o, c_cs, c_co, c_last = [cur[:, i, :] for i in range(5)]
            count = {}

            def steps(name, per, order=[0]):
                count[name] = order[0]
                order[0] += per
                return order[0]
            steps("search", 2)
            steps("pos", 3)
            steps("fields", 7)
            steps("L", 5)
            PER = steps("swap", 1)

            def after(k, name, i):
                dve.wait_ge(S["dve"], k * PER + (base2 + count[name] + i))

            def sig(ins):
                ins.then_inc(S["dve"], 1)

            def search(k):
                for g in range(G):
                    last = TS(junk[:, g, :], ends, slotnum[:, g:g + 1], 0.0, ALU.is_le, ALU.add, accum_out=f_blk[:, g:g + 1])
                sig(last)
                after(k, "search", 1)
                sig(TS(f_blk, f_blk, float(NB - 1), None, ALU.min))
                after(k, "search", 2)
                nc.vector.tensor_copy(idx[:, 0, :], f_blk).then_inc(S["blk_ready"], 1)

            def search_in(k):
                dve.wait_ge(S["rows_in"], k * (16 * G) + 16 * G)
                for g in range(G):
                    last = TS(junk[:, g, 0:BL], rows[:, g, :], slotnum[:, g:g + 1], 0.0, ALU.is_le, ALU.add,
                              accum_out=f_pos[:, g:g + 1])
                sig(last)
                after(k, "pos", 1)
                sig(STT(f_edge, f_blk, float(BL), f_pos, ALU.mult, ALU.add))
                after(k, "pos", 2)
                sig(TS(f_edge, f_edge, float(NE - 1), None, ALU.min))
                after(k, "pos", 3)
                nc.vector.tensor_copy(idx[:, 1, :], f_edge).then_inc(S["pos_ready"], 1)

            def fields(k):
                dve.wait_ge(S["recs_in"], k * (16 * G) + 16 * G)
                r_i, r_d, r_j, r_c, r_s, r_n, r_g = [recs[:, :, i] for i in range(7)]
                sig(TT(sub, slotnum[:, :], r_n, ALU.subtract))
                after(k, "fields", 1)
                TS(v1, sub, minsub[:, :], None, ALU.is_ge)
                TS(lim, sub, -1.0, prow[:, :], ALU.mult, ALU.add)
                sig(TT(isj, sub, r_g, ALU.add))
                after(k, "fields", 2)
                STT(v2, sub, maxsub[:, :], v1, ALU.is_le, ALU.mult)
                TS(sg, isj, 2.0, -1.0, ALU.mult, ALU.add)
                sig(TT(dj, isj, r_d, ALU.mult))
                after(k, "fields", 3)
                STT(valid, slotnum[:, :], total[:, :], v2, ALU.is_lt, ALU.mult)
                TT(tgt, dj, r_i, ALU.add)
                TT(oth, r_j, dj, ALU.subtract)
                sig(TT(co, r_s, sg, ALU.mult))
                after(k, "fields", 4)
                STT(tn, tgt, NOROW, valid, ALU.subtract, ALU.mult)
                TT(cs, r_c, valid, ALU.mult)
                sig(TT(co, co, valid, ALU.mult))
                after(k, "fields", 5)
                sig(TS(tgt, tn, NOROW, None, ALU.add))
                after(k, "fields", 6)
                sig(TS(slotnum[:, :], slotnum[:, :], float(CAP * G), None, ALU.add))
                after(k, "fields", 7)
                nc.vector.tensor_copy(tb16, tgt).then_inc(S["flds_ready"], 1)

            def build_L(k):
                dve.wait_ge(S["TB_psum"], k + 1)
                for g in range(G):
                    last = STT(slotmask[:, g, :], col0[:, 0:P], lim[:, g:g + 1], col1[:, :], ALU.is_lt, ALU.mult)
                sig(last)
                after(k, "L", 1)
                for g in range(G):
                    tb = TB[:, g * P:(g + 1) * P]
                    STT(hits[:, g, :], tb, tgt[:, g:g + 1], slotmask[:, g, :], ALU.is_equal, ALU.mult)
                    STT(hits[:, G + g, :], tb, oth[:, g:g + 1], slotmask[:, g, :], ALU.is_equal, ALU.mult)
                    last = STT(hits[:, 2 * G + g, :], tb, tgt[:, g:g + 1], col1[:, :], ALU.is_equal, ALU.mult)
                sig(last)
                after(k, "L", 2)
                sig(nc.vector.tensor_reduce(pos[:, :, :].rearrange("p a g -> p (a g)"), hits[:, :, :], AX_X, ALU.max))
                after(k, "L", 3)
                for g in range(G):
                    TS(Lself[:, g, :], col1[:, :], posA[:, g:g + 1], cs[:, g:g + 1], ALU.is_equal, ALU.mult)
                    TS(hits[:, g, :], col1[:, :], posB[:, g:g + 1], co[:, g:g + 1], ALU.is_equal, ALU.mult)
                STT(csb, posA, 0.0, cs, ALU.is_equal, ALU.mult)
                STT(cob, posB, 0.0, co, ALU.is_equal, ALU.mult)
                sig(TS(lastw, posL, prow1[:, :], None, ALU.is_equal))
                after(k, "L", 4)
                sig(TT(Lnext[:, :, :], Lself[:, :, :], hits[:, 0:G, :], ALU.add))
                after(k, "L", 5)

            def swap(k):
                for dst_, s_ in ((c_t, tgt), (c_o, oth), (c_cs, csb), (c_co, cob), (c_last, lastw)):
                    last = nc.vector.tensor_copy(dst_, s_)
                sig(last)
                after(k, "swap", 1)

            def apply_m(k, g):
                dve.wait_ge(S["M_psum"], k * G + (g + 1))
                for kb in range(KB):
                    last = STT(Mrot[:, kb, :], Mrot[:, kb, :], keep[:, g, kb:kb + 1], apM[:, kb * D:(kb + 1) * D],
                               ALU.mult, ALU.add)
                last.then_inc(S["M_done"], 1)

            search(0)
            search_in(0)
            fields(0)
            build_L(0)
            dve.sem_inc(S["Lready"], 1)
            with dve.Fori(0, n) as k:
                k1 = k + 1
                swap(k)
                dve.wait_ge(S["WK_act"], k * (1 + 2 * (LEVELS - 1)) + 1)
                for g in range(G):
                    last = TT(WK[:, g, 2 * P:3 * P], ident[:, :], WK[:, g, P:2 * P], ALU.add)
                last.then_inc(S["WK_dve"], 1)
                for s in range(2 * LEVELS):
                    lv, hf = s // 2, s % 2
                    if lv >= 1:
                        dve.wait_ge(S["sq_psum"], k * (2 * LEVELS) + (s + 1))
                        TT(WK[:, 2 * hf:2 * hf + 2, 2 * P:3 * P], WK[:, 2 * hf:2 * hf + 2, 2 * P:3 * P], jb[hf],
                           ALU.add).then_inc(S["WK_dve"], 1)
                    if s == 0:
                        search(k1)
                    if s in (2, 4, 6, 8):
                        apply_m(k, s // 2 - 1)
                    if s in (1, 3):
                        for g in (s - 1, s):
                            TS(Bself[:, g, :], col0[:, :], c_t[:, g:g + 1], c_cs[:, g:g + 1], ALU.is_equal, ALU.mult)
                            last = TS(Bmat[:, g, :], col0[:, :], c_o[:, g:g + 1], c_co[:, g:g + 1], ALU.is_equal, ALU.mult)
                        last.then_inc(S["B_ready"], 1)
                    if s == 5:
                        dve.wait_ge(S["B_ready"], k * 3 + 2)
                        TT(Bmat[:, :, :], Bmat[:, :, :], Bself[:, :, :], ALU.add).then_inc(S["B_ready"], 1)
                        search_in(k1)
                    if s == 9:
                        for g in range(G):
                            last = TS(STm[:, g, :], col0[:, :], c_t[:, g:g + 1], c_last[:, g:g + 1], ALU.is_equal, ALU.mult)
                        last.then_inc(S["ST_ready"], 1)
                        fields(k1)
                    if s == 11:
                        build_L(k1)
                        dve.sem_inc(S["Lready"], 1)
                dve.wait_ge(S["D_psum"], k + 1)
                TS(keep[:, :, :], misc[:, 0:G * KB].rearrange("p (g k) -> p g k", g=G), -1.0, 1.0, ALU.mult,
                   ALU.add).then_inc(S["D_done"], 1)
                dve.wait_ge(S["D_done"], k + 1)
            for g in range(G):
                apply_m(n, g)
            dve.wait_ge(S["comb_pe"], 1)
            nc.vector.tensor_copy(comb[:, :, :], bank[0][:, :].rearrange("p (a b) -> p a b", a=KB)).then_inc(S["comb_dve"], 1)
            nc.vector.tensor_copy(addrow[:, :], bank[2][:, 0:D]).then_inc(S["comb_dve"], 1)
            dve.wait_ge(S["comb_dve"], 2)
            TT(comb[:, :, :], comb[:, :, :], bank[1][:, :].rearrange("p (a b) -> p a b", a=KB), ALU.add)\
                .then_inc(S["comb_dve"], 1)
            nc.vector.memset(mskb[:, :, :], 0.0)
            nc.vector.memset(topd[:, :], 0.0)
            nc.vector.memset(mv2[:, :, :], 1.0)
            nc.vector.tensor_copy(base8[:, :], reg8[:, :]).then_inc(S["comb_dve"], 1)
            dve.wait_ge(S["comb_dve"], 4)

            def over_tiles(v, nt):
                return v.rearrange("p (a d) -> p a d", a=1).broadcast_to([v.shape[0], nt, v.shape[1]])

            def own(s, q, per, i):
                dve.wait_ge(S[s], q * per + i)
                settle(dve)

            def sum_rows(q, b, uses, nt=4, r=P):
                dve.wait_ge(S["x2_psum"], q + 1)
                for h in range((nt + 1) // 2):
                    m = min(2, nt - 2 * h)
                    last = TT(x2_all[0:r, bass.ds(q * 4 + 2 * h, m), :],
                              bank[h][0:r, 0:m * D].rearrange("p (t d) -> p t d", t=m), over_tiles(addrow[0:r, :], m), ALU.add)
                last.then_inc(S["x_own"], 1)
                own("x_own", q, 5, 1)
                dve.wait_ge(S[f"xt{b}"], uses * 16 + 16)
                x2 = x2_all[0:r, bass.ds(q * 4, nt), :]
                TT(x2, x2, xt[b][0:r, 0:nt, :], ALU.add).then_inc(S["x2_done"], 1)
                dve.wait_ge(S["x2_done"], q + 1)
                settle(dve)
                for t in range(nt):
                    last = nc.vector.bn_stats(st2[0:r, t, :], x2_all[0:r, bass.ds(q * 4 + t, 1), :].rearrange("p a d -> p (a d)"))
                last.then_inc(S["x_own"], 1)
                own("x_own", q, 5, 2)
                for t in range(nt):
                    last = nc.vector.bn_aggr(mv2[0:r, t, :], st2[0:r, t, :])
                last.then_inc(S["std_need"], 1)

            def norm_out(q, b, uses, nt=4, r=P):
                dve.wait_ge(S["std_done"], q + 1)
                nc.vector.reciprocal(scl[:, :], dev[:, :]).then_inc(S["x_own"], 1)
                own("x_own", q, 5, 3)
                at_least(dve, S[f"sc{b}"], uses * (16 * 8))
                y = xf[b][0:r, 0:nt, 0:D]
                for t in range(nt):
                    last = TS(xf[b][0:r, t, 0:D], x2_all[0:r, bass.ds(q * 4 + t, 1), :].rearrange("p a d -> p (a d)"),
                              mv2[0:r, t, 0:1], scl[0:r, t:t + 1], ALU.subtract, ALU.mult)
                last.then_inc(S["x_own"], 1)
                own("x_own", q, 5, 4)
                nc.vector.tensor_copy(xf[b][0:r, 0:nt, D], tokens[0:r, 0:nt])
                TT(y, y, over_tiles(gamB[0:r, :], nt), ALU.mult).then_inc(S["x_own"], 1)
                own("x_own", q, 5, 5)
                TT(y, y, over_tiles(betB[0:r, :], nt), ALU.add).then_inc(S["xf_ready"], 1)
                TS(tokens[:, :], tokens[:, :], float(GRP), None, ALU.add).then_inc(S["tokens_next"], 1)
                dve.wait_ge(S["tokens_next"], q + 1)

            def choose(q, b, nt=4, r=P):
                dve.wait_ge(S["lg_psum"], q + 1)
                TT(lg[0:r, 0:nt, :], bank[4][0:r, 0:nt * NX].rearrange("p (t e) -> p t e", t=nt), over_tiles(brB[0:r, :], nt),
                   ALU.add).then_inc(S["r_own"], 1)
                own("r_own", q, 8, 1)
                for t in range(nt):
                    last = nc.vector.max(top[0:r, t, :], lg[0:r, t, :])
                last.then_inc(S["r_own"], 1)
                own("r_own", q, 8, 2)
                for t in range(nt):
                    last = nc.vector.max_index(topi[0:r, t, :], top[0:r, t, :], lg[0:r, t, :])
                last.then_inc(S["r_own"], 1)
                own("r_own", q, 8, 3)
                TT(topd[0:r, bass.ds(q * 4, nt)], top[0:r, 0:nt, 1], top[0:r, 0:nt, 0], ALU.subtract)
                nc.vector.tensor_copy(topf[0:r, 0:nt, :], topi[0:r, 0:nt, :]).then_inc(S["r_own"], 1)
                own("r_own", q, 8, 4)
                for c in range(2):
                    last = TT(oh[0:r, c * 4:c * 4 + nt, :], over_tiles(col0[0:r, 0:NX], nt),
                              topf[0:r, 0:nt, c:c + 1].broadcast_to([r, nt, NX]), ALU.is_equal)
                last.then_inc(S["r_own"], 1)
                own("r_own", q, 8, 5)
                nc.vector.tensor_copy(xf[b][0:r, 0:nt, D + 1], topf[0:r, 0:nt, 0])
                TT(mskb[0:r, 0:nt, :], oh[0:r, 0:nt, :], oh[0:r, 4:4 + nt, :], ALU.add).then_inc(S["msk_ready"], 1)

            def place_rows(q, b, nt=4, r=P):
                dve.wait_ge(S["rank_psum"], q + 1)
                TT(slot8[0:r, 0:nt, :], bank[5][0:r, 0:nt * NX].rearrange("p (t e) -> p t e", t=nt),
                   over_tiles(base8[0:r, :], nt), ALU.add).then_inc(S["r_own"], 1)
                own("r_own", q, 8, 6)
                TT(base8[:, :], bank[5][:, 4 * NX:5 * NX], base8[:, :], ALU.add)
                for c in range(2):
                    last = TT(sel[0:r, c * 4:c * 4 + nt, :], oh[0:r, c * 4:c * 4 + nt, :], slot8[0:r, 0:nt, :], ALU.mult)
                last.then_inc(S["r_own"], 1)
                own("r_own", q, 8, 7)
                for c in range(2):
                    last = nc.vector.tensor_reduce(slotf[0:r, c * 4:c * 4 + nt], sel[0:r, c * 4:c * 4 + nt, :], AX_X, ALU.add)
                last.then_inc(S["r_own"], 1)
                own("r_own", q, 8, 8)
                for c in range(2):
                    last = nc.vector.tensor_copy(slot_now[b][0:r, c * 4:c * 4 + nt], slotf[0:r, c * 4:c * 4 + nt])
                last.then_inc(S["slot_ready"], 1)

            def group_step(q, b, uses):
                n_ = (1, TAIL) if isinstance(q, int) and q + 1 == NG12 else (4, P)
                m_ = (1, TAIL) if isinstance(q, int) and q == NG12 else (4, P)
                more = not isinstance(q, int) or q < NG12
                if more:
                    sum_rows(q + 1, 1 - b, uses, *n_)
                if m_[0] < 4:
                    nc.vector.memset(mskb[:, :, :], 0.0).then_inc(S["tail_own"], 1)
                    dve.wait_ge(S["tail_own"], 1)
                choose(q, b, *m_)
                if more:
                    norm_out(q + 1, 1 - b, uses, *n_)
                place_rows(q, b, *m_)
            sum_rows(0, 0, 0)
            norm_out(0, 0, 0)
            for q in range(2):
                group_step(q, q % 2, (q + 1) // 2)
            with dve.Fori(1, NG12 // 2 - 1) as k:
                for b in range(2):
                    group_step(k * 2 + b, b, k + b)
            for q in range(NG12 - 2, NG12 + 1):
                group_step(q, q % 2, (q + 1) // 2)
            dve.sem_inc(S["wexp_need"], 1)
            tl = chain(dve, S["t_own"])
            tl(TS(padf[:, :], base8[:, :], prow[:, :], None, ALU.add))
            nc.vector.tensor_copy(padu[:, :], padf[:, :])
            tl(TT(ntile[:, 0, :], base8[:, :], reg8[:, :], ALU.subtract))
            tl(TS(ntile[:, 0, :], ntile[:, 0, :], 1.0 / P, 0.5 - 1.0 / (2 * P), ALU.mult, ALU.add))
            tl(TS(ntile[:, 0, :], ntile[:, 0, :], MAGIC, None, ALU.add))
            tl(TS(ntile[:, 0, :], ntile[:, 0, :], -MAGIC, None, ALU.add))
            tl(nc.vector.tensor_tensor_scan(ntile[:, 1, :], ones[:, 0:NX], ntile[:, 0, :], 0.0, ALU.mult, ALU.add))
            tl(TS(ntile[:, 2, :], ntile[:, 0, :], -float(P), float(STRIDE), ALU.mult, ALU.add))
            nc.vector.memset(tacc[:, 0, :], 0.0)
            tl(TS(tacc[:, 1, :], tnum[:, :], float(P), None, ALU.mult))
            for e in range(NX):
                tl(TS(tacc[:, 2, :], tnum[:, :], ntile[:, 1, e:e + 1], None, ALU.is_ge))
                tl(TT(tacc[:, 0, :], tacc[:, 0, :], tacc[:, 2, :], ALU.add))
                tl(STT(tacc[:, 1, :], tacc[:, 2, :], ntile[:, 2, e:e + 1], tacc[:, 1, :], ALU.mult, ALU.add))
            tl(TS(tacc[:, 0, :], tacc[:, 0, :], float(NX - 1), None, ALU.min))
            tl(nc.vector.tensor_copy(ttab[:, :, :], tacc[0:1, 0:2, :]))
            dve.sem_inc(S["tiles_ready"], 1)
            dve.wait_ge(S["wexp_done"], 1)
            tl(TS(w_a[:, :], wexp[:, :], 1.0, None, ALU.add))
            tl(nc.vector.reciprocal(w_a[:, :], w_a[:, :]))
            tl(TT(w_b[:, :], w_a[:, :], wexp[:, :], ALU.mult))

            dve.wait_ge(S["bias_loaded"], 32)

            def expert_of(i):
                return dve.value_load(ttab[0:1, 0, bass.ds(i, 1)], min_val=0, max_val=NX - 1)

            def destinations(i, b, uses):
                dve.wait_ge(S[f"xm{b}"], uses * 16 + 16)
                TS(second[:, b:b + 1], xm[b][:, D + 1:D + 2], tacc[:, 0, bass.ds(i, 1)], -float(N), ALU.is_equal,
                   ALU.mult).then_inc(S["second_own"], 1)
                dve.wait_ge(S["second_own"], i + 1)
                TT(dest_u[:, bass.ds(i, 1)], second[:, b:b + 1], xm[b][:, D:D + 1], ALU.add).then_inc(S["dest_ready"], 1)

            def hidden(i, b):
                e = expert_of(i)
                dve.wait_ge(S["h_psum"], i + 1)
                at_least(dve, S["hact_done"], i - 1)
                TT(hpre[b], bank[2 + b][:, 0:H], b1B[:, bass.ds(e, 1), :].rearrange("p a h -> p (a h)"),
                   ALU.add).then_inc(S["hpre_done"], 1)

            def turned_hidden(i, b):
                dve.wait_ge(S["hT_psum"], i + 1)
                nc.vector.tensor_copy(hT[b], bank[4 + b][:, 0:H]).then_inc(S["hT_done"], 1)

            def results(i, b, uses):
                e = expert_of(i)
                dve.wait_ge(S["y_psum"], i + 1)
                at_least(dve, S[f"ysc{b}"], uses * 16)
                TT(yb[b], bank[6 + b][:, 0:D], b2B[:, bass.ds(e, 1), :].rearrange("p a h -> p (a h)"),
                   ALU.add).then_inc(S["y_done"], 1)

            def moe_step(i, b, k):
                const = isinstance(i, int)
                if not const or i + 3 < MT:
                    destinations(i + 3, 1 - b, (i + 3) // 2 if const else k + (1 + b))
                if not const or 0 <= i + 2 < MT:
                    hidden(i + 2, b)
                if not const or 0 <= i + 1 < MT:
                    turned_hidden(i + 1, 1 - b)
                if not const or i >= 0:
                    results(i, b, k)
            dve.sem_inc(S["y_done"], 1)
            for i in range(-3, 2):
                moe_step(i, i % 2, 0)
            with dve.Fori(1, MT // 2 - 2) as k:
                for b in range(2):
                    moe_step(k * 2 + b, b, k)
            for i in range(MT - 4, MT):
                moe_step(i, i % 2, i // 2)

            def final(q, b, uses, nt=4, r=P):
                dve.wait_ge(S[f"back{b}"], uses * 32 + 32)
                for t in range(nt):
                    last = STT(ya[b][0:r, t, :], ya[b][0:r, t, :], w_a[0:r, bass.ds(q * 4 + t, 1)],
                               x2_all[0:r, bass.ds(q * 4 + t, 1), :].rearrange("p a d -> p (a d)"), ALU.mult, ALU.add)
                last.then_inc(S["sum_a"], 1)
                dve.wait_ge(S["sum_a"], q + 1)
                for t in range(nt):
                    last = STT(yc[b][0:r, t, :], yc[b][0:r, t, :], w_b[0:r, bass.ds(q * 4 + t, 1)], ya[b][0:r, t, :],
                               ALU.mult, ALU.add)
                last.then_inc(S["fin_done"], 1)
            with dve.Fori(0, NG12 // 2) as k:
                for b in range(2):
                    final(k * 2 + b, b, k)
            final(NG12, 0, NG12 // 2, 1, TAIL)

        @block.tensor
        def _(pe):
            link = chain(pe, S["pe"])
            mm, tr = nc.tensor.matmul, nc.tensor.transpose
            pe.wait_ge(S["consts"], 1)
            pe.wait_ge(S["scan_ok"], 1)
            mm(misc[:, 0:1], tri[0:EP, :], incl[:, EL - 1:EL], start=True, stop=True)
            mm(misc[:, 1:2], ones[0:EP, :], incl[:, EL - 1:EL], start=True, stop=True).then_inc(S["pe"], 1)

            pe.wait_ge(S["wload"], 16 * 12)

            def turn_in(q, b, W=GRP):
                nt, r = (W + P - 1) // P, W % P or P
                pe.wait_ge(S["xn_ready"], q + 1)
                for kb in range(KB):
                    for t in range(nt):
                        last = tr(bank[kb][:, t * P:t * P + r], xng[b][0:r, t, kb * P:(kb + 1) * P], ident[0:r, 0:r])
                last.then_inc(S["xT_psum"], 1)

            def keys(q, W=GRP):
                pe.wait_ge(S["xT_done"], q + 1)
                at_least(pe, S["exp_done"], q)
                for db in range(KB):
                    for kb in range(KB):
                        last = mm(bank[2 + db][:, 0:W], wk[:, kb, db * P:(db + 1) * P],
                                  xnT[:, kb, bass.ds(q * GRP, W)], start=(kb == 0), stop=(kb == KB - 1))
                last.then_inc(S["keys_psum"], 1)

            def turn_exps(q, W=GRP):
                nt, r = (W + P - 1) // P, W % P or P
                pe.wait_ge(S["exp_done"], q + 1)
                for kb in range(KB):
                    for t in range(nt):
                        last = tr(bank[4 + kb][0:r, t * P:(t + 1) * P], ex[:, kb, t * P:t * P + r], ident[:, :])
                last.then_inc(S["exT_psum"], 1)

            def weigh(q, b, W=GRP):
                nt, r = (W + P - 1) // P, W % P or P
                pe.wait_ge(S["exT_done"], q + 1)
                at_least(pe, S["mix_acc"], q)
                for kb in range(KB):
                    for t in range(nt):
                        last = mm(bank[6][:, kb * D:(kb + 1) * D], exT[0:r, t, kb * P:(kb + 1) * P], xng[b][0:r, t, :],
                                  start=(t == 0), stop=(t == nt - 1))
                last.then_inc(S["mix_psum"], 1)

            def mix_step(q, b, W=GRP, Wn=GRP):
                turn_exps(q, W)
                if Wn:
                    turn_in(q + 1, 1 - b, Wn)
                    keys(q + 1, Wn)
                weigh(q, b, W)
            turn_in(0, 0)
            keys(0)
            mix_step(0, 0)
            with pe.Fori(0, NG12 // 2 - 1) as k:
                for b in range(2):
                    mix_step(k * 2 + (b + 1), 1 - b)
            mix_step(NG12 - 1, 1, Wn=TAIL)
            mix_step(NG12, 0, W=TAIL, Wn=0)

            pe.wait_ge(S["pn_ok"], 1)
            for src_, bk in ((Pacc, 0), (wq, 1)):
                for a in range(KB):
                    for b in range(KB):
                        last = tr(bank[bk][:, b * D + a * P:b * D + (a + 1) * P], src_[:, a, b * P:(b + 1) * P], ident[:, :])
            last.then_inc(S["pe"], 1)
            pe.wait_ge(S["pT_ok"], 1)
            for db in range(KB):
                for kb in range(KB):
                    last = mm(bank[2][:, db * D:(db + 1) * D], PT[:, kb, db * P:(db + 1) * P], wv[:, kb, :],
                              start=(kb == 0), stop=(kb == KB - 1))
            last.then_inc(S["pe"], 1)
            pe.wait_ge(S["chunk_init_ok"], 1)

            n = pe.value_load(n_groups_i[0:1, 0:1], min_val=1, max_val=4 * NE)

            def spread_targets(k):
                pe.wait_ge(S["flds_ready"], k + 1)
                for g in range(G):
                    last = mm(TB[:, g * P:(g + 1) * P], tb16[:, g:g + 1].broadcast_to([P, P]), identb[:, :],
                              start=True, stop=True)
                last.then_inc(S["TB_psum"], 1)

            def apply_v(k, g):
                pe.wait_ge(S["M_done"], k * G + (g + 1))
                for kb in range(KB):
                    last = mm(apV[:, 0:D], GT[:, g, kb * P:(kb + 1) * P], Mrot[:, kb, :], start=(kb == 0), stop=(kb == KB - 1))
                last.then_inc(S["V_psum"], 1)

            def apply_m(k, g):
                pe.wait_ge(S["V_done"], k * G + (g + 1))
                for rb in range(KB):
                    last = mm(apM[:, rb * D:(rb + 1) * D], STm[:, g, rb * P:(rb + 1) * P], Vs[:, :], start=True, stop=True)
                last.then_inc(S["M_psum"], 1)

            spread_targets(0)
            with pe.Fori(0, n) as k:
                pe.wait_ge(S["Lready"], k + 1)
                pe.wait_ge(S["GT_done"], k + 1)
                for g in range(G):
                    last = tr(pw[g // 2][:, g % 2, P:2 * P], Lnext[:, g, :], ident[:, :])
                last.then_inc(S["LT_psum"], 1)
                NACT = 1 + 2 * (LEVELS - 1)
                NDVE = 1 + 2 * (LEVELS - 1)
                for s in range(2 * LEVELS):
                    lv, hf = s // 2, s % 2
                    pe.wait_ge(S["WK_act"], k * NACT + (1 if lv == 0 else 2 * lv + hf))
                    pe.wait_ge(S["WK_dve"], k * NDVE + (1 if lv <= 1 else 2 * (lv - 1) + hf))
                    for g in (2 * hf, 2 * hf + 1):
                        Lk, LkT, J = WK[:, g, 0:P], WK[:, g, P:2 * P], WK[:, g, 2 * P:3 * P]
                        if lv < LEVELS - 1:
                            mm(pw[hf][:, g % 2, 0:P], LkT, Lk, start=True, stop=True)
                            last = mm(pw[hf][:, g % 2, P:2 * P], Lk, LkT, start=True, stop=True)
                        if lv >= 1:
                            last = mm(jb[hf][:, g % 2, :], Lk, J, start=True, stop=True)
                    last.then_inc(S["sq_psum"], 1)
                    if 1 <= s <= 2 * G:
                        (apply_v if s % 2 else apply_m)(k, (s - 1) // 2)
                    if s == 10:
                        spread_targets(k + 1)
                pe.wait_ge(S["WK_dve"], k * NDVE + NDVE)
                pe.wait_ge(S["B_ready"], k * 3 + 3)
                for g in range(G):
                    for kb in range(KB):
                        last = mm(pw[g // 2][:, g % 2, kb * P:(kb + 1) * P], Bmat[:, g, kb * P:(kb + 1) * P], WK[:, g, 2 * P:3 * P],
                                  start=True, stop=True)
                last.then_inc(S["GT_psum"], 1)
                pe.wait_ge(S["ST_ready"], k + 1)
                for g in range(G):
                    for kb in range(KB):
                        last = mm(misc[:, g * KB + kb:g * KB + kb + 1], STm[:, g, kb * P:(kb + 1) * P], ones[:, 0:1],
                                  start=True, stop=True)
                last.then_inc(S["D_psum"], 1)
            pe.wait_ge(S["D_done"], n)
            pe.wait_ge(S["GT_done"], n + 1)
            for g in range(G):
                apply_v(n, g)
                apply_m(n, g)
            pe.wait_ge(S["M_done"], n * G + (G + 1))
            for a in range(KB):
                for b in range(KB):
                    tr(bank[0][:, b * D + a * P:b * D + (a + 1) * P], Mrot[:, a, b * P:(b + 1) * P], ident[:, :])
            for ib in range(KB):
                for kb in range(KB):
                    mm(bank[1][:, ib * D:(ib + 1) * D], wqT[:, kb, ib * P:(ib + 1) * P], bn[:, kb, :],
                       start=(kb == 0), stop=(kb == KB - 1))
            for kb in range(KB):
                last = mm(bank[2][:, 0:D], bq_c[:, kb:kb + 1].broadcast_to([P, P]), bn[:, kb, :],
                          start=(kb == 0), stop=(kb == KB - 1))
            last.then_inc(S["comb_pe"], 1)
            pe.wait_ge(S["comb_dve"], 4)

            def sum_pe(q, b, nt=4, r=P):
                pe.wait_ge(S["stg_done"], q + 1)
                at_least(pe, S["x2_done"], q)
                for t in range(nt):
                    for kb in range(KB):
                        last = mm(bank[t // 2][0:r, (t % 2) * D:(t % 2 + 1) * D], stg[b][:, kb, t * P:t * P + r], comb[:, kb, :],
                                  start=(kb == 0), stop=(kb == KB - 1))
                last.then_inc(S["x2_psum"], 1)

            def router_pe(q, b, nt=4, r=P):
                pe.wait_ge(S["xf_ready"], q + 1)
                for kb in range(KB):
                    for t in range(nt):
                        last = tr(bank[2 + kb][:, t * P:t * P + r], xf[b][0:r, t, kb * P:(kb + 1) * P], ident[0:r, 0:r])
                last.then_inc(S["xfT_psum"], 1)
                pe.wait_ge(S["xfT_done"], q + 1)
                for t in range(nt):
                    for kb in range(KB):
                        last = mm(bank[4][0:r, t * NX:(t + 1) * NX], xfT[:, kb, t * P:t * P + r], wr_s[:, kb, :],
                                  start=(kb == 0), stop=(kb == KB - 1))
                last.then_inc(S["lg_psum"], 1)
                pe.wait_ge(S["msk_ready"], q + 1)
                mm(bank[5][:, 0:5 * NX], trib[:, :], mskb[:, :, :].rearrange("p t e -> p (t e)"), start=True, stop=False)
                for t in range(4):
                    last = mm(bank[5][:, (t + 1) * NX:5 * NX].rearrange("p (t e) -> p t e", e=NX), onesb[:, :],
                              mskb[:, t:t + 1, :].broadcast_to([P, 4 - t, NX]), start=False, stop=(t == 3))
                last.then_inc(S["rank_psum"], 1)
            sum_pe(0, 0)
            with pe.Fori(0, NG12 // 2 - 1) as k:
                for b in range(2):
                    sum_pe(k * 2 + (b + 1), 1 - b)
                    router_pe(k * 2 + b, b)
            sum_pe(NG12 - 1, 1)
            router_pe(NG12 - 2, 0)
            sum_pe(NG12, 0, 1, TAIL)
            router_pe(NG12 - 1, 1)
            router_pe(NG12, 0, 1, TAIL)

            pe.wait_ge(S["tiles_ready"], 1)
            pe.wait_ge(S["w_loaded"], 16 * 2 * NX)

            def expert_of(i):
                return pe.value_load(ttab[0:1, 0, bass.ds(i, 1)], min_val=0, max_val=NX - 1)

            def turn_x(i, b, uses):
                pe.wait_ge(S[f"xm{b}"], uses * 16 + 16)
                at_least(pe, S["xmT_done"], i - 1)
                for kb in range(KB):
                    last = tr(bank[b][:, kb * P:(kb + 1) * P], xm[b][:, kb * P:(kb + 1) * P], ident[:, :])
                last.then_inc(S["xmT_psum"], 1)

            def first_product(i, b):
                e = expert_of(i)
                pe.wait_ge(S["xmT_done"], i + 1)
                at_least(pe, S["hpre_done"], i - 1)
                for kb in range(KB):
                    last = mm(bank[2 + b][:, 0:H], xmT[b][:, kb * P:(kb + 1) * P],
                              w1s[:, bass.ds(e, 1), kb, :].rearrange("p a h -> p (a h)"), start=(kb == 0), stop=(kb == KB - 1))
                last.then_inc(S["h_psum"], 1)

            def turn_hidden(i, b):
                pe.wait_ge(S["hact_done"], i + 1)
                for kb in range(H // P):
                    last = tr(bank[4 + b][:, kb * P:(kb + 1) * P], hact[b][:, kb * P:(kb + 1) * P], ident[:, :])
                last.then_inc(S["hT_psum"], 1)

            def second_product(i, b):
                e = expert_of(i)
                pe.wait_ge(S["hT_done"], i + 1)
                pe.wait_ge(S["y_done"], i + 1)
                for kb in range(H // P):
                    last = mm(bank[6 + b][:, 0:D], hT[b][:, kb * P:(kb + 1) * P],
                              w2s[:, bass.ds(e, 1), kb, :].rearrange("p a h -> p (a h)"),
                              start=(kb == 0), stop=(kb == H // P - 1))
                last.then_inc(S["y_psum"], 1)

            def moe_step(i, b, k):
                const = isinstance(i, int)
                if not const or i + 3 < MT:
                    turn_x(i + 3, 1 - b, (i + 3) // 2 if const else k + (1 + b))
                if not const or 0 <= i + 2 < MT:
                    first_product(i + 2, b)
                if not const or 0 <= i + 1 < MT:
                    turn_hidden(i + 1, 1 - b)
                if not const or i >= 0:
                    second_product(i, b)
            for i in range(-3, 0):
                moe_step(i, i % 2, 0)
            with pe.Fori(0, MT // 2 - 2) as k:
                for b in range(2):
                    moe_step(k * 2 + b, b, k)
            for i in range(MT - 4, MT):
                moe_step(i, i % 2, i // 2)


_INS = ["x", "src", "dst", "edge_weight", "L0_mix_W_qk", "L0_mix_b_qk", "L0_mix_W_v", "L0_mix_b_v", "L0_mix_gamma",
        "L0_mix_beta", "L0_ffn_gamma", "L0_ffn_beta", "L0_ffn_Wr", "L0_ffn_br", "L0_ffn_W1", "L0_ffn_b1",
        "L0_ffn_W2", "L0_ffn_b2"]


def kernel(**inputs):
    import numpy as _np
    import concourse.bacc as _bacc
    from concourse import mybir as _mybir
    from concourse.bass_utils import run_bass_kernel_spmd as _run

    nc = _bacc.Bacc("TRN2", target_bir_lowering=False, num_devices=1)
    arrays, args = {}, []
    for name in _INS:
        a = _np.ascontiguousarray(inputs[name])
        arrays[f"in_{name}_dram"] = a
        args.append(nc.dram_tensor(f"in_{name}_dram", a.shape, _mybir.dt.from_np(a.dtype), kind="ExternalInput").ap())
    out = nc.dram_tensor("out_0_dram", inputs["x"].shape, _mybir.dt.from_np(_np.dtype("float32")), kind="ExternalOutput")
    gnn_layer(nc, *args, out.ap())
    r = _run(nc, [arrays], core_ids=[0])
    return r.results[0]["out_0_dram"]
```

```python
from contextlib import ExitStack

import concourse.bass as bass
from concourse import mybir

F32 = mybir.dt.float32
BF16 = mybir.dt.bfloat16
I32 = mybir.dt.int32
U32 = mybir.dt.uint32
ALU = mybir.AluOpType
ACT = mybir.ActivationFunctionType
AX_X = mybir.AxisListType.X

P = 128
PI = 3.141592653589793
MAGIC = 12582912.0
TURN_HI = 6.28125
TURN_MID = 0.0019350051879882812
TURN_LO = 2.0 * PI - TURN_HI - TURN_MID


def gnn_layer(nc, x, src, dst, edge_weight, W_qk, b_qk, W_v, b_v, bn_gamma, bn_beta,
              gamma, beta, Wr, br, W1, b1, W2, b2, out):
    N, D = x.shape
    NE = src.shape[0]
    NX, _, H = W1.shape
    KB = D // P
    NT = (N + P - 1) // P
    FULL = N // P
    TAIL = N - FULL * P
    EPS = 1e-5

    EP = 125
    EL = NE // EP
    BL = 200
    NB = NE // BL
    REC = 8
    CAP = P - 1
    G = 4
    NOROW = 512.0
    V_AT = 6
    LEVELS = 7

    FB = 4
    GRP = 4 * P
    STRIDE = N + P + 22
    MT = (2 * N + P - 1) // P + NX
    MT += MT % 2
    DM = D + 2
    LEAST = ((2 * N + P - 1) // P + 1) // 2
    SPARE = 1
    assert EP * EL == NE and EL % BL == 0 and TAIL and D == 2 * P and H % P == 0

    ctx = ExitStack()
    with ctx:
        def sb(name, shape, dt=F32):
            return ctx.enter_context(nc.sbuf_tensor(name, shape, dt))

        def sem(name):
            return ctx.enter_context(nc.semaphore(name))

        def dram(name, shape, dt=F32):
            return nc.dram_tensor(name, shape, dt).ap()

        incl_d = dram("incl_d", [NB, BL])
        incl_out = incl_d.rearrange("(p c) l -> p (c l)", p=EP)
        ends_d = dram("ends_d", [EP, NB // EP])
        rec_d = dram("rec_d", [NE, REC])
        send_d = dram("send_d", [(NX + 1) * STRIDE, DM])
        back_d = dram("back_d", [2 * N, D])

        R1 = sb("R1", [P, NT * D])
        R2 = sb("R2", [P, KB * NT * P])
        R3 = sb("R3", [P, NX * (KB * H + (H // P) * D)])

        R4 = sb("R4", [P, 8 * D + 2 * KB * GRP + 8 * DM + KB * GRP])

        class Carve:
            def __init__(self, region):
                self.region, self.at = region, 0

            def __call__(self, *shape, dt=F32, parts=P):
                n = 1
                for s in shape:
                    n *= s
                words = n if dt in (F32, I32, U32) else (n + 1) // 2
                v = self.region[0:parts, self.at:self.at + words]
                self.at += words
                assert self.at <= self.region.shape[1]
                if dt != F32:
                    v = v.bitcast(dt)
                if len(shape) == 2:
                    v = v.rearrange("p (a b) -> p a b", a=shape[0])
                if len(shape) == 3:
                    v = v.rearrange("p (a b c) -> p a b c", a=shape[0], b=shape[1])
                return v

        x_all = R1[:, :].rearrange("p (t d) -> p t d", t=NT)
        x2_all = x_all
        xnT = R2[:, :].rearrange("p (k n) -> p k n", k=KB)

        prep = Carve(R3)
        i_f, j_f, g_i, g_j, cnt, incl, theta, turn = [prep(EL, parts=EP) for _ in range(8)]
        i_raw, j_raw = incl.bitcast(I32), cnt.bitcast(I32)
        rec = prep(EL, REC, parts=EP)
        ex = prep(KB, GRP)
        exT = prep(4, D)
        PT = prep(KB, D)
        lam = prep(KB, D)
        stats = prep(NT, 6)
        w1s = R3[:, 0:NX * KB * H].rearrange("p (e k h) -> p e k h", e=NX, k=KB)
        w2s = R3[:, NX * KB * H:].rearrange("p (e k d) -> p e k d", e=NX, k=H // P)

        chunk = Carve(R1)
        ends = chunk(NB)
        junk = chunk(G, NB, dt=BF16)
        rows = chunk(G, BL)
        recs = chunk(G, REC)
        slotmask = chunk(G, P)
        hits = chunk(3 * G, P)
        Lself = chunk(G, P)
        Lnext = chunk(G, P)
        LTnext = chunk(G, P)
        WK = chunk(G, 3 * P)
        Bself = chunk(G, D)
        Bmat = chunk(G, D)
        STm = chunk(G, D)
        STb = chunk(G, D, dt=BF16)
        GT = chunk(G, KB * P)
        Vs = chunk(D)
        fld = chunk(24, G)
        pos = chunk(3, G)
        cur = chunk(5, G)
        idx = chunk(2, G, dt=U32)
        tb16 = chunk(G, dt=BF16)
        keep = chunk(G, KB)

        soft = Carve(R4)
        xng = [soft(4, D) for _ in range(3)]
        wk, wv, Pacc, wq, wqT, bn = [soft(KB, D) for _ in range(6)]
        bvB = soft(D)
        Jnext = Pacc.rearrange("p k d -> p (k d)").rearrange("p (g n) -> p g n", g=G)
        addrow = Pacc[:, 0, :]
        addhi = Pacc[:, 1, 0:P].bitcast(BF16)
        late = Carve(R4)
        xt = [late(4, D) for _ in range(2)]
        stg = [late(KB, GRP) for _ in range(2)]
        xf = [late(4, DM) for _ in range(2)]
        xfT = late(KB, GRP)
        fin = Carve(R3)
        ya = [fin(4, D) for _ in range(FB)]
        yc = [fin(4, D) for _ in range(FB)]

        moe = Carve(R2)
        b1B = moe(NX, H)
        b2B = moe(NX, D)
        xm = [moe(DM) for _ in range(2)]
        xmT = [moe(D) for _ in range(2)]
        hpre = [moe(H) for _ in range(2)]
        hact = [moe(H) for _ in range(2)]
        hT = [moe(H) for _ in range(2)]
        yb = [moe(D) for _ in range(2)]
        tacc = moe(3, MT)
        past = moe(MT, NX)
        dest_u = moe(MT, dt=U32)

        ident = sb("ident", [P, P])
        identb = sb("identb", [P, P], BF16)
        tri = sb("tri", [P, P])
        trib = sb("trib", [P, P], BF16)
        ones = sb("ones", [P, P])
        onesb = sb("onesb", [P, P], BF16)
        col0 = sb("col0", [P, D])
        col1 = sb("col1", [P, P])
        prow = sb("prow", [P, 1])
        prow1 = sb("prow1", [P, 1])
        minsub = sb("minsub", [P, 1])
        maxsub = sb("maxsub", [P, 1])
        slotnum = sb("slotnum", [P, G])
        sought = sb("sought", [P, G])
        sought_in = sb("sought_in", [P, G])
        seen = sb("seen", [P, 2, G])
        found = sb("found", [P, 3, G])
        Mrot = sb("Mrot", [P, KB, D])
        comb = sb("comb", [P, KB, D])
        small = sb("small", [P, 16])
        bq_c = sb("bq_c", [P, KB])
        bk_c = sb("bk_c", [P, KB])
        bng_c = sb("bng_c", [P, KB])
        bnb_c = sb("bnb_c", [P, KB])
        gamB = sb("gamB", [P, D])
        betB = sb("betB", [P, D])
        wr_s = sb("wr_s", [P, KB, NX])
        brB = sb("brB", [P, NX])
        addparts = sb("addparts", [96, D], BF16)
        mv = sb("mv", [P, NT, 2])
        rstd = sb("rstd", [P, NT])
        nmr = sb("nmr", [P, NT])
        run_m = sb("run_m", [P, KB])
        grp_m = sb("grp_m", [P, KB])
        new_m = sb("new_m", [P, KB])
        ebias = sb("ebias", [P, KB])
        dm = sb("dm", [P, KB])
        alpha = sb("alpha", [P, KB])
        alpha2 = sb("alpha2", [P, KB])
        gsum = sb("gsum", [P, KB])
        ssum = sb("ssum", [P, KB])
        rsum = sb("rsum", [P, KB])
        n_groups_i = sb("n_groups_i", [1, 1], I32)
        total = sb("total", [P, 1])
        poff = sb("poff", [P, 1])

        st2 = sb("st2", [P, 4, 6])
        mv2 = sb("mv2", [P, 4, 2])
        dev = sb("dev", [P, 4])
        scl = sb("scl", [P, 4])
        shift = sb("shift", [P, 4])
        lg = sb("lg", [P, 4, NX])
        top = sb("top", [P, 4, 8])
        topi = sb("topi", [P, 4, 8], U32)
        topf = sb("topf", [P, 4, 8])
        oh = sb("oh", [P, 2 * 4, NX])
        slotf = sb("slotf", [P, 2 * 4])
        sel = sb("sel", [P, 2 * 4, NX])
        mskb = sb("mskb", [P, 5, NX], BF16)
        slot8 = sb("slot8", [P, 4, NX])
        base8 = sb("base8", [P, NX])
        reg8 = sb("reg8", [P, NX])
        slot_now = [sb(f"slot_now{b}", [P, 2 * 4], U32) for b in range(2)]
        tokens = sb("tokens", [P, 4])
        padf = sb("padf", [P, NX])
        padu = sb("padu", [P, NX], U32)
        topd = sb("topd", [P, NT])
        wexp = sb("wexp", [P, NT])
        w_a = sb("w_a", [P, NT])
        w_b = sb("w_b", [P, NT])
        zrow = sb("zrow", [P, DM])
        ntile = sb("ntile", [P, 3, NX])
        tnum = sb("tnum", [P, MT])
        second = sb("second", [P, 2])
        dest_now = [sb(f"dest_now{b}", [P, 1], U32) for b in range(2)]
        pairs_i = sb("pairs_i", [1, 2], I32)
        ttab = sb("ttab", [1, 2, MT], I32)

        bank = [ctx.enter_context(nc.psum_tensor(f"bank{i}", [P, 512], F32)) for i in range(8)]
        pw = [bank[h][:, :].rearrange("p (c n) -> p c n", c=2) for h in range(2)]
        jb = [bank[2 + h][:, 0:2 * P].rearrange("p (c n) -> p c n", c=2) for h in range(2)]
        gb = [bank[5 + h][:, :].rearrange("p (c n) -> p c n", c=2) for h in range(2)]
        TB, apV, apM, misc = bank[4:8]

        S = {}
        for n in ("const consts edges wload xld0 xld1 xld2 xld3 xld4 xld5 xld_tail sines cnt_ready poff_ready counts_own dve act pool pe recs_out ends_in "
                  "xn_ready xT_psum xT_done keys_psum ebias_ready exp_done exT_psum exT_done "
                  "mix_psum mix_acc Lready LT_psum LT_done WK_act WK_dve pw_psum jb_psum V_psum V_done M_psum M_done "
                  "blk_seen rows_in pos_seen recs_in sought_next found_own flds_ready TB_psum mask_own lim_ready mask_ready Lparts Bparts B_ready GT_psum GT_done ST_ready STb_ready J0_ready D_psum D_done "
                  "reserve ngroups comb_pe comb_dve parts_own x2_psum stg_done x2_done "
                  "std_need std_done scl_ready z_ready xf_ready xfT_psum xfT_done lg_psum msk_ready rank_psum slot_ready "
                  "w_loaded bias_loaded pads_ready pads zeros_out tiles_ready sc00 sc01 sc02 sc03 sc10 sc11 sc12 sc13 xt0 xt1 xm0 xm1 dest_ready dest_copied "
                  "xmT_psum xmT_done h_psum hpre_done hact_done hT_psum hT_done y_psum y_done ysc0 ysc1 "
                  "back0 back1 back2 back3 out0 out1 out2 out3 sum_a fin_done wexp_need wexp_done x_own r_own t_own tail_own tokens_next second_own "
                  "scan_ok angles_ok xstats_ok pn_ok pT_ok lamstats_ok bn_ok chunk_init_ok dve_settled pool_settled idx_set empty_group swap_ready").split():
            S[n] = sem("s_" + n)
        block = ctx.enter_context(nc.Block())

        def chain(eng, s):
            n = [0]

            def link(ins):
                n[0] += 1
                ins.then_inc(s, 1)
                eng.wait_ge(s, n[0])
            link.n = n
            return link

        def at_least(eng, s, v):
            if not isinstance(v, int) or v > 0:
                eng.wait_ge(s, v)

        def settle(eng):
            eng.sem_inc(S["dve_settled"] if eng is nc.vector else S["pool_settled"], 1)

        def bcast_row(ap, n):
            return ap.rearrange("(a n) -> a n", a=1).broadcast_to([P, n])

        def over_tiles(v, nt):
            return v.rearrange("p (a d) -> p a d", a=1).broadcast_to([v.shape[0], nt, v.shape[1]])

        THIRD = (FULL // 4 - 3) // 9
        NG12 = FULL // 4
        xg_src = x[0:FULL * P, :].rearrange("(t p) d -> p t d", p=P)

        @block.sync
        def _(sp):
            for i, c in enumerate(range(0, FULL, 8)):
                sp.dma_start(x_all[:, c:c + 8, :], xg_src[:, c:c + 8, :]).then_inc(S[f"xld{i}"], 16)
            sp.dma_start(x_all[0:TAIL, FULL, :], x[FULL * P:N, :]).then_inc(S["xld_tail"], 16)
            for dstt, s in ((wq, W_qk[0]), (wk, W_qk[1]), (wv, W_v)):
                sp.dma_start(dstt, s.rearrange("(k p) e -> p k e", p=P)).then_inc(S["wload"], 16)
            sp.dma_start(wr_s[:, :, :], Wr.rearrange("(k p) e -> p k e", p=P)).then_inc(S["wload"], 16)
            for dstt, s in ((bq_c, b_qk[0]), (bk_c, b_qk[1]), (bng_c, bn_gamma), (bnb_c, bn_beta)):
                with nc.allow_non_contiguous_dma(reason="one column of a small vector"):
                    sp.dma_start(dstt[:, :], s.rearrange("(k p) -> p k", p=P)).then_inc(S["wload"], 16)
            for dstt, s, n in ((bvB, b_v, D), (gamB, gamma, D), (betB, beta, D), (brB, br, NX)):
                sp.dma_start(dstt[:, :], bcast_row(s, n)).then_inc(S["wload"], 16)
            sp.dma_start(i_raw, src.rearrange("(p l) -> p l", p=EP)).then_inc(S["edges"], 16)
            sp.dma_start(j_raw, dst.rearrange("(p l) -> p l", p=EP)).then_inc(S["edges"], 16)
            sp.dma_start(theta, edge_weight.rearrange("(p l) -> p l", p=EP)).then_inc(S["edges"], 16)
            sp.wait_ge(S["recs_out"], 1)
            sp.dma_start(incl_out, incl[:, :]).then_inc(S["reserve"], 16)
            with nc.allow_non_contiguous_dma(reason="four words per partition"):
                sp.dma_start(ends_d, incl.rearrange("p (c l) -> p c l", l=BL)[:, :, BL - 1]).then_inc(S["reserve"], 16)
            sp.wait_ge(S["sines"], 2)
            sp.dma_start(rec_d.rearrange("(p l) r -> p (l r)", p=EP), rec.rearrange("p l r -> p (l r)")).then_inc(S["reserve"], 16)
            sp.wait_ge(S["reserve"], 48)
            sp.wait_ge(S["xn_ready"], NG12 + 1)
            sp.dma_start(ends, ends_d.rearrange("a b -> (a b)").rearrange("(o n) -> o n", o=1).broadcast_to([P, NB])).then_inc(S["ends_in"], 16)
            sp.wait_ge(S["bn_ok"], 1)
            sp.wait_ge(S["recs_in"], 2 * 16 * G)
            sp.wait_ge(S["rows_in"], 3 * 16 * G)
            for e in range(NX):
                if e:
                    sp.wait_ge(S["w_loaded"], 32 * e)
                sp.dma_start(w1s[:, e], W1[e].rearrange("(k p) h -> p k h", p=P)).then_inc(S["w_loaded"], 16)
                sp.dma_start(w2s[:, e], W2[e].rearrange("(k p) d -> p k d", p=P)).then_inc(S["w_loaded"], 16)
            sp.wait_ge(S["consts"], 1)
            for t in range(SPARE):
                r = NX * STRIDE + t * P
                sp.dma_start(send_d[r:r + P, :], zrow[:, :]).then_inc(S["zeros_out"], 16)

            def load_x(q, b):
                sp.dma_start(xt[b], x[bass.ds(q * GRP, GRP), :].rearrange("(t p) d -> p t d", p=P)).then_inc(S[f"xt{b}"], 16)
            for b in range(2):
                load_x(b, b)
            with sp.Fori(1, NG12 // 2) as k:
                for b in range(2):
                    sp.wait_ge(S["xf_ready"], k * 2 + (b - 1))
                    load_x(k * 2 + b, b)
            sp.wait_ge(S["xf_ready"], NG12 - 1)
            sp.dma_start(xt[0][0:TAIL, 0, :], x[FULL * P:N, :]).then_inc(S["xt0"], 16)

            sp.wait_ge(S["x2_psum"], NG12 + 1)
            sp.dma_start(b1B, b1.rearrange("e h -> (e h)").rearrange("(o n) -> o n", o=1).broadcast_to([P, NX * H]).rearrange("p (e h) -> p e h", e=NX)).then_inc(S["bias_loaded"], 16)
            sp.dma_start(b2B, b2.rearrange("e h -> (e h)").rearrange("(o n) -> o n", o=1).broadcast_to([P, NX * D]).rearrange("p (e h) -> p e h", e=NX)).then_inc(S["bias_loaded"], 16)

            sp.wait_ge(S["tiles_ready"], 1)
            for b in range(2):
                for t in range(4):
                    sp.wait_ge(S[f"sc{b}{t}"], 32 * (NG12 // 2 + (b == 0 and t == 0)))
            sp.wait_ge(S["pads"], 16 * NX)
            sp.wait_ge(S["zeros_out"], 16 * SPARE)

            def load_tile(i, b):
                r = sp.value_load(ttab[0:1, 1, bass.ds(i, 1)], min_val=0, max_val=(NX + 1) * STRIDE - P)
                sp.dma_start(xm[b], send_d[bass.ds(r, P), :]).then_inc(S[f"xm{b}"], 16)
            for b in range(2):
                load_tile(b, b)
            pairs = sp.value_load(pairs_i[0:1, 0:1], min_val=LEAST, max_val=MT // 2)
            with sp.Fori(1, pairs) as k:
                for b in range(2):
                    sp.wait_ge(S["xmT_psum"], k * 2 + (b - 1))
                    sp.wait_ge(S["dest_ready"], k * 2 + (b - 1))
                    load_tile(k * 2 + b, b)

            sent = pairs * 16
            sp.wait_ge(S["ysc0"], sent)
            sp.wait_ge(S["ysc1"], sent)

            def load_back(q, b):
                for c, y in ((0, ya), (1, yc)):
                    sp.dma_start(y[b], back_d[bass.ds(q * GRP + c * N, GRP), :].rearrange("(t p) d -> p t d", p=P))\
                        .then_inc(S[f"back{b}"], 16)
            for b in range(FB):
                load_back(b, b)
            with sp.Fori(1, NG12 // FB) as k:
                for b in range(FB):
                    sp.wait_ge(S[f"out{b}"], k * 16)
                    load_back(k * FB + b, b)
            sp.wait_ge(S["out0"], (NG12 // FB) * 16)
            for c, y in ((0, ya), (1, yc)):
                sp.dma_start(y[0][0:TAIL, 0, :], back_d[c * N + FULL * P:c * N + N, :]).then_inc(S["back0"], 16)

        @block.gpsimd
        def _(pool):
            link = chain(pool, S["pool"])
            TSp, TTp = nc.gpsimd.tensor_scalar, nc.gpsimd.tensor_tensor
            nc.gpsimd.memset(ones[:, :], 1.0).then_inc(S["const"], 1)
            nc.gpsimd.memset(onesb[:, :], 1.0).then_inc(S["const"], 1)
            nc.gpsimd.memset(zrow[:, 0:D], 0.0).then_inc(S["const"], 1)
            nc.gpsimd.memset(zrow[:, D:DM], 3.0 * N).then_inc(S["const"], 1)
            link(nc.gpsimd.memset(ident[:, :], 0.0))
            link(nc.gpsimd.affine_select(out=ident[:, :], in_=ident[:, :], compare_op=ALU.not_equal, fill=1.0,
                                         base=0, pattern=[[-1, P]], channel_multiplier=1))
            link(nc.gpsimd.tensor_copy(identb[:, :], ident[:, :]))
            link(nc.gpsimd.memset(tri[:, :], 0.0))
            link(nc.gpsimd.affine_select(out=tri[:, :], in_=tri[:, :], compare_op=ALU.is_ge, fill=1.0,
                                         base=0, pattern=[[-1, P]], channel_multiplier=1))
            link(nc.gpsimd.tensor_copy(trib[:, :], tri[:, :]))
            for ap, pat, base, mult in ((col0[:, :], [[1, D]], 0, 0), (col1[:, :], [[1, P]], 1, 0),
                                        (prow[:, :], [[0, 1]], 0, 1), (prow1[:, :], [[0, 1]], 1, 1),
                                        (slotnum[:, :], [[CAP, G]], 0, 1), (reg8[:, :], [[STRIDE, NX]], 0, 0),
                                        (tnum[:, :], [[1, MT]], 0, 0),
                                        (tokens[:, :], [[P, 4]], N, 1), (sought[:, :], [[CAP, G]], 0, 1)):
                link(nc.gpsimd.iota(ap, pattern=pat, base=base, channel_multiplier=mult,
                                    allow_small_or_imprecise_dtypes=True))
            link(nc.gpsimd.tensor_scalar(sought[:, :], sought[:, :], 0.5, None, ALU.add))
            link(nc.gpsimd.tensor_scalar(minsub[:, :], prow[:, :], float(P - 1), None, ALU.is_ge))
            link(nc.gpsimd.tensor_scalar(maxsub[:, :], prow[:, :], 1.0, None, ALU.is_ge))
            pool.wait_ge(S["const"], 4)
            link(nc.gpsimd.memset(small[:, 0:12], EPS))
            nc.gpsimd.memset(small[:, 12:13], EPS * EPS).then_inc(S["consts"], 1)

            pool.wait_ge(S["edges"], 48)
            link(nc.gpsimd.tensor_copy(i_f, i_raw))
            link(nc.gpsimd.tensor_copy(j_f, j_raw))
            link(TSp(g_i, i_f, float(D), None, ALU.is_ge))
            link(TSp(g_j, j_f, float(D), None, ALU.is_ge))
            link(TTp(incl, g_i, g_j, ALU.add))
            TSp(cnt, incl, -1.0, 2.0, ALU.mult, ALU.add).then_inc(S["cnt_ready"], 1)
            link(TSp(rec[:, :, 0], i_f, float(D - 1), None, ALU.min))
            link(TSp(rec[:, :, 2], j_f, float(D - 1), None, ALU.min))
            link(nc.gpsimd.tensor_copy(rec[:, :, 6], g_i))
            link(TTp(rec[:, :, 1], rec[:, :, 2], rec[:, :, 0], ALU.subtract))
            link(nc.gpsimd.memset(rec[:, :, 7], 0.0))
            part_turn = i_f
            link(TSp(turn, theta, 1.0 / (2 * PI), MAGIC, ALU.mult, ALU.add))
            link(TSp(turn, turn, -MAGIC, None, ALU.add))
            for part in (TURN_HI, TURN_MID, TURN_LO):
                link(TSp(part_turn, turn, -part, None, ALU.mult))
                link(TTp(theta, theta, part_turn, ALU.add))
            link(TSp(theta, theta, 3.1415925, -3.1415925, ALU.min, ALU.max))
            link(TSp(turn, theta, 0.0, None, ALU.max))
            link(TSp(part_turn, theta, 0.0, None, ALU.min))
            link(TTp(turn, turn, part_turn, ALU.subtract))
            link(TSp(turn, turn, -1.0, PI / 2, ALU.mult, ALU.add))
            pool.sem_inc(S["angles_ok"], 1)
            pool.wait_ge(S["scan_ok"], 1)
            pool.wait_ge(S["poff_ready"], 1)
            link(TSp(incl, incl, poff[0:EP, :], None, ALU.add))
            TTp(rec[:, :, 5], incl, cnt, ALU.subtract).then_inc(S["recs_out"], 1)

            def found_by(k, i, last):
                last.then_inc(S["found_own"], 1)
                pool.wait_ge(S["found_own"], k * 4 + i)
                settle(pool)

            def gather_blocks(k):
                pool.wait_ge(S["blk_seen"], k + 1)
                settle(pool)
                nc.gpsimd.tensor_copy(sought_in[:, :], sought[:, :])
                found_by(k, 1, TSp(found[:, 0, :], seen[:, 0, :], 0.5, NB / 2.0, ALU.mult, ALU.add))
                found_by(k, 2, TSp(found[:, 1, :], found[:, 0, :], float(NB - 1), None, ALU.min))
                nc.gpsimd.tensor_copy(idx[:, 0, :], found[:, 1, :]).then_inc(S["idx_set"], 1)
                pool.wait_ge(S["idx_set"], k * 2 + 1)
                settle(pool)
                TSp(sought[:, :], sought[:, :], float(CAP * G), None, ALU.add).then_inc(S["sought_next"], 1)
                for g in range(G):
                    nc.gpsimd.indirect_dma_start(
                        out=rows[:, g, :], out_offset=None, in_=incl_d,
                        in_offset=bass.IndirectOffsetOnAxis(ap=idx[:, 0, g:g + 1], axis=0)).then_inc(S["rows_in"], 16)

            def gather_steps(k):
                pool.wait_ge(S["pos_seen"], k + 1)
                at_least(pool, S["flds_ready"], k)
                settle(pool)
                TSp(found[:, 0, :], found[:, 1, :], float(BL), BL / 2.0, ALU.mult, ALU.add)
                found_by(k, 3, TSp(found[:, 2, :], seen[:, 1, :], 0.5, None, ALU.mult))
                found_by(k, 4, nc.gpsimd.tensor_tensor(found[:, 2, :], found[:, 2, :], found[:, 0, :], ALU.add))
                TSp(idx[:, 1, :], found[:, 2, :], float(NE - 1), None, ALU.min).then_inc(S["idx_set"], 1)
                pool.wait_ge(S["idx_set"], k * 2 + 2)
                settle(pool)
                for g in range(G):
                    nc.gpsimd.indirect_dma_start(
                        out=recs[:, g, :], out_offset=None, in_=rec_d,
                        in_offset=bass.IndirectOffsetOnAxis(ap=idx[:, 1, g:g + 1], axis=0)).then_inc(S["recs_in"], 16)

            def masks(k):
                pool.wait_ge(S["lim_ready"], k + 1)
                settle(pool)
                for g in range(G):
                    last = TSp(slotmask[:, g, :], col0[:, 0:P], fld[:, 9, g:g + 1], None, ALU.is_lt)
                last.then_inc(S["mask_own"], 1)
                pool.wait_ge(S["mask_own"], k + 1)
                nc.gpsimd.tensor_tensor(slotmask[:, :, :], slotmask[:, :, :],
                                        col1[:, :].rearrange("p (a n) -> p a n", a=1).broadcast_to([P, G, P]), ALU.mult)\
                    .then_inc(S["mask_ready"], 1)

            def join_L(k):
                pool.wait_ge(S["Lparts"], k + 1)
                nc.gpsimd.tensor_tensor(Lnext[:, :, :], Lself[:, :, :], hits[:, 0:G, :], ALU.add).then_inc(S["Lready"], 1)
            pool.wait_ge(S["ngroups"], 1)
            pool.wait_ge(S["reserve"], 48)
            n = pool.value_load(n_groups_i[0:1, 0:1], min_val=1, max_val=4 * NE)
            pool.wait_ge(S["xn_ready"], NG12 + 1)
            nc.gpsimd.memset(Bmat[:, :, :], 0.0)
            nc.gpsimd.memset(WK[:, :, :], 0.0)
            nc.gpsimd.memset(STm[:, :, :], 0.0).then_inc(S["empty_group"], 1)
            gather_blocks(0)
            gather_steps(0)
            gather_blocks(1)
            gather_steps(1)
            join_L(0)
            gather_blocks(2)
            pool.sem_inc(S["B_ready"], 1)
            with pool.Fori(0, n) as k:
                masks(k + 1)
                gather_steps(k + 2)
                gather_blocks(k + 3)
                pool.wait_ge(S["Bparts"], k + 1)
                nc.gpsimd.tensor_tensor(Bmat[:, :, :], Bmat[:, :, :], Bself[:, :, :], ALU.add).then_inc(S["B_ready"], 1)
                join_L(k + 1)

            def scatter(q, b, nt=4, rows_=P):
                pool.wait_ge(S["slot_ready"], q + 1)
                settle(pool)
                for t in range(nt):
                    for c in range(2):
                        nc.gpsimd.indirect_dma_start(
                            out=send_d, out_offset=bass.IndirectOffsetOnAxis(ap=slot_now[b][0:rows_, c * 4 + t:c * 4 + t + 1], axis=0),
                            in_=xf[b][0:rows_, t, :], in_offset=None).then_inc(S[f"sc{b}{t}"], 16)
            with pool.Fori(0, NG12 // 2) as k:
                for b in range(2):
                    scatter(k * 2 + b, b)
            scatter(NG12, 0, 1, TAIL)
            pool.wait_ge(S["pads_ready"], 1)
            for e in range(NX):
                nc.gpsimd.indirect_dma_start(
                    out=send_d, out_offset=bass.IndirectOffsetOnAxis(ap=padu[:, e:e + 1], axis=0),
                    in_=zrow[:, :], in_offset=None).then_inc(S["pads"], 16)

            def send_back(i, b, k):
                at_least(pool, S[f"ysc{b}"], k * 16)
                pool.wait_ge(S["dest_ready"], i + 1)
                nc.gpsimd.tensor_copy(dest_now[b][:, :], dest_u[:, bass.ds(i, 1)]).then_inc(S["dest_copied"], 1)
                pool.wait_ge(S["dest_copied"], i + 1)
                pool.wait_ge(S["y_done"], i + 2)
                settle(pool)
                nc.gpsimd.indirect_dma_start(
                    out=back_d, out_offset=bass.IndirectOffsetOnAxis(ap=dest_now[b][:, :], axis=0),
                    in_=yb[b], in_offset=None, bounds_check=2 * N - 1, oob_is_err=False).then_inc(S[f"ysc{b}"], 16)
            pool.wait_ge(S["tiles_ready"], 1)
            pairs = pool.value_load(pairs_i[0:1, 0:1], min_val=LEAST, max_val=MT // 2)
            for b in range(2):
                send_back(b, b, 0)
            with pool.Fori(1, pairs) as k:
                for b in range(2):
                    send_back(k * 2 + b, b, k)

        @block.scalar
        def _(act):
            eps, eps_sq = small[:, 0:1], small[:, 12:13]
            act.wait_ge(S["xstats_ok"], 1)
            act.wait_ge(S["consts"], 1)
            nc.scalar.activation(rstd[:, :], mv[:, :, 1], ACT.Sqrt, bias=eps).then_inc(S["act"], 1)

            def search(k, gs):
                at_least(act, S["sought_next"], k)
                for g in gs:
                    last = nc.scalar.activation(junk[:, g, :], ends, ACT.Sign, bias=sought[:, g:g + 1], scale=-1.0,
                                                accum_out=seen[:, 0, g:g + 1])
                if gs[-1] == G - 1:
                    last.then_inc(S["blk_seen"], 1)

            def search_in(k, gs):
                act.wait_ge(S["rows_in"], k * (16 * G) + 16 * G)
                for g in gs:
                    last = nc.scalar.activation(rows[:, g, :], rows[:, g, :], ACT.Sign, bias=sought_in[:, g:g + 1], scale=-1.0,
                                                accum_out=seen[:, 1, g:g + 1])
                if gs[-1] == G - 1:
                    last.then_inc(S["pos_seen"], 1)

            def turned_in(q, W=GRP):
                act.wait_ge(S["xT_psum"], q + 1)
                for kb in range(KB):
                    last = nc.scalar.activation(xnT[:, kb, bass.ds(q * GRP, W)], bank[kb][:, 0:W], ACT.Copy)
                last.then_inc(S["xT_done"], 1)

            def exps(q, W=GRP):
                act.wait_ge(S["ebias_ready"], q + 1)
                at_least(act, S["exT_psum"], q)
                nc.scalar.activation(alpha[:, :], dm[:, :], ACT.Exp)
                for kb in range(KB):
                    last = nc.scalar.activation(ex[:, kb, 0:W], bank[2 + kb][:, 0:W], ACT.Exp,
                                                bias=ebias[:, kb:kb + 1], accum_out=gsum[:, kb:kb + 1])
                last.then_inc(S["exp_done"], 1)
            turned_in(0)
            turned_in(1)
            exps(0)
            with act.Fori(0, NG12 // 2) as q:
                turned_in(q + 2)
                exps(q + 1)
            act.wait_ge(S["angles_ok"], 1)
            nc.scalar.activation(rec[:, :, 4], theta[:, :], ACT.Sin).then_inc(S["sines"], 1)
            nc.scalar.activation(rec[:, :, 3], turn[:, :], ACT.Sin).then_inc(S["sines"], 1)
            with act.Fori(NG12 // 2, NG12 - 2) as q:
                turned_in(q + 2)
                exps(q + 1)
            turned_in(NG12, TAIL)
            exps(NG12 - 1)
            exps(NG12, TAIL)
            act.wait_ge(S["ends_in"], 16)
            search(0, range(G))
            search_in(0, range(G))
            act.wait_ge(S["lamstats_ok"], 1)
            nc.scalar.activation(small[:, 4:6], small[:, 6:8], ACT.Sqrt, bias=eps).then_inc(S["act"], 1)

            act.wait_ge(S["ngroups"], 1)
            n = act.value_load(n_groups_i[0:1, 0:1], min_val=1, max_val=4 * NE)

            def apply_v(k, g):
                act.wait_ge(S["V_psum"], k * G + (g + 1))
                nc.scalar.activation(Vs[:, :], apV[:, 0:D], ACT.Copy).then_inc(S["V_done"], 1)

            def turned_L(k):
                act.wait_ge(S["LT_psum"], k + 1)
                nc.scalar.activation(LTnext[:, :, :], TB[:, :].rearrange("p (g n) -> p g n", g=G), ACT.Copy)\
                    .then_inc(S["LT_done"], 1)

            def moved_GT(k):
                act.wait_ge(S["GT_psum"], k + 1)
                for h in range(2):
                    last = nc.scalar.activation(GT[:, 2 * h:2 * h + 2, :], gb[h], ACT.Copy)
                last.then_inc(S["GT_done"], 1)

            def last_writes(k):
                act.wait_ge(S["ST_ready"], k + 1)
                at_least(act, S["D_psum"], k)
                nc.scalar.activation(STb[:, :, :], STm[:, :, :], ACT.Copy).then_inc(S["STb_ready"], 1)
            search(1, range(G))
            search_in(1, range(G))
            turned_L(0)
            search(2, range(G))
            with act.Fori(0, n) as k:
                for s in range(2 * LEVELS):
                    lv, hf = s // 2, s % 2
                    hh = slice(2 * hf, 2 * hf + 2)
                    if lv < LEVELS - 1:
                        act.wait_ge(S["pw_psum"], k * (2 * (LEVELS - 1)) + (s + 1))
                        if lv == 1:
                            act.wait_ge(S["jb_psum"], k * (2 * (LEVELS - 1)) + (hf + 1))
                        w = 2 * P if lv < LEVELS - 2 else P // 2
                        nc.scalar.activation(WK[:, hh, 0:w], pw[hf][:, :, 0:w], ACT.Copy).then_inc(S["WK_act"], 1)
                    if s == 1:
                        moved_GT(k)
                    if s == 3:
                        last_writes(k)
                    if V_AT <= s < V_AT + 2 * G and (s - V_AT) % 2 == 0:
                        apply_v(k, (s - V_AT) // 2)
                    if s in (0, 1):
                        search_in(k + 2, (2 * s, 2 * s + 1))
                    if s in (4, 5):
                        search(k + 3, (2 * s - 8, 2 * s - 7))
                turned_L(k + 1)
            moved_GT(n)
            last_writes(n)
            for g in range(G):
                apply_v(n, g)

            def stage(q, b, W=GRP):
                at_least(act, S["x2_psum"], q - 1)
                nc.scalar.activation(stg[b][:, :, 0:W], xnT[:, :, bass.ds(q * GRP, W)], ACT.Copy).then_inc(S["stg_done"], 1)

            def norms(q):
                act.wait_ge(S["std_need"], q + 1)
                nc.scalar.activation(dev[:, :], mv2[:, :, 1], ACT.Sqrt, bias=eps_sq, scale=1.0 + EPS).then_inc(S["std_done"], 1)

            def normed(q, b, nt=4, r=P):
                act.wait_ge(S["scl_ready"], q + 1)
                for t in range(nt):
                    last = nc.scalar.activation(xt[b][0:r, t, :], x2_all[0:r, bass.ds(q * 4 + t, 1), :].rearrange("p a d -> p (a d)"),
                                                ACT.Identity, bias=shift[0:r, t:t + 1], scale=scl[0:r, t:t + 1])
                last.then_inc(S["z_ready"], 1)

            def turned_xf(q, W=GRP):
                act.wait_ge(S["xfT_psum"], q + 1)
                for kb in range(KB):
                    last = nc.scalar.activation(xfT[:, kb, 0:W], bank[2 + kb][:, 0:W], ACT.Copy)
                last.then_inc(S["xfT_done"], 1)
            act.wait_ge(S["comb_dve"], 4)
            stage(0, 0)
            stage(1, 1)
            norms(0)
            normed(0, 0)
            stage(2, 0)

            def route_step(q, b):
                const = isinstance(q, int)
                turned_xf(q, GRP if not const or q < NG12 else TAIL)
                if not const or q < NG12:
                    norms(q + 1)
                    normed(q + 1, 1 - b, *((1, TAIL) if const and q + 1 == NG12 else (4, P)))
                if not const or q + 3 <= NG12:
                    stage(q + 3, 1 - b, TAIL if const and q + 3 == NG12 else GRP)
            with act.Fori(0, NG12 // 2 - 2) as k:
                for b in range(2):
                    route_step(k * 2 + b, b)
            for q in range(NG12 - 4, NG12 + 1):
                route_step(q, q % 2)
            act.wait_ge(S["wexp_need"], 1)
            nc.scalar.activation(wexp[:, :], topd[:, :], ACT.Exp).then_inc(S["wexp_done"], 1)

            def moe_in(i, b):
                act.wait_ge(S["xmT_psum"], i + 1)
                nc.scalar.activation(xmT[b], bank[b][:, 0:D], ACT.Copy).then_inc(S["xmT_done"], 1)

            def moe_gelu(i, b):
                act.wait_ge(S["hpre_done"], i + 1)
                nc.scalar.activation(hact[b], hpre[b], ACT.Gelu).then_inc(S["hact_done"], 1)

            def moe_step(i, b, left=4):
                if left > 3:
                    moe_in(i + 3, 1 - b)
                if left > 2 and (not isinstance(i, int) or i + 2 >= 0):
                    moe_gelu(i + 2, b)
            act.wait_ge(S["tiles_ready"], 1)
            for i in range(-3, 0):
                moe_step(i, i % 2)
            m = act.value_load(pairs_i[0:1, 1:2], min_val=LEAST - 2, max_val=MT // 2 - 2)
            with act.Fori(0, m) as k:
                for b in range(2):
                    moe_step(k * 2 + b, b)
            for j in range(4):
                moe_step(m * 2 + j, j % 2, 4 - j)

            def store_out(q, b):
                act.wait_ge(S["fin_done"], q + 1)
                act.dma_start(out[bass.ds(q * GRP, GRP), :].rearrange("(t p) d -> p t d", p=P), yc[b]).then_inc(S[f"out{b}"], 16)
            with act.Fori(0, NG12 // FB) as k:
                for b in range(FB):
                    store_out(k * FB + b, b)
            act.wait_ge(S["fin_done"], NG12 + 1)
            act.dma_start(out[FULL * P:N, :], yc[0][0:TAIL, 0, :]).then_inc(S["out0"], 16)
            act.wait_ge(S["out0"], 16 * (NG12 // FB + 1))
            for b in range(1, FB):
                act.wait_ge(S[f"out{b}"], 16 * (NG12 // FB))

        @block.vector
        def _(dve):
            link = chain(dve, S["dve"])
            TT, TS, STT = nc.vector.tensor_tensor, nc.vector.tensor_scalar, nc.vector.scalar_tensor_tensor

            link(nc.vector.memset(mv[:, :, :], 0.0))
            link(nc.vector.memset(Mrot[:, :, :], 0.0))
            for i, c in enumerate(range(0, FULL, 8)):
                dve.wait_ge(S[f"xld{i}"], 16)
                for t in range(c, c + 8):
                    last = nc.vector.bn_stats(stats[:, t, :], x_all[:, t, :])
                link(last)
                for t in range(c, c + 8):
                    nc.vector.bn_aggr(mv[:, t, :], stats[:, t, :])
            dve.wait_ge(S["xld_tail"], 16)
            link(nc.vector.bn_stats(stats[0:TAIL, FULL, :], x_all[0:TAIL, FULL, :]))
            link(nc.vector.bn_aggr(mv[0:TAIL, FULL, :], stats[0:TAIL, FULL, :]))
            dve.sem_inc(S["xstats_ok"], 1)
            nc.vector.memset(run_m[:, :], -1e30)
            nc.vector.memset(ssum[:, :], 0.0)
            link(nc.vector.memset(Pacc, 0.0))
            dve.wait_ge(S["act"], 1)
            link(nc.vector.reciprocal(rstd[:, :], rstd[:, :]))
            link(STT(nmr[:, :], mv[:, :, 0], -1.0, rstd[:, :], ALU.mult, ALU.mult))
            base = link.n[0]
            PERM = 5

            def norm_rows(q, b, W=GRP):
                nt, r = (W + P - 1) // P, W % P or P
                at_least(dve, S["mix_psum"], q - 2)
                for t in range(nt):
                    tt = q * 4 + t
                    last = TS(xng[b][0:r, t, :], x_all[0:r, bass.ds(tt, 1), :].rearrange("p a d -> p (a d)"),
                              rstd[0:r, bass.ds(tt, 1)], nmr[0:r, bass.ds(tt, 1)], ALU.mult, ALU.add)
                last.then_inc(S["xn_ready"], 1)

            def maxima(q, W=GRP):
                n0 = q * PERM + base
                dve.wait_ge(S["keys_psum"], q + 1)
                for kb in range(KB):
                    last = nc.vector.reduce_max(grp_m[:, kb:kb + 1], bank[2 + kb][:, 0:W], AX_X)
                last.then_inc(S["dve"], 1)
                dve.wait_ge(S["dve"], n0 + 1)
                at_least(dve, S["exp_done"], q)
                TT(new_m[:, :], run_m[:, :], grp_m[:, :], ALU.max).then_inc(S["dve"], 1)
                dve.wait_ge(S["dve"], n0 + 2)
                TT(dm[:, :], run_m[:, :], new_m[:, :], ALU.subtract)
                TT(ebias[:, :], bk_c[:, :], new_m[:, :], ALU.subtract).then_inc(S["dve"], 1)
                dve.wait_ge(S["dve"], n0 + 3)
                nc.vector.tensor_copy(run_m[:, :], new_m[:, :])
                TT(ebias[:, :], ebias[:, :], bk_c[:, :], ALU.subtract).then_inc(S["ebias_ready"], 1)

            def turned_exps(q, W=GRP):
                nt, r = (W + P - 1) // P, W % P or P
                dve.wait_ge(S["exT_psum"], q + 1)
                for kb in range(KB):
                    last = nc.vector.tensor_copy(exT[0:r, 0:nt, kb * P:(kb + 1) * P],
                                                 bank[4 + kb][0:r, 0:nt * P].rearrange("p (t d) -> p t d", d=P))
                last.then_inc(S["exT_done"], 1)
                TT(ssum[:, :], ssum[:, :], alpha[:, :], ALU.mult).then_inc(S["dve"], 1)
                dve.wait_ge(S["dve"], q * PERM + (base + 4))
                TT(ssum[:, :], ssum[:, :], gsum[:, :], ALU.add)
                nc.vector.tensor_copy(alpha2[:, :], alpha[:, :]).then_inc(S["dve"], 1)
                dve.wait_ge(S["dve"], q * PERM + (base + 5))

            def weighted_sum(q):
                dve.wait_ge(S["mix_psum"], q + 1)
                for kb in range(KB):
                    last = STT(Pacc[:, kb, :], Pacc[:, kb, :], alpha2[:, kb:kb + 1], bank[6][:, kb * D:(kb + 1) * D],
                               ALU.mult, ALU.add)
                last.then_inc(S["mix_acc"], 1)
            dve.wait_ge(S["consts"], 1)
            dve.wait_ge(S["wload"], 16 * 12)

            def mix_step(q, b):
                const = isinstance(q, int)
                if not const or q > 0:
                    weighted_sum(q - 1)
                turned_exps(q, TAIL if const and q == NG12 else GRP)
                if not const or q + 2 <= NG12:
                    norm_rows(q + 2, (b + 2) % 3, TAIL if const and q + 2 == NG12 else GRP)
                if not const or q + 1 <= NG12:
                    maxima(q + 1, TAIL if const and q + 1 == NG12 else GRP)
            norm_rows(0, 0)
            norm_rows(1, 1)
            maxima(0)
            mix_step(0, 0)
            def mix_steps(lo, hi):
                with dve.Fori(lo, hi) as k:
                    for b in range(3):
                        mix_step(k * 3 + (b + 1), (b + 1) % 3)
            mix_steps(0, THIRD)
            dve.wait_ge(S["cnt_ready"], 1)
            nc.vector.tensor_tensor_scan(incl, ones[0:EP, 0:1].broadcast_to([EP, EL]), cnt, 0.0, ALU.mult, ALU.add)\
                .then_inc(S["scan_ok"], 1)
            mix_steps(THIRD, 2 * THIRD)
            dve.wait_ge(S["pe"], 1)
            nc.vector.tensor_copy(poff[:, :], misc[:, 0:1]).then_inc(S["poff_ready"], 1)
            nc.vector.tensor_copy(total[:, :], misc[:, 1:2]).then_inc(S["counts_own"], 1)
            dve.wait_ge(S["counts_own"], 1)
            TS(small[0:1, 1:2], total[0:1, :], CAP * G - 0.5, 1.0 / (CAP * G), ALU.add, ALU.mult).then_inc(S["counts_own"], 1)
            dve.wait_ge(S["counts_own"], 2)
            TS(small[0:1, 1:2], small[0:1, 1:2], 1.0, None, ALU.max).then_inc(S["counts_own"], 1)
            dve.wait_ge(S["counts_own"], 3)
            nc.vector.tensor_copy(n_groups_i[:, :], small[0:1, 1:2]).then_inc(S["ngroups"], 1)
            mix_steps(2 * THIRD, (NG12 - 3) // 3)
            for q in range(NG12 - 2, NG12 + 1):
                mix_step(q, q % 3)
            weighted_sum(NG12)
            link.n[0] = base + PERM * (NG12 + 1)
            link(nc.vector.reciprocal(rsum[:, :], ssum[:, :]))
            dve.wait_ge(S["mix_acc"], NG12 + 1)
            for kb in range(KB):
                last = TS(Pacc[:, kb, :], Pacc[:, kb, :], rsum[:, kb:kb + 1], None, ALU.mult)
            link(last)
            dve.sem_inc(S["pn_ok"], 1)
            dve.wait_ge(S["pe"], 2)
            link(nc.vector.tensor_copy(PT, bank[0][:, :].rearrange("p (a b) -> p a b", a=KB)))
            dve.sem_inc(S["pT_ok"], 1)
            link(nc.vector.tensor_copy(wqT, bank[1][:, :].rearrange("p (a b) -> p a b", a=KB)))
            dve.wait_ge(S["pe"], 3)
            for kb in range(KB):
                last = TT(lam[:, kb, :], bank[2][:, kb * D:(kb + 1) * D], bvB[:, :], ALU.add)
            link(last)
            for kb in range(KB):
                last = nc.vector.bn_stats(stats[:, kb, :], lam[:, kb, :])
            link(last)
            for kb in range(KB):
                last = nc.vector.bn_aggr(mv[:, kb, :], stats[:, kb, :])
            link(last)
            link(nc.vector.tensor_copy(small[:, 6:8], mv[:, 0:KB, 1]))
            dve.sem_inc(S["lamstats_ok"], 1)
            dve.wait_ge(S["act"], 2)
            link(nc.vector.reciprocal(small[:, 8:10], small[:, 4:6]))
            link(TT(small[:, 8:10], small[:, 8:10], bng_c[:, :], ALU.mult))
            for kb in range(KB):
                last = TS(lam[:, kb, :], lam[:, kb, :], mv[:, kb, 0:1], small[:, 8 + kb:9 + kb], ALU.subtract, ALU.mult)
            link(last)
            for kb in range(KB):
                last = TS(bn[:, kb, :], lam[:, kb, :], bnb_c[:, kb:kb + 1], None, ALU.add)
            link(last)
            dve.sem_inc(S["bn_ok"], 1)

            for kb in range(KB):
                last = nc.vector.tensor_copy(Mrot[:, kb, kb * P:(kb + 1) * P], ident[:, :])
            link(last)
            dve.sem_inc(S["chunk_init_ok"], 1)
            dve.sem_inc(S["WK_dve"], 1)
            dve.sem_inc(S["ST_ready"], 1)
            dve.sem_inc(S["M_done"], 1)
            dve.wait_ge(S["empty_group"], 1)
            n = dve.value_load(n_groups_i[0:1, 0:1], min_val=1, max_val=4 * NE)
            base2 = link.n[0]
            sub, v1, v2, valid, isj, dj, tgt, tn, oth, lim, cs, sg, co, csb, cob, lastw = [fld[:, i, :] for i in range(16)]
            posA, posB, posL = [pos[:, i, :] for i in range(3)]
            c_t, c_o, c_cs, c_co, c_last = [cur[:, i, :] for i in range(5)]
            FIELDS, LAST, SWAP, PER = 0, 7, 10, 11

            def after(k, part, i):
                dve.wait_ge(S["dve"], k * PER + (base2 + part + i))

            def sig(ins):
                ins.then_inc(S["dve"], 1)

            def fields_a(k):
                dve.wait_ge(S["recs_in"], k * (16 * G) + 16 * G)
                r_i, r_d, r_j, r_c, r_s, r_n, r_g = [recs[:, :, i] for i in range(7)]
                sig(TT(sub, slotnum[:, :], r_n, ALU.subtract))
                after(k, FIELDS, 1)
                TS(v1, sub, minsub[:, :], None, ALU.is_ge)
                TS(lim, sub, -1.0, prow[:, :], ALU.mult, ALU.add).then_inc(S["lim_ready"], 1)
                sig(TT(isj, sub, r_g, ALU.add))
                after(k, FIELDS, 2)
                STT(v2, sub, maxsub[:, :], v1, ALU.is_le, ALU.mult)
                TS(sg, isj, 2.0, -1.0, ALU.mult, ALU.add)
                sig(TT(dj, isj, r_d, ALU.mult))
                after(k, FIELDS, 3)
                STT(valid, slotnum[:, :], total[:, :], v2, ALU.is_lt, ALU.mult)
                TT(tgt, dj, r_i, ALU.add)
                TT(oth, r_j, dj, ALU.subtract)
                sig(TT(co, r_s, sg, ALU.mult))
                after(k, FIELDS, 4)

            def fields_b(k):
                r_c = recs[:, :, 3]
                STT(tn, tgt, NOROW, valid, ALU.subtract, ALU.mult)
                TT(cs, r_c, valid, ALU.mult)
                sig(TT(co, co, valid, ALU.mult))
                after(k, FIELDS, 5)
                sig(TS(tgt, tn, NOROW, None, ALU.add))
                after(k, FIELDS, 6)
                sig(TS(slotnum[:, :], slotnum[:, :], float(CAP * G), None, ALU.add))
                nc.vector.tensor_copy(tb16, tgt).then_inc(S["flds_ready"], 1)
                after(k, FIELDS, 7)

            def find_hits(k, g):
                if g == 0:
                    dve.wait_ge(S["TB_psum"], k + 1)
                    dve.wait_ge(S["mask_ready"], k + 1)
                    at_least(dve, S["Lready"], k)
                tb = TB[:, g * P:(g + 1) * P]
                STT(hits[:, g, :], tb, tgt[:, g:g + 1], slotmask[:, g, :], ALU.is_equal, ALU.mult)
                STT(hits[:, G + g, :], tb, oth[:, g:g + 1], slotmask[:, g, :], ALU.is_equal, ALU.mult)
                last = STT(hits[:, 2 * G + g, :], tb, tgt[:, g:g + 1], col1[:, :], ALU.is_equal, ALU.mult)
                if g == G - 1:
                    sig(last)
                    after(k, LAST, 1)

            def find_latest(k):
                sig(nc.vector.tensor_reduce(pos[:, 0:2, :].rearrange("p a g -> p (a g)"), hits[:, 0:2 * G, :], AX_X, ALU.max))
                after(k, LAST, 2)

            def build_L(k):
                for g in range(G):
                    TS(Lself[:, g, :], col1[:, :], posA[:, g:g + 1], cs[:, g:g + 1], ALU.is_equal, ALU.mult)
                    last = TS(hits[:, g, :], col1[:, :], posB[:, g:g + 1], co[:, g:g + 1], ALU.is_equal, ALU.mult)
                last.then_inc(S["Lparts"], 1)
                STT(csb, posA, 0.0, cs, ALU.is_equal, ALU.mult)
                STT(cob, posB, 0.0, co, ALU.is_equal, ALU.mult)

            def find_last(k):
                sig(nc.vector.tensor_reduce(posL, hits[:, 2 * G:3 * G, :], AX_X, ALU.max))
                after(k, LAST, 3)
                TS(lastw, posL, prow1[:, :], None, ALU.is_equal).then_inc(S["swap_ready"], 1)

            def swap(k):
                for dst_, s_ in ((c_t, tgt), (c_o, oth), (c_cs, csb), (c_co, cob), (c_last, lastw)):
                    last = nc.vector.tensor_copy(dst_, s_)
                sig(last)
                after(k, SWAP, 1)

            def first_factor(k):
                dve.wait_ge(S["LT_done"], k + 1)
                TT(Jnext, LTnext[:, :, :], ident[:, :].rearrange("p (a n) -> p a n", a=1).broadcast_to([P, G, P]), ALU.add)\
                    .then_inc(S["J0_ready"], 1)

            def apply_m(k, g):
                dve.wait_ge(S["M_psum"], k * G + (g + 1))
                for kb in range(KB):
                    last = STT(Mrot[:, kb, :], Mrot[:, kb, :], keep[:, g, kb:kb + 1], apM[:, kb * D:(kb + 1) * D],
                               ALU.mult, ALU.add)
                last.then_inc(S["M_done"], 1)

            def kept(k):
                dve.wait_ge(S["D_psum"], k + 1)
                TS(keep[:, :, :], misc[:, 0:G * KB].rearrange("p (g k) -> p g k", g=G), -1.0, 1.0, ALU.mult,
                   ALU.add).then_inc(S["D_done"], 1)
                dve.wait_ge(S["D_done"], k + 1)

            fields_a(0)
            fields_b(0)
            for g in range(G):
                last = STT(slotmask[:, g, :], col0[:, 0:P], lim[:, g:g + 1], col1[:, :], ALU.is_lt, ALU.mult)
            last.then_inc(S["mask_own"], 1)
            dve.wait_ge(S["mask_own"], 1)
            dve.sem_inc(S["mask_ready"], 1)
            for g in range(G):
                find_hits(0, g)
            find_latest(0)
            build_L(0)
            find_last(0)
            first_factor(0)
            with dve.Fori(0, n) as k:
                k1 = k + 1
                dve.wait_ge(S["swap_ready"], k + 1)
                swap(k)
                fields_a(k1)
                fields_b(k1)
                for s in range(2, 2 * LEVELS):
                    lv, hf = s // 2, s % 2
                    c = 2 ** lv if lv > 1 else 0
                    dve.wait_ge(S["jb_psum"], k * (2 * (LEVELS - 1)) + (s - 1))
                    w = P if lv < LEVELS - 2 else P - c
                    grown = WK[0:w, 2 * hf:2 * hf + 2, 2 * P + c:3 * P]
                    TT(grown, Jnext[:, 2 * hf:2 * hf + 2, :] if lv == 1 else grown, jb[hf][0:w, :, c:P], ALU.add)\
                        .then_inc(S["WK_dve"], 1)
                    if s in (2, 3):
                        for g in (2 * s - 4, 2 * s - 3):
                            TS(Bself[:, g, :], col0[:, :], c_t[:, g:g + 1], c_cs[:, g:g + 1], ALU.is_equal, ALU.mult)
                            last = TS(Bmat[:, g, :], col0[:, :], c_o[:, g:g + 1], c_co[:, g:g + 1], ALU.is_equal, ALU.mult)
                        if s == 3:
                            last.then_inc(S["Bparts"], 1)
                    if 5 <= s <= 8:
                        find_hits(k1, s - 5)
                    if s == 6:
                        kept(k)
                    if s == 9:
                        find_latest(k1)
                    if s == 10:
                        build_L(k1)
                    if s == 11:
                        find_last(k1)
                    if s in range(V_AT + 1, V_AT + 2 * G, 2):
                        apply_m(k, (s - V_AT) // 2)
                for g in range(G):
                    last = TS(STm[:, g, :], col0[:, :], c_t[:, g:g + 1], c_last[:, g:g + 1], ALU.is_equal, ALU.mult)
                last.then_inc(S["ST_ready"], 1)
                first_factor(k1)
                dve.wait_ge(S["ST_ready"], k + 2)
            kept(n)
            for g in range(G):
                apply_m(n, g)
            dve.wait_ge(S["recs_in"], n * (16 * G) + 2 * 16 * G)
            dve.wait_ge(S["rows_in"], n * (16 * G) + 3 * 16 * G)
            dve.wait_ge(S["Lready"], n + 1)
            dve.wait_ge(S["LT_done"], n + 1)
            dve.wait_ge(S["comb_pe"], 1)
            nc.vector.tensor_copy(comb[:, :, :], bank[0][:, :].rearrange("p (a b) -> p a b", a=KB)).then_inc(S["comb_dve"], 1)
            nc.vector.tensor_copy(addrow, bank[2][:, 0:D]).then_inc(S["comb_dve"], 1)
            dve.wait_ge(S["comb_dve"], 2)
            pl = chain(dve, S["parts_own"])
            pl(nc.vector.memset(addparts[:, :], 0.0))
            for i in range(3):
                part = addparts[32 * i:32 * i + 1, :]
                pl(nc.vector.tensor_copy(addhi, addrow))
                pl(nc.vector.tensor_copy(part, addhi[32 * i:32 * i + 1, :]))
                if i < 2:
                    pl(TT(addrow, addrow, addhi, ALU.subtract))
            TT(comb[:, :, :], comb[:, :, :], bank[1][:, :].rearrange("p (a b) -> p a b", a=KB), ALU.add)\
                .then_inc(S["comb_dve"], 1)
            nc.vector.memset(mskb[:, :, :], 0.0)
            nc.vector.memset(topd[:, :], 0.0)
            nc.vector.memset(mv2[:, :, :], 1.0)
            nc.vector.tensor_copy(base8[:, :], reg8[:, :]).then_inc(S["comb_dve"], 1)
            dve.wait_ge(S["comb_dve"], 4)

            def own(s, q, per, i):
                dve.wait_ge(S[s], q * per + i)
                settle(dve)

            def sum_rows(q, b, uses, nt=4, r=P):
                dve.wait_ge(S["x2_psum"], q + 1)
                dve.wait_ge(S[f"xt{b}"], uses * 16 + 16)
                for h in range((nt + 1) // 2):
                    m = min(2, nt - 2 * h)
                    last = TT(x2_all[0:r, bass.ds(q * 4 + 2 * h, m), :],
                              bank[h][0:r, 0:m * D].rearrange("p (t d) -> p t d", t=m), xt[b][0:r, 2 * h:2 * h + m, :], ALU.add)
                last.then_inc(S["x2_done"], 1)
                dve.wait_ge(S["x2_done"], q + 1)
                settle(dve)
                for t in range(nt):
                    last = nc.vector.bn_stats(st2[0:r, t, :], x2_all[0:r, bass.ds(q * 4 + t, 1), :].rearrange("p a d -> p (a d)"))
                last.then_inc(S["x_own"], 1)
                own("x_own", q, 3, 1)
                for t in range(nt):
                    last = nc.vector.bn_aggr(mv2[0:r, t, :], st2[0:r, t, :])
                last.then_inc(S["std_need"], 1)

            def norm_scales(q):
                dve.wait_ge(S["std_done"], q + 1)
                nc.vector.reciprocal(scl[:, :], dev[:, :]).then_inc(S["x_own"], 1)
                own("x_own", q, 3, 2)
                STT(shift[:, :], mv2[:, :, 0], -1.0, scl[:, :], ALU.mult, ALU.mult).then_inc(S["scl_ready"], 1)

            def norm_gain(q, b, nt=4, r=P):
                if not isinstance(q, int) or q > 0:
                    TS(tokens[:, :], tokens[:, :], float(GRP), None, ALU.add).then_inc(S["tokens_next"], 1)
                dve.wait_ge(S["z_ready"], q + 1)
                TT(xt[b][0:r, 0:nt, :], xt[b][0:r, 0:nt, :], over_tiles(gamB[0:r, :], nt), ALU.mult).then_inc(S["x_own"], 1)

            def norm_out(q, b, uses, nt=4, r=P):
                own("x_own", q, 3, 3)
                at_least(dve, S["tokens_next"], q)
                for t in range(nt):
                    at_least(dve, S[f"sc{b}{t}"], uses * 32)
                nc.vector.tensor_copy(xf[b][0:r, 0:nt, D], tokens[0:r, 0:nt])
                TT(xf[b][0:r, 0:nt, 0:D], xt[b][0:r, 0:nt, :], over_tiles(betB[0:r, :], nt), ALU.add).then_inc(S["xf_ready"], 1)

            def choose(q, b, nt=4, r=P):
                dve.wait_ge(S["lg_psum"], q + 1)
                TT(lg[0:r, 0:nt, :], bank[4][0:r, 0:nt * NX].rearrange("p (t e) -> p t e", t=nt), over_tiles(brB[0:r, :], nt),
                   ALU.add).then_inc(S["r_own"], 1)
                own("r_own", q, 8, 1)
                for t in range(nt):
                    last = nc.vector.max(top[0:r, t, :], lg[0:r, t, :])
                last.then_inc(S["r_own"], 1)
                own("r_own", q, 8, 2)
                for t in range(nt):
                    last = nc.vector.max_index(topi[0:r, t, :], top[0:r, t, :], lg[0:r, t, :])
                last.then_inc(S["r_own"], 1)
                own("r_own", q, 8, 3)
                TT(topd[0:r, bass.ds(q * 4, nt)], top[0:r, 0:nt, 1], top[0:r, 0:nt, 0], ALU.subtract)
                nc.vector.tensor_copy(topf[0:r, 0:nt, :], topi[0:r, 0:nt, :]).then_inc(S["r_own"], 1)
                own("r_own", q, 8, 4)
                for c in range(2):
                    last = TT(oh[0:r, c * 4:c * 4 + nt, :], over_tiles(col0[0:r, 0:NX], nt),
                              topf[0:r, 0:nt, c:c + 1].broadcast_to([r, nt, NX]), ALU.is_equal)
                last.then_inc(S["r_own"], 1)
                own("r_own", q, 8, 5)
                nc.vector.tensor_copy(xf[b][0:r, 0:nt, D + 1], topf[0:r, 0:nt, 0])
                TT(mskb[0:r, 0:nt, :], oh[0:r, 0:nt, :], oh[0:r, 4:4 + nt, :], ALU.add).then_inc(S["msk_ready"], 1)

            def place_rows(q, b, nt=4, r=P):
                dve.wait_ge(S["rank_psum"], q + 1)
                TT(slot8[0:r, 0:nt, :], bank[5][0:r, 0:nt * NX].rearrange("p (t e) -> p t e", t=nt),
                   over_tiles(base8[0:r, :], nt), ALU.add).then_inc(S["r_own"], 1)
                own("r_own", q, 8, 6)
                TT(base8[:, :], bank[5][:, 4 * NX:5 * NX], base8[:, :], ALU.add)
                for c in range(2):
                    last = TT(sel[0:r, c * 4:c * 4 + nt, :], oh[0:r, c * 4:c * 4 + nt, :], slot8[0:r, 0:nt, :], ALU.mult)
                last.then_inc(S["r_own"], 1)
                own("r_own", q, 8, 7)
                for c in range(2):
                    last = nc.vector.tensor_reduce(slotf[0:r, c * 4:c * 4 + nt], sel[0:r, c * 4:c * 4 + nt, :], AX_X, ALU.add)
                last.then_inc(S["r_own"], 1)
                own("r_own", q, 8, 8)
                for c in range(2):
                    last = nc.vector.tensor_copy(slot_now[b][0:r, c * 4:c * 4 + nt], slotf[0:r, c * 4:c * 4 + nt])
                last.then_inc(S["slot_ready"], 1)

            def group_step(q, b, uses):
                n_ = (1, TAIL) if isinstance(q, int) and q + 1 == NG12 else (4, P)
                m_ = (1, TAIL) if isinstance(q, int) and q == NG12 else (4, P)
                more = not isinstance(q, int) or q < NG12
                if more:
                    sum_rows(q + 1, 1 - b, uses, *n_)
                    norm_scales(q + 1)
                if m_[0] < 4:
                    nc.vector.memset(mskb[:, :, :], 0.0).then_inc(S["tail_own"], 1)
                    dve.wait_ge(S["tail_own"], 1)
                choose(q, b, *m_)
                if more:
                    norm_gain(q + 1, 1 - b, *n_)
                place_rows(q, b, *m_)
                if more:
                    norm_out(q + 1, 1 - b, uses, *n_)
            sum_rows(0, 0, 0)
            norm_scales(0)
            norm_gain(0, 0)
            norm_out(0, 0, 0)
            for q in range(2):
                group_step(q, q % 2, (q + 1) // 2)
            with dve.Fori(1, NG12 // 2 - 1) as k:
                for b in range(2):
                    group_step(k * 2 + b, b, k + b)
            for q in range(NG12 - 2, NG12 + 1):
                group_step(q, q % 2, (q + 1) // 2)
            dve.sem_inc(S["wexp_need"], 1)
            tl = chain(dve, S["t_own"])
            tl(TS(padf[:, :], base8[:, :], prow[:, :], None, ALU.add))
            nc.vector.tensor_copy(padu[:, :], padf[:, :]).then_inc(S["pads_ready"], 1)
            tl(TT(ntile[:, 0, :], base8[:, :], reg8[:, :], ALU.subtract))
            tl(TS(ntile[:, 0, :], ntile[:, 0, :], 1.0 / P, 0.5 - 1.0 / (2 * P), ALU.mult, ALU.add))
            tl(TS(ntile[:, 0, :], ntile[:, 0, :], MAGIC, None, ALU.add))
            tl(TS(ntile[:, 0, :], ntile[:, 0, :], -MAGIC, None, ALU.add))
            tl(nc.vector.tensor_tensor_scan(ntile[:, 1, :], ones[:, 0:NX], ntile[:, 0, :], 0.0, ALU.mult, ALU.add))
            tl(TS(ntile[:, 2, :], ntile[:, 0, :], -float(P), float(STRIDE), ALU.mult, ALU.add))
            TS(tacc[:, 1, :], tnum[:, :], float(P), None, ALU.mult)
            tl(TT(past, tnum[:, :].rearrange("p (t a) -> p t a", a=1).broadcast_to([P, MT, NX]), over_tiles(ntile[:, 1, :], MT), ALU.is_ge))
            tl(nc.vector.tensor_reduce(tacc[:, 0, :], past, AX_X, ALU.add))
            tl(TT(past, past, over_tiles(ntile[:, 2, :], MT), ALU.mult))
            tl(nc.vector.tensor_reduce(tacc[:, 2, :], past, AX_X, ALU.add))
            tl(TT(tacc[:, 1, :], tacc[:, 1, :], tacc[:, 2, :], ALU.add))
            tl(TS(tacc[:, 0, :], tacc[:, 0, :], float(NX - 1), None, ALU.min))
            tl(nc.vector.tensor_copy(ttab[:, :, :], tacc[0:1, 0:2, :]))
            tl(TS(ntile[0:1, 0, 0:1], ntile[0:1, 1, NX - 1:NX], 0.5, 0.25, ALU.mult, ALU.add))
            tl(TS(ntile[0:1, 0, 0:1], ntile[0:1, 0, 0:1], MAGIC, None, ALU.add))
            tl(TS(ntile[0:1, 0, 0:1], ntile[0:1, 0, 0:1], -MAGIC, None, ALU.add))
            tl(TS(ntile[0:1, 0, 1:2], ntile[0:1, 0, 0:1], -2.0, None, ALU.add))
            tl(nc.vector.tensor_copy(pairs_i[:, :], ntile[0:1, 0, 0:2]))
            dve.sem_inc(S["tiles_ready"], 1)
            dve.wait_ge(S["wexp_done"], 1)
            tl(TS(w_a[:, :], wexp[:, :], 1.0, None, ALU.add))
            tl(nc.vector.reciprocal(w_a[:, :], w_a[:, :]))
            tl(TT(w_b[:, :], w_a[:, :], wexp[:, :], ALU.mult))

            dve.wait_ge(S["bias_loaded"], 32)

            def expert_of(i):
                return dve.value_load(ttab[0:1, 0, bass.ds(i, 1)], min_val=0, max_val=NX - 1)

            def destinations(i, b, uses):
                dve.wait_ge(S[f"xm{b}"], uses * 16 + 16)
                TS(second[:, b:b + 1], xm[b][:, D + 1:D + 2], tacc[:, 0, bass.ds(i, 1)], -float(N), ALU.is_equal,
                   ALU.mult).then_inc(S["second_own"], 1)
                dve.wait_ge(S["second_own"], i + 1)
                TT(dest_u[:, bass.ds(i, 1)], second[:, b:b + 1], xm[b][:, D:D + 1], ALU.add).then_inc(S["dest_ready"], 1)

            def hidden(i, b):
                e = expert_of(i)
                dve.wait_ge(S["h_psum"], i + 1)
                at_least(dve, S["hact_done"], i - 1)
                TT(hpre[b], bank[2 + b][:, 0:H], b1B[:, bass.ds(e, 1), :].rearrange("p a h -> p (a h)"),
                   ALU.add).then_inc(S["hpre_done"], 1)

            def turned_hidden(i, b):
                dve.wait_ge(S["hT_psum"], i + 1)
                nc.vector.tensor_copy(hT[b], bank[4 + b][:, 0:H]).then_inc(S["hT_done"], 1)

            def results(i, b, uses):
                e = expert_of(i)
                dve.wait_ge(S["y_psum"], i + 1)
                at_least(dve, S[f"ysc{b}"], uses * 16)
                TT(yb[b], bank[6 + b][:, 0:D], b2B[:, bass.ds(e, 1), :].rearrange("p a h -> p (a h)"),
                   ALU.add).then_inc(S["y_done"], 1)

            def moe_step(i, b, k, left=4):
                const = isinstance(i, int)
                if left > 3:
                    destinations(i + 3, 1 - b, (i + 3) // 2 if const else k + (1 + b))
                if left > 2 and (not const or i + 2 >= 0):
                    hidden(i + 2, b)
                if left > 1 and (not const or i + 1 >= 0):
                    turned_hidden(i + 1, 1 - b)
                if not const or i >= 0:
                    results(i, b, k)
            dve.sem_inc(S["y_done"], 1)
            m = dve.value_load(pairs_i[0:1, 1:2], min_val=LEAST - 2, max_val=MT // 2 - 2)
            for i in range(-3, 2):
                moe_step(i, i % 2, 0)
            with dve.Fori(1, m) as k:
                for b in range(2):
                    moe_step(k * 2 + b, b, k)
            for j in range(4):
                moe_step(m * 2 + j, j % 2, m + j // 2, 4 - j)

            def final(q, b, uses, nt=4, r=P):
                dve.wait_ge(S[f"back{b}"], uses * 32 + 32)
                for t in range(nt):
                    last = STT(ya[b][0:r, t, :], ya[b][0:r, t, :], w_a[0:r, bass.ds(q * 4 + t, 1)],
                               x2_all[0:r, bass.ds(q * 4 + t, 1), :].rearrange("p a d -> p (a d)"), ALU.mult, ALU.add)
                last.then_inc(S["sum_a"], 1)
                dve.wait_ge(S["sum_a"], q + 1)
                for t in range(nt):
                    last = STT(yc[b][0:r, t, :], yc[b][0:r, t, :], w_b[0:r, bass.ds(q * 4 + t, 1)], ya[b][0:r, t, :],
                               ALU.mult, ALU.add)
                last.then_inc(S["fin_done"], 1)
            with dve.Fori(0, NG12 // FB) as k:
                for b in range(FB):
                    final(k * FB + b, b, k)
            final(NG12, 0, NG12 // FB, 1, TAIL)

        @block.tensor
        def _(pe):
            link = chain(pe, S["pe"])
            mm, tr = nc.tensor.matmul, nc.tensor.transpose
            pe.wait_ge(S["consts"], 1)
            pe.wait_ge(S["wload"], 16 * 12)

            def turn_in(q, b, W=GRP):
                nt, r = (W + P - 1) // P, W % P or P
                pe.wait_ge(S["xn_ready"], q + 1)
                for kb in range(KB):
                    for t in range(nt):
                        last = tr(bank[kb][:, t * P:t * P + r], xng[b][0:r, t, kb * P:(kb + 1) * P], ident[0:r, 0:r])
                last.then_inc(S["xT_psum"], 1)

            def keys(q, W=GRP):
                pe.wait_ge(S["xT_done"], q + 1)
                at_least(pe, S["exp_done"], q)
                for db in range(KB):
                    for kb in range(KB):
                        last = mm(bank[2 + db][:, 0:W], wk[:, kb, db * P:(db + 1) * P],
                                  xnT[:, kb, bass.ds(q * GRP, W)], start=(kb == 0), stop=(kb == KB - 1))
                last.then_inc(S["keys_psum"], 1)

            def turn_exps(q, W=GRP):
                nt, r = (W + P - 1) // P, W % P or P
                pe.wait_ge(S["exp_done"], q + 1)
                for kb in range(KB):
                    for t in range(nt):
                        last = tr(bank[4 + kb][0:r, t * P:(t + 1) * P], ex[:, kb, t * P:t * P + r], ident[:, :])
                last.then_inc(S["exT_psum"], 1)

            def weigh(q, b, W=GRP):
                nt, r = (W + P - 1) // P, W % P or P
                pe.wait_ge(S["exT_done"], q + 1)
                at_least(pe, S["mix_acc"], q)
                for kb in range(KB):
                    for t in range(nt):
                        last = mm(bank[6][:, kb * D:(kb + 1) * D], exT[0:r, t, kb * P:(kb + 1) * P], xng[b][0:r, t, :],
                                  start=(t == 0), stop=(t == nt - 1))
                last.then_inc(S["mix_psum"], 1)

            def mix_step(q, b):
                const = isinstance(q, int)
                turn_exps(q, TAIL if const and q == NG12 else GRP)
                if not const or q + 1 <= NG12:
                    keys(q + 1, TAIL if const and q + 1 == NG12 else GRP)
                if not const or q + 2 <= NG12:
                    turn_in(q + 2, (b + 2) % 3, TAIL if const and q + 2 == NG12 else GRP)
                weigh(q, b, TAIL if const and q == NG12 else GRP)
            turn_in(0, 0)
            keys(0)
            turn_in(1, 1)
            mix_step(0, 0)
            def mix_steps(lo, hi):
                with pe.Fori(lo, hi) as k:
                    for b in range(3):
                        mix_step(k * 3 + (b + 1), (b + 1) % 3)
            mix_steps(0, THIRD)
            pe.wait_ge(S["scan_ok"], 1)
            mm(misc[:, 0:1], tri[0:EP, :], incl[:, EL - 1:EL], start=True, stop=True)
            mm(misc[:, 1:2], ones[0:EP, :], incl[:, EL - 1:EL], start=True, stop=True).then_inc(S["pe"], 1)
            mix_steps(THIRD, (NG12 - 3) // 3)
            for q in range(NG12 - 2, NG12 + 1):
                mix_step(q, q % 3)

            pe.wait_ge(S["pn_ok"], 1)
            for src_, bk in ((Pacc, 0), (wq, 1)):
                for a in range(KB):
                    for b in range(KB):
                        last = tr(bank[bk][:, b * D + a * P:b * D + (a + 1) * P], src_[:, a, b * P:(b + 1) * P], ident[:, :])
            last.then_inc(S["pe"], 1)
            pe.wait_ge(S["pT_ok"], 1)
            for db in range(KB):
                for kb in range(KB):
                    last = mm(bank[2][:, db * D:(db + 1) * D], PT[:, kb, db * P:(db + 1) * P], wv[:, kb, :],
                              start=(kb == 0), stop=(kb == KB - 1))
            last.then_inc(S["pe"], 1)
            pe.wait_ge(S["chunk_init_ok"], 1)
            pe.wait_ge(S["empty_group"], 1)

            n = pe.value_load(n_groups_i[0:1, 0:1], min_val=1, max_val=4 * NE)

            def spread_targets(k):
                pe.wait_ge(S["flds_ready"], k + 1)
                for g in range(G):
                    last = mm(TB[:, g * P:(g + 1) * P], tb16[:, g:g + 1].broadcast_to([P, P]), identb[:, :],
                              start=True, stop=True)
                last.then_inc(S["TB_psum"], 1)

            def apply_v(k, g):
                pe.wait_ge(S["M_done"], k * G + (g + 1))
                for kb in range(KB):
                    last = mm(apV[:, 0:D], GT[:, g, kb * P:(kb + 1) * P], Mrot[:, kb, :], start=(kb == 0), stop=(kb == KB - 1))
                last.then_inc(S["V_psum"], 1)

            def apply_m(k, g):
                pe.wait_ge(S["V_done"], k * G + (g + 1))
                for rb in range(KB):
                    last = mm(apM[:, rb * D:(rb + 1) * D], STm[:, g, rb * P:(rb + 1) * P], Vs[:, :], start=True, stop=True)
                last.then_inc(S["M_psum"], 1)

            def turn_L(k):
                pe.wait_ge(S["Lready"], k + 1)
                for g in range(G):
                    last = tr(TB[:, g * P:(g + 1) * P], Lnext[:, g, :], ident[:, :])
                last.then_inc(S["LT_psum"], 1)
            def count_writes(k):
                pe.wait_ge(S["STb_ready"], k + 1)
                for g in range(G):
                    for kb in range(KB):
                        last = mm(misc[:, g * KB + kb:g * KB + kb + 1], STb[:, g, kb * P:(kb + 1) * P], onesb[:, 0:1],
                                  start=True, stop=True)
                last.then_inc(S["D_psum"], 1)

            def transform(k):
                pe.wait_ge(S["WK_dve"], k * NDVE + 1)
                pe.wait_ge(S["M_done"], k * G + 1)
                pe.wait_ge(S["B_ready"], k + 1)
                for g in range(G):
                    for kb in range(KB):
                        last = mm(gb[g // 2][:, g % 2, kb * P:(kb + 1) * P], Bmat[:, g, kb * P:(kb + 1) * P], WK[:, g, 2 * P:3 * P],
                                  start=True, stop=True)
                last.then_inc(S["GT_psum"], 1)
            spread_targets(0)
            turn_L(0)
            NACT = 2 * (LEVELS - 1)
            NDVE = 2 * (LEVELS - 1)

            def inverse(k, lv, hf):
                w = P if lv < LEVELS - 2 else P - 2 ** lv
                c = 2 ** lv if lv > 1 else 0
                if lv == 1:
                    pe.wait_ge(S["J0_ready"], k + 1)
                else:
                    pe.wait_ge(S["WK_dve"], k * NDVE + (2 * (lv - 1) + hf))
                for g in (2 * hf, 2 * hf + 1):
                    so_far = Jnext[:, g, :] if lv == 1 else WK[:, g, 2 * P + c:3 * P]
                    last = mm(jb[hf][0:w, g % 2, c:P], WK[:, g, 0:w], so_far, start=True, stop=True)
                last.then_inc(S["jb_psum"], 1)
            with pe.Fori(0, n) as k:
                pe.wait_ge(S["LT_done"], k + 1)
                for s in range(2 * LEVELS):
                    lv, hf = s // 2, s % 2
                    if lv >= 1:
                        pe.wait_ge(S["WK_act"], k * NACT + (2 * (lv - 1) + hf + 1))
                    if lv >= 2:
                        inverse(k, lv, hf)
                    for g in (2 * hf, 2 * hf + 1):
                        Lk, LkT = (WK[:, g, 0:P], WK[:, g, P:2 * P]) if lv else (Lnext[:, g, :], LTnext[:, g, :])
                        if lv < LEVELS - 1:
                            w = P if lv < LEVELS - 3 else P - 2 ** (lv + 1)
                            last = mm(pw[hf][:, g % 2, 0:w], LkT, Lk[:, 0:w], start=True, stop=True)
                        if lv < LEVELS - 2:
                            last = mm(pw[hf][:, g % 2, P:2 * P], Lk, LkT, start=True, stop=True)
                    if lv < LEVELS - 1:
                        last.then_inc(S["pw_psum"], 1)
                    if lv == 1:
                        inverse(k, lv, hf)
                    if s == 1:
                        transform(k)
                    if s == V_AT:
                        pe.wait_ge(S["GT_done"], k + 1)
                    if V_AT <= s < V_AT + 2 * G:
                        (apply_m if (s - V_AT) % 2 else apply_v)(k, (s - V_AT) // 2)
                    if s == 5:
                        count_writes(k)
                    if s == 4:
                        spread_targets(k + 1)
                    if s == 12:
                        turn_L(k + 1)
            transform(n)
            count_writes(n)
            pe.wait_ge(S["GT_done"], n + 1)
            pe.wait_ge(S["D_done"], n + 1)
            for g in range(G):
                apply_v(n, g)
                apply_m(n, g)
            pe.wait_ge(S["M_done"], n * G + (G + 1))
            for a in range(KB):
                for b in range(KB):
                    tr(bank[0][:, b * D + a * P:b * D + (a + 1) * P], Mrot[:, a, b * P:(b + 1) * P], ident[:, :])
            for ib in range(KB):
                for kb in range(KB):
                    mm(bank[1][:, ib * D:(ib + 1) * D], wqT[:, kb, ib * P:(ib + 1) * P], bn[:, kb, :],
                       start=(kb == 0), stop=(kb == KB - 1))
            for kb in range(KB):
                last = mm(bank[2][:, 0:D], bq_c[:, kb:kb + 1].broadcast_to([P, P]), bn[:, kb, :],
                          start=(kb == 0), stop=(kb == KB - 1))
            last.then_inc(S["comb_pe"], 1)
            pe.wait_ge(S["comb_dve"], 4)

            def sum_pe(q, b, nt=4, r=P, halves=(0, 1)):
                for h in halves:
                    if h == 0:
                        pe.wait_ge(S["stg_done"], q + 1)
                        at_least(pe, S["x2_done"], q)
                    m = min(2, nt - 2 * h)
                    if m <= 0:
                        continue
                    mm(bank[h][0:r, 0:m * D].rearrange("p (t d) -> p t d", t=m), onesb[0:96, 0:r], over_tiles(addparts[:, :], m),
                       start=True, stop=False)
                    for t in range(2 * h, 2 * h + m):
                        for kb in range(KB):
                            last = mm(bank[h][0:r, (t % 2) * D:(t % 2 + 1) * D], stg[b][:, kb, t * P:t * P + r], comb[:, kb, :],
                                      start=False, stop=(kb == KB - 1 and t == 2 * h + m - 1))
                    if t == nt - 1:
                        last.then_inc(S["x2_psum"], 1)

            def router_pe(q, b, nt=4, r=P):
                pe.wait_ge(S["xf_ready"], q + 1)
                for kb in range(KB):
                    for t in range(nt):
                        last = tr(bank[2 + kb][:, t * P:t * P + r], xf[b][0:r, t, kb * P:(kb + 1) * P], ident[0:r, 0:r])
                last.then_inc(S["xfT_psum"], 1)
                pe.wait_ge(S["xfT_done"], q + 1)
                for t in range(nt):
                    for kb in range(KB):
                        last = mm(bank[4][0:r, t * NX:(t + 1) * NX], xfT[:, kb, t * P:t * P + r], wr_s[:, kb, :],
                                  start=(kb == 0), stop=(kb == KB - 1))
                last.then_inc(S["lg_psum"], 1)

            def rank_pe(q):
                pe.wait_ge(S["msk_ready"], q + 1)
                mm(bank[5][:, 0:5 * NX], trib[:, :], mskb[:, :, :].rearrange("p t e -> p (t e)"), start=True, stop=False)
                for t in range(4):
                    last = mm(bank[5][:, (t + 1) * NX:5 * NX].rearrange("p (t e) -> p t e", e=NX), onesb[:, :],
                              mskb[:, t:t + 1, :].broadcast_to([P, 4 - t, NX]), start=False, stop=(t == 3))
                last.then_inc(S["rank_psum"], 1)
            sum_pe(0, 0)
            sum_pe(1, 1)
            with pe.Fori(0, NG12 // 2 - 1) as k:
                for b in range(2):
                    router_pe(k * 2 + b, b)
                    sum_pe(k * 2 + (b + 2), b, halves=(0,))
                    rank_pe(k * 2 + b)
                    sum_pe(k * 2 + (b + 2), b, halves=(1,))
            for q in range(NG12 - 2, NG12 + 1):
                router_pe(q, q % 2, *((4, P) if q < NG12 else (1, TAIL)))
                if q + 2 == NG12:
                    sum_pe(NG12, 0, 1, TAIL)
                rank_pe(q)

            pe.wait_ge(S["tiles_ready"], 1)
            pe.wait_ge(S["w_loaded"], 16 * 2 * NX)

            def expert_of(i):
                return pe.value_load(ttab[0:1, 0, bass.ds(i, 1)], min_val=0, max_val=NX - 1)

            def turn_x(i, b, uses):
                pe.wait_ge(S[f"xm{b}"], uses * 16 + 16)
                at_least(pe, S["xmT_done"], i - 1)
                for kb in range(KB):
                    last = tr(bank[b][:, kb * P:(kb + 1) * P], xm[b][:, kb * P:(kb + 1) * P], ident[:, :])
                last.then_inc(S["xmT_psum"], 1)

            def first_product(i, b):
                e = expert_of(i)
                pe.wait_ge(S["xmT_done"], i + 1)
                at_least(pe, S["hpre_done"], i - 1)
                for kb in range(KB):
                    last = mm(bank[2 + b][:, 0:H], xmT[b][:, kb * P:(kb + 1) * P],
                              w1s[:, bass.ds(e, 1), kb, :].rearrange("p a h -> p (a h)"), start=(kb == 0), stop=(kb == KB - 1))
                last.then_inc(S["h_psum"], 1)

            def turn_hidden(i, b):
                pe.wait_ge(S["hact_done"], i + 1)
                for kb in range(H // P):
                    last = tr(bank[4 + b][:, kb * P:(kb + 1) * P], hact[b][:, kb * P:(kb + 1) * P], ident[:, :])
                last.then_inc(S["hT_psum"], 1)

            def second_product(i, b):
                e = expert_of(i)
                pe.wait_ge(S["hT_done"], i + 1)
                pe.wait_ge(S["y_done"], i + 1)
                for kb in range(H // P):
                    last = mm(bank[6 + b][:, 0:D], hT[b][:, kb * P:(kb + 1) * P],
                              w2s[:, bass.ds(e, 1), kb, :].rearrange("p a h -> p (a h)"),
                              start=(kb == 0), stop=(kb == H // P - 1))
                last.then_inc(S["y_psum"], 1)

            def moe_step(i, b, k, left=4):
                const = isinstance(i, int)
                if left > 3:
                    turn_x(i + 3, 1 - b, (i + 3) // 2 if const else k + (1 + b))
                if left > 2 and (not const or i + 2 >= 0):
                    first_product(i + 2, b)
                if left > 1 and (not const or i + 1 >= 0):
                    turn_hidden(i + 1, 1 - b)
                if not const or i >= 0:
                    second_product(i, b)
            m = pe.value_load(pairs_i[0:1, 1:2], min_val=LEAST - 2, max_val=MT // 2 - 2)
            for i in range(-3, 0):
                moe_step(i, i % 2, 0)
            with pe.Fori(0, m) as k:
                for b in range(2):
                    moe_step(k * 2 + b, b, k)
            for j in range(4):
                moe_step(m * 2 + j, j % 2, m + j // 2, 4 - j)


_INS = ["x", "src", "dst", "edge_weight", "L0_mix_W_qk", "L0_mix_b_qk", "L0_mix_W_v", "L0_mix_b_v", "L0_mix_gamma",
        "L0_mix_beta", "L0_ffn_gamma", "L0_ffn_beta", "L0_ffn_Wr", "L0_ffn_br", "L0_ffn_W1", "L0_ffn_b1",
        "L0_ffn_W2", "L0_ffn_b2"]


def kernel(**inputs):
    import numpy as _np
    import concourse.bacc as _bacc
    from concourse import mybir as _mybir
    from concourse.bass_utils import run_bass_kernel_spmd as _run

    nc = _bacc.Bacc("TRN2", target_bir_lowering=False, num_devices=1)
    arrays, args = {}, []
    for name in _INS:
        a = _np.ascontiguousarray(inputs[name])
        arrays[f"in_{name}_dram"] = a
        args.append(nc.dram_tensor(f"in_{name}_dram", a.shape, _mybir.dt.from_np(a.dtype), kind="ExternalInput").ap())
    out = nc.dram_tensor("out_0_dram", inputs["x"].shape, _mybir.dt.from_np(_np.dtype("float32")), kind="ExternalOutput")
    gnn_layer(nc, *args, out.ap())
    r = _run(nc, [arrays], core_ids=[0])
    return r.results[0]["out_0_dram"]
```
